# Optimizing a Trainium2 kernel written in Bass

```python
import numpy as np
import jax
import jax.numpy as jnp

def _softmax(x, axis=-1):
    return jax.nn.softmax(x, axis=axis)

def _gelu(x):
    return jax.nn.gelu(x, approximate=True)

def _silu(x):
    return jax.nn.silu(x)

def _sigmoid(x):
    return jax.nn.sigmoid(x)

def _layernorm(x, axis=-1, eps=1e-05):
    m = jnp.mean(x, axis=axis, keepdims=True)
    v = jnp.var(x, axis=axis, keepdims=True)
    return (x - m) / jnp.sqrt(v + eps)

def _scatter_add(tgt, idx, src, axis=0):
    return tgt.at[idx].add(src)

def _segment_sum(src, seg, n):
    return jax.ops.segment_sum(src, seg, n)
kernel_name = 'mk_hybrid_d1_jaxref_r8_a42d21'

def setup_inputs(seed: int=0):
    np.random.seed(seed)
    _w = jnp.asarray

    def _L0_attn_a_setup():
        import jax, jax.numpy as jnp
        import numpy as np
        D_MODEL = 128
        D_STATE = 16
        D_CONV = 4
        EXPAND = 2
        HEADDIM = 64
        CHUNK = 64
        D_INNER = EXPAND * D_MODEL
        NHEADS = D_INNER // HEADDIM
        CONV_DIM = D_INNER + 2 * D_STATE
        D_IN_PROJ = 2 * D_INNER + 2 * D_STATE + NHEADS

        def silu(x):
            return x * jax.nn.sigmoid(x)

        def segsum(x):
            T = x.shape[-1]
            xe = jnp.repeat(x[..., None], T, axis=-1)
            mask_lower = jnp.tril(jnp.ones((T, T), bool), -1)
            xe = jnp.where(mask_lower, xe, 0.0)
            s = jnp.cumsum(xe, axis=-2)
            mask_diag = jnp.tril(jnp.ones((T, T), bool), 0)
            return jnp.where(mask_diag, s, -jnp.inf)

        def ssd(x, A, B, C, chunk):
            b, L, h, p = x.shape
            n = B.shape[-1]
            c = L // chunk
            x = x.reshape(b, c, chunk, h, p)
            A = A.reshape(b, c, chunk, h).transpose(0, 3, 1, 2)
            B = jnp.broadcast_to(B[:, :, None] if B.ndim == 3 else B, (b, L, h, n)).reshape(b, c, chunk, h, n)
            C = jnp.broadcast_to(C[:, :, None] if C.ndim == 3 else C, (b, L, h, n)).reshape(b, c, chunk, h, n)
            A_cumsum = jnp.cumsum(A, axis=-1)
            Lmat = jnp.exp(segsum(A))
            Y_diag = jnp.einsum('bclhn,bcshn,bhcls,bcshp->bclhp', C, B, Lmat, x)
            decay_states = jnp.exp(A_cumsum[:, :, :, -1:] - A_cumsum)
            states = jnp.einsum('bclhn,bhcl,bclhp->bchpn', B, decay_states, x)
            init = jnp.zeros_like(states[:, :1])
            states = jnp.concatenate([init, states], axis=1)
            A_last = jnp.pad(A_cumsum[:, :, :, -1], ((0, 0), (0, 0), (1, 0)))
            decay_chunk = jnp.exp(segsum(A_last))
            new_states = jnp.einsum('bhzc,bchpn->bzhpn', decay_chunk, states)
            states, final_state = (new_states[:, :-1], new_states[:, -1])
            state_decay_out = jnp.exp(A_cumsum)
            Y_off = jnp.einsum('bclhn,bchpn,bhcl->bclhp', C, states, state_decay_out)
            Y = (Y_diag + Y_off).reshape(b, L, h, p)
            return (Y, final_state)
        key = jax.random.key(seed)
        ks = jax.random.split(key, 8)
        B, L = (2, 512)
        u = jax.random.normal(ks[0], (B, L, D_MODEL), dtype=jnp.float32)
        W_in = jax.random.normal(ks[1], (D_IN_PROJ, D_MODEL), dtype=jnp.float32) * 0.02
        conv_w = jax.random.normal(ks[2], (CONV_DIM, 1, D_CONV), dtype=jnp.float32) * 0.2
        conv_b = jnp.zeros((CONV_DIM,), dtype=jnp.float32)
        dt_bias = jax.random.uniform(ks[3], (NHEADS,), dtype=jnp.float32, minval=-4.0, maxval=1.0)
        A_log = jnp.full((NHEADS,), -np.log(2.0), dtype=jnp.float32)
        D = jnp.ones((NHEADS,), dtype=jnp.float32)
        norm_w = jnp.ones((D_INNER,), dtype=jnp.float32)
        W_out = jax.random.normal(ks[4], (D_MODEL, D_INNER), dtype=jnp.float32) * 0.02
        return {'u': u, 'W_in': W_in, 'conv_w': conv_w, 'conv_b': conv_b, 'dt_bias': dt_bias, 'A_log': A_log, 'D': D, 'norm_w': norm_w, 'W_out': W_out}
    _L0_attn_a_in = _L0_attn_a_setup()

    def _L0_attn_b_setup():
        import jax, jax.numpy as jnp
        import numpy as np
        B_, T_, D_ = (2, 256, 128)
        DS_, EXPAND_ = (16, 2)
        DI_ = D_ * EXPAND_

        def _forward(x, Win, A_log, WB, WC, Wdt, bdt, dt_bias, gamma, beta, Wout):
            B, T, d = x.shape
            di, ds = A_log.shape
            xz = jnp.einsum('btd,ed->bte', x, Win)
            xi, z = (xz[..., :di], xz[..., di:])
            z = jax.nn.silu(z)
            A = -jnp.exp(A_log)
            Bm = jnp.einsum('btd,sd->bts', x, WB)
            C = jnp.einsum('btd,sd->bts', x, WC)
            dt = jax.nn.softplus(jnp.einsum('btd,ed->bte', x, Wdt) + bdt + dt_bias)
            dtA = dt[..., None] * A
            denom = 1.0 - dtA * 0.5
            A_bar = (1.0 + dtA * 0.5) / denom
            B_bar = dt[..., None] / denom

            def step(state, inp):
                Ab, Bb, Bt, xt, Ct = inp
                state = Ab * state + Bb * Bt[:, None, :] * xt[:, :, None]
                out = jnp.einsum('bds,bs->bd', state, Ct)
                return (state, out)
            tm = lambda a: jnp.swapaxes(a, 0, 1)
            state0 = jnp.zeros((B, di, ds), x.dtype)
            state, outs = jax.lax.scan(step, state0, (tm(A_bar), tm(B_bar), tm(Bm), tm(xi), tm(C)))
            out = jnp.swapaxes(outs, 0, 1) * z
            mu = out.mean(-1, keepdims=True)
            var = ((out - mu) ** 2).mean(-1, keepdims=True)
            normed = (out - mu) * jax.lax.rsqrt(var + 1e-05) * gamma + beta
            y = jnp.einsum('bte,de->btd', normed, Wout)
            return (y, state)

        def _reference_tuple_inner(x, Win, A_log, WB, WC, Wdt, bdt, dt_bias, gamma, beta, Wout):
            return _forward(x, Win, A_log, WB, WC, Wdt, bdt, dt_bias, gamma, beta, Wout)
        key = jax.random.key(seed)
        ks = jax.random.split(key, 10)
        s = 0.02
        x = jax.random.normal(ks[0], (B_, T_, D_), jnp.float32)
        Win = jax.random.normal(ks[1], (2 * DI_, D_), jnp.float32) * s
        A_log = jax.random.uniform(ks[2], (DI_, DS_), jnp.float32, -4.0, -1.0)
        WB = jax.random.normal(ks[3], (DS_, D_), jnp.float32) * s
        WC = jax.random.normal(ks[4], (DS_, D_), jnp.float32) * s
        Wdt = jax.random.normal(ks[5], (DI_, D_), jnp.float32) * s
        bdt = jnp.zeros((DI_,), jnp.float32)
        dt_bias = jnp.full((DI_,), -4.0, jnp.float32)
        gamma = jnp.ones((DI_,), jnp.float32)
        beta = jnp.zeros((DI_,), jnp.float32)
        Wout = jax.random.normal(ks[6], (D_, DI_), jnp.float32) * s
        return dict(x=x, Win=Win, A_log=A_log, WB=WB, WC=WC, Wdt=Wdt, bdt=bdt, dt_bias=dt_bias, gamma=gamma, beta=beta, Wout=Wout)
    _L0_attn_b_in = _L0_attn_b_setup()

    def _L0_ffn_setup():
        import jax, jax.numpy as jnp
        import numpy as np
        DIM = 128
        DEPTH = 2
        HEADS = 8
        DIM_HEAD = 64
        WINDOW = 64
        INNER = HEADS * DIM_HEAD
        HID = int(DIM * 4 * 2 / 3)
        B, N = (2, 1024)
        QK_SCALE = 8.0

        def shift_token(t):
            t1, t2 = jnp.split(t, 2, axis=-1)
            t2 = jnp.pad(t2, ((0, 0), (1, 0), (0, 0)))[:, :-1]
            return jnp.concatenate([t1, t2], axis=-1)

        def l2norm(t):
            return t / jnp.clip(jnp.linalg.norm(t, axis=-1, keepdims=True), 1e-12)

        def rotate_half(x):
            x1, x2 = jnp.split(x, 2, axis=-1)
            return jnp.concatenate([-x2, x1], axis=-1)

        def rotary_xpos(q, k):
            n = q.shape[-2]
            half_idx = jnp.arange(0, DIM_HEAD, 2, dtype=jnp.float32)
            inv_freq = 1.0 / 10000.0 ** (half_idx / DIM_HEAD)
            t = jnp.arange(n, dtype=jnp.float32)
            freqs = t[:, None] * inv_freq[None, :]
            freqs = jnp.concatenate([freqs, freqs], axis=-1)
            base = (half_idx + 0.4 * DIM_HEAD) / (1.4 * DIM_HEAD)
            power = (t - n // 2) / float(WINDOW // 2)
            scale = base[None, :] ** power[:, None]
            scale = jnp.concatenate([scale, scale], axis=-1)
            cos, sin = (jnp.cos(freqs), jnp.sin(freqs))
            q = q * cos * scale + rotate_half(q) * sin * scale
            k = k * cos / scale + rotate_half(k) * sin / scale
            return (q, k)

        def local_attention(q, k, v):
            b, h, n, d = q.shape
            w = n // WINDOW
            bq = q.reshape(b, h, w, WINDOW, d) * QK_SCALE
            bk = k.reshape(b, h, w, WINDOW, d)
            bv = v.reshape(b, h, w, WINDOW, d)

            def look_around(t):
                p = jnp.pad(t, ((0, 0), (0, 0), (1, 0), (0, 0), (0, 0)))
                return jnp.concatenate([p[:, :, :w], p[:, :, 1:]], axis=3)
            bk, bv = (look_around(bk), look_around(bv))
            bt = jnp.arange(n).reshape(w, WINDOW)
            btp = jnp.pad(bt, ((1, 0), (0, 0)), constant_values=-1)
            btk = jnp.concatenate([btp[:w], btp[1:]], axis=1)
            sim = jnp.einsum('bhwid,bhwjd->bhwij', bq, bk)
            i = bt[:, :, None]
            j = btk[:, None, :]
            mask = (i < j) | (i > j + WINDOW) | (j == -1)
            sim = jnp.where(mask, -jnp.finfo(sim.dtype).max, sim)
            attn = jax.nn.softmax(sim, axis=-1)
            out = jnp.einsum('bhwij,bhwjd->bhwid', attn, bv)
            return out.reshape(b, h, n, d)

        def _layer(x, wqkv, qs, ksc, wo, lg, lb, w1, b1, w2, b2):
            b, n, _ = x.shape
            h = shift_token(x)
            qkv = h @ wqkv
            q, k, v = jnp.split(qkv, 3, axis=-1)
            to_heads = lambda t: t.reshape(b, n, HEADS, DIM_HEAD).transpose(0, 2, 1, 3)
            q, k, v = (to_heads(q), to_heads(k), to_heads(v))
            q = l2norm(q) * qs
            k = l2norm(k) * ksc
            q, k = rotary_xpos(q, k)
            o = local_attention(q, k, v)
            o = o.transpose(0, 2, 1, 3).reshape(b, n, INNER)
            x = x + o @ wo
            h = shift_token(x)
            mu = h.mean(-1, keepdims=True)
            var = h.var(-1, keepdims=True)
            h = (h - mu) / jnp.sqrt(var + 1e-05) * lg + lb
            h = h @ w1 + b1
            a, g = jnp.split(h, 2, axis=-1)
            h = a * jax.nn.gelu(g, approximate=False)
            x = x + h @ w2 + b2
            return x
        key = jax.random.key(seed)
        ks = jax.random.split(key, 6)
        return {'x': jax.random.normal(ks[0], (B, N, DIM), jnp.float32), 'wqkv': jax.random.normal(ks[1], (DEPTH, DIM, 3 * INNER), jnp.float32) * 0.02, 'q_scale': jnp.ones((DEPTH, DIM_HEAD), jnp.float32), 'k_scale': jnp.ones((DEPTH, DIM_HEAD), jnp.float32), 'wo': jax.random.normal(ks[2], (DEPTH, INNER, DIM), jnp.float32) * 0.02, 'ln_g': jnp.ones((DEPTH, DIM), jnp.float32), 'ln_b': jnp.zeros((DEPTH, DIM), jnp.float32), 'w1': jax.random.normal(ks[3], (DEPTH, DIM, 2 * HID), jnp.float32) * 0.02, 'b1': jnp.zeros((DEPTH, 2 * HID), jnp.float32), 'w2': jax.random.normal(ks[4], (DEPTH, HID, DIM), jnp.float32) * 0.02, 'b2': jnp.zeros((DEPTH, DIM), jnp.float32)}
    _L0_ffn_in = _L0_ffn_setup()
    _d = {'L0_attn_a_u': _L0_attn_a_in['u'], 'L0_attn_a_W_in': _L0_attn_a_in['W_in'], 'L0_attn_a_conv_w': _L0_attn_a_in['conv_w'], 'L0_attn_a_conv_b': _L0_attn_a_in['conv_b'], 'L0_attn_a_dt_bias': _L0_attn_a_in['dt_bias'], 'L0_attn_a_A_log': _L0_attn_a_in['A_log'], 'L0_attn_a_D': _L0_attn_a_in['D'], 'L0_attn_a_norm_w': _L0_attn_a_in['norm_w'], 'L0_attn_a_W_out': _L0_attn_a_in['W_out'], 'L0_attn_b_Win': _L0_attn_b_in['Win'], 'L0_attn_b_A_log': _L0_attn_b_in['A_log'], 'L0_attn_b_WB': _L0_attn_b_in['WB'], 'L0_attn_b_WC': _L0_attn_b_in['WC'], 'L0_attn_b_Wdt': _L0_attn_b_in['Wdt'], 'L0_attn_b_bdt': _L0_attn_b_in['bdt'], 'L0_attn_b_dt_bias': _L0_attn_b_in['dt_bias'], 'L0_attn_b_gamma': _L0_attn_b_in['gamma'], 'L0_attn_b_beta': _L0_attn_b_in['beta'], 'L0_attn_b_Wout': _L0_attn_b_in['Wout'], 'L0_ffn_wqkv': _L0_ffn_in['wqkv'], 'L0_ffn_q_scale': _L0_ffn_in['q_scale'], 'L0_ffn_k_scale': _L0_ffn_in['k_scale'], 'L0_ffn_wo': _L0_ffn_in['wo'], 'L0_ffn_ln_g': _L0_ffn_in['ln_g'], 'L0_ffn_ln_b': _L0_ffn_in['ln_b'], 'L0_ffn_w1': _L0_ffn_in['w1'], 'L0_ffn_b1': _L0_ffn_in['b1'], 'L0_ffn_w2': _L0_ffn_in['w2'], 'L0_ffn_b2': _L0_ffn_in['b2']}
    _x0 = _d['L0_attn_a_u']
    _d['L0_attn_a_u'] = jax.random.normal(jax.random.fold_in(jax.random.key(seed), 1), (16, 256, 128), dtype=_x0.dtype)
    del _x0
    return _d

def reference(L0_attn_a_u, L0_attn_a_W_in, L0_attn_a_conv_w, L0_attn_a_conv_b, L0_attn_a_dt_bias, L0_attn_a_A_log, L0_attn_a_D, L0_attn_a_norm_w, L0_attn_a_W_out, L0_attn_b_Win, L0_attn_b_A_log, L0_attn_b_WB, L0_attn_b_WC, L0_attn_b_Wdt, L0_attn_b_bdt, L0_attn_b_dt_bias, L0_attn_b_gamma, L0_attn_b_beta, L0_attn_b_Wout, L0_ffn_wqkv, L0_ffn_q_scale, L0_ffn_k_scale, L0_ffn_wo, L0_ffn_ln_g, L0_ffn_ln_b, L0_ffn_w1, L0_ffn_b1, L0_ffn_w2, L0_ffn_b2):

    def _L0_attn_a_ref(u, W_in, conv_w, conv_b, dt_bias, A_log, D, norm_w, W_out):
        import jax, jax.numpy as jnp
        import numpy as np
        D_MODEL = 128
        D_STATE = 16
        D_CONV = 4
        EXPAND = 2
        HEADDIM = 64
        CHUNK = 64
        D_INNER = EXPAND * D_MODEL
        NHEADS = D_INNER // HEADDIM
        CONV_DIM = D_INNER + 2 * D_STATE
        D_IN_PROJ = 2 * D_INNER + 2 * D_STATE + NHEADS

        def silu(x):
            return x * jax.nn.sigmoid(x)

        def segsum(x):
            T = x.shape[-1]
            xe = jnp.repeat(x[..., None], T, axis=-1)
            mask_lower = jnp.tril(jnp.ones((T, T), bool), -1)
            xe = jnp.where(mask_lower, xe, 0.0)
            s = jnp.cumsum(xe, axis=-2)
            mask_diag = jnp.tril(jnp.ones((T, T), bool), 0)
            return jnp.where(mask_diag, s, -jnp.inf)

        def ssd(x, A, B, C, chunk):
            b, L, h, p = x.shape
            n = B.shape[-1]
            c = L // chunk
            x = x.reshape(b, c, chunk, h, p)
            A = A.reshape(b, c, chunk, h).transpose(0, 3, 1, 2)
            B = jnp.broadcast_to(B[:, :, None] if B.ndim == 3 else B, (b, L, h, n)).reshape(b, c, chunk, h, n)
            C = jnp.broadcast_to(C[:, :, None] if C.ndim == 3 else C, (b, L, h, n)).reshape(b, c, chunk, h, n)
            A_cumsum = jnp.cumsum(A, axis=-1)
            Lmat = jnp.exp(segsum(A))
            Y_diag = jnp.einsum('bclhn,bcshn,bhcls,bcshp->bclhp', C, B, Lmat, x)
            decay_states = jnp.exp(A_cumsum[:, :, :, -1:] - A_cumsum)
            states = jnp.einsum('bclhn,bhcl,bclhp->bchpn', B, decay_states, x)
            init = jnp.zeros_like(states[:, :1])
            states = jnp.concatenate([init, states], axis=1)
            A_last = jnp.pad(A_cumsum[:, :, :, -1], ((0, 0), (0, 0), (1, 0)))
            decay_chunk = jnp.exp(segsum(A_last))
            new_states = jnp.einsum('bhzc,bchpn->bzhpn', decay_chunk, states)
            states, final_state = (new_states[:, :-1], new_states[:, -1])
            state_decay_out = jnp.exp(A_cumsum)
            Y_off = jnp.einsum('bclhn,bchpn,bhcl->bclhp', C, states, state_decay_out)
            Y = (Y_diag + Y_off).reshape(b, L, h, p)
            return (Y, final_state)
        b, L, _ = u.shape
        A = -jnp.exp(A_log)
        zxbcdt = u @ W_in.T
        z = zxbcdt[..., :D_INNER]
        xBC = zxbcdt[..., D_INNER:D_INNER + CONV_DIM]
        dt = jax.nn.softplus(zxbcdt[..., -NHEADS:] + dt_bias)
        conv = jax.lax.conv_general_dilated(xBC.transpose(0, 2, 1), conv_w, window_strides=(1,), padding=[(D_CONV - 1, 0)], feature_group_count=CONV_DIM)
        xBC = silu((conv + conv_b[None, :, None]).transpose(0, 2, 1))
        x = xBC[..., :D_INNER].reshape(b, L, NHEADS, HEADDIM)
        Bm = xBC[..., D_INNER:D_INNER + D_STATE]
        Cm = xBC[..., D_INNER + D_STATE:]
        y, _ = ssd(x * dt[..., None], A * dt, Bm, Cm, CHUNK)
        y = y + x * D[:, None]
        y = y.reshape(b, L, D_INNER)
        y = y * silu(z)
        y = y * jax.lax.rsqrt(jnp.mean(y * y, axis=-1, keepdims=True) + 1e-05) * norm_w
        return y @ W_out.T

    def _L0_attn_b_ref(x, Win, A_log, WB, WC, Wdt, bdt, dt_bias, gamma, beta, Wout):
        import jax, jax.numpy as jnp
        import numpy as np
        B_, T_, D_ = (2, 256, 128)
        DS_, EXPAND_ = (16, 2)
        DI_ = D_ * EXPAND_

        def _forward(x, Win, A_log, WB, WC, Wdt, bdt, dt_bias, gamma, beta, Wout):
            B, T, d = x.shape
            di, ds = A_log.shape
            xz = jnp.einsum('btd,ed->bte', x, Win)
            xi, z = (xz[..., :di], xz[..., di:])
            z = jax.nn.silu(z)
            A = -jnp.exp(A_log)
            Bm = jnp.einsum('btd,sd->bts', x, WB)
            C = jnp.einsum('btd,sd->bts', x, WC)
            dt = jax.nn.softplus(jnp.einsum('btd,ed->bte', x, Wdt) + bdt + dt_bias)
            dtA = dt[..., None] * A
            denom = 1.0 - dtA * 0.5
            A_bar = (1.0 + dtA * 0.5) / denom
            B_bar = dt[..., None] / denom

            def step(state, inp):
                Ab, Bb, Bt, xt, Ct = inp
                state = Ab * state + Bb * Bt[:, None, :] * xt[:, :, None]
                out = jnp.einsum('bds,bs->bd', state, Ct)
                return (state, out)
            tm = lambda a: jnp.swapaxes(a, 0, 1)
            state0 = jnp.zeros((B, di, ds), x.dtype)
            state, outs = jax.lax.scan(step, state0, (tm(A_bar), tm(B_bar), tm(Bm), tm(xi), tm(C)))
            out = jnp.swapaxes(outs, 0, 1) * z
            mu = out.mean(-1, keepdims=True)
            var = ((out - mu) ** 2).mean(-1, keepdims=True)
            normed = (out - mu) * jax.lax.rsqrt(var + 1e-05) * gamma + beta
            y = jnp.einsum('bte,de->btd', normed, Wout)
            return (y, state)

        def _reference_tuple_inner(x, Win, A_log, WB, WC, Wdt, bdt, dt_bias, gamma, beta, Wout):
            return _forward(x, Win, A_log, WB, WC, Wdt, bdt, dt_bias, gamma, beta, Wout)
        return _reference_tuple_inner(x, Win, A_log, WB, WC, Wdt, bdt, dt_bias, gamma, beta, Wout)[0]

    def _L0_ffn_ref(x, wqkv, q_scale, k_scale, wo, ln_g, ln_b, w1, b1, w2, b2):
        import jax, jax.numpy as jnp
        import numpy as np
        DIM = 128
        DEPTH = 2
        HEADS = 8
        DIM_HEAD = 64
        WINDOW = 64
        INNER = HEADS * DIM_HEAD
        HID = int(DIM * 4 * 2 / 3)
        B, N = (2, 1024)
        QK_SCALE = 8.0

        def shift_token(t):
            t1, t2 = jnp.split(t, 2, axis=-1)
            t2 = jnp.pad(t2, ((0, 0), (1, 0), (0, 0)))[:, :-1]
            return jnp.concatenate([t1, t2], axis=-1)

        def l2norm(t):
            return t / jnp.clip(jnp.linalg.norm(t, axis=-1, keepdims=True), 1e-12)

        def rotate_half(x):
            x1, x2 = jnp.split(x, 2, axis=-1)
            return jnp.concatenate([-x2, x1], axis=-1)

        def rotary_xpos(q, k):
            n = q.shape[-2]
            half_idx = jnp.arange(0, DIM_HEAD, 2, dtype=jnp.float32)
            inv_freq = 1.0 / 10000.0 ** (half_idx / DIM_HEAD)
            t = jnp.arange(n, dtype=jnp.float32)
            freqs = t[:, None] * inv_freq[None, :]
            freqs = jnp.concatenate([freqs, freqs], axis=-1)
            base = (half_idx + 0.4 * DIM_HEAD) / (1.4 * DIM_HEAD)
            power = (t - n // 2) / float(WINDOW // 2)
            scale = base[None, :] ** power[:, None]
            scale = jnp.concatenate([scale, scale], axis=-1)
            cos, sin = (jnp.cos(freqs), jnp.sin(freqs))
            q = q * cos * scale + rotate_half(q) * sin * scale
            k = k * cos / scale + rotate_half(k) * sin / scale
            return (q, k)

        def local_attention(q, k, v):
            b, h, n, d = q.shape
            w = n // WINDOW
            bq = q.reshape(b, h, w, WINDOW, d) * QK_SCALE
            bk = k.reshape(b, h, w, WINDOW, d)
            bv = v.reshape(b, h, w, WINDOW, d)

            def look_around(t):
                p = jnp.pad(t, ((0, 0), (0, 0), (1, 0), (0, 0), (0, 0)))
                return jnp.concatenate([p[:, :, :w], p[:, :, 1:]], axis=3)
            bk, bv = (look_around(bk), look_around(bv))
            bt = jnp.arange(n).reshape(w, WINDOW)
            btp = jnp.pad(bt, ((1, 0), (0, 0)), constant_values=-1)
            btk = jnp.concatenate([btp[:w], btp[1:]], axis=1)
            sim = jnp.einsum('bhwid,bhwjd->bhwij', bq, bk)
            i = bt[:, :, None]
            j = btk[:, None, :]
            mask = (i < j) | (i > j + WINDOW) | (j == -1)
            sim = jnp.where(mask, -jnp.finfo(sim.dtype).max, sim)
            attn = jax.nn.softmax(sim, axis=-1)
            out = jnp.einsum('bhwij,bhwjd->bhwid', attn, bv)
            return out.reshape(b, h, n, d)

        def _layer(x, wqkv, qs, ksc, wo, lg, lb, w1, b1, w2, b2):
            b, n, _ = x.shape
            h = shift_token(x)
            qkv = h @ wqkv
            q, k, v = jnp.split(qkv, 3, axis=-1)
            to_heads = lambda t: t.reshape(b, n, HEADS, DIM_HEAD).transpose(0, 2, 1, 3)
            q, k, v = (to_heads(q), to_heads(k), to_heads(v))
            q = l2norm(q) * qs
            k = l2norm(k) * ksc
            q, k = rotary_xpos(q, k)
            o = local_attention(q, k, v)
            o = o.transpose(0, 2, 1, 3).reshape(b, n, INNER)
            x = x + o @ wo
            h = shift_token(x)
            mu = h.mean(-1, keepdims=True)
            var = h.var(-1, keepdims=True)
            h = (h - mu) / jnp.sqrt(var + 1e-05) * lg + lb
            h = h @ w1 + b1
            a, g = jnp.split(h, 2, axis=-1)
            h = a * jax.nn.gelu(g, approximate=False)
            x = x + h @ w2 + b2
            return x
        for l in range(DEPTH):
            x = _layer(x, wqkv[l], q_scale[l], k_scale[l], wo[l], ln_g[l], ln_b[l], w1[l], b1[l], w2[l], b2[l])
        return x
    x = L0_attn_a_u
    x = x + _L0_attn_a_ref(_layernorm(x, axis=-1), L0_attn_a_W_in, L0_attn_a_conv_w, L0_attn_a_conv_b, L0_attn_a_dt_bias, L0_attn_a_A_log, L0_attn_a_D, L0_attn_a_norm_w, L0_attn_a_W_out)
    x = x + _L0_ffn_ref(_layernorm(x, axis=-1), L0_ffn_wqkv, L0_ffn_q_scale, L0_ffn_k_scale, L0_ffn_wo, L0_ffn_ln_g, L0_ffn_ln_b, L0_ffn_w1, L0_ffn_b1, L0_ffn_w2, L0_ffn_b2)
    x = x + _L0_attn_b_ref(_layernorm(x, axis=-1), L0_attn_b_Win, L0_attn_b_A_log, L0_attn_b_WB, L0_attn_b_WC, L0_attn_b_Wdt, L0_attn_b_bdt, L0_attn_b_dt_bias, L0_attn_b_gamma, L0_attn_b_beta, L0_attn_b_Wout)
    x = x + _L0_ffn_ref(_layernorm(x, axis=-1), L0_ffn_wqkv, L0_ffn_q_scale, L0_ffn_k_scale, L0_ffn_wo, L0_ffn_ln_g, L0_ffn_ln_b, L0_ffn_w1, L0_ffn_b1, L0_ffn_w2, L0_ffn_b2)
    return x

_drawn_inputs = setup_inputs


def setup_inputs(seed=0):
    import zlib

    import numpy as np

    out = dict(_drawn_inputs(seed))
    spreads = {'L0_attn_a_conv_b': (0.0, 0.1),
     'L0_attn_a_A_log': (-0.6931471824645996, 0.6),
     'L0_attn_a_D': (1.0, 0.6),
     'L0_attn_a_norm_w': (1.0, 0.2),
     'L0_attn_b_bdt': (0.0, 0.8),
     'L0_attn_b_dt_bias': (-4.0, 0.2),
     'L0_attn_b_gamma': (1.0, 0.6),
     'L0_attn_b_beta': (0.0, 0.476),
     'L0_ffn_q_scale': (1.0, 0.6),
     'L0_ffn_k_scale': (1.0, 0.6),
     'L0_ffn_ln_g': (1.0, 0.6),
     'L0_ffn_ln_b': (0.0, 0.8),
     'L0_ffn_b1': (0.0, 0.8),
     'L0_ffn_b2': (0.0, 0.1)}
    factors = {'L0_attn_a_dt_bias': 24.713,
     'L0_attn_b_A_log': 114.264,
     'L0_attn_b_Wdt': 4.788,
     'L0_ffn_w1': 3.784,
     'L0_ffn_w2': 3.731}
    for name, (base, spread) in spreads.items():
        noise = np.random.default_rng([zlib.crc32(name.encode()), seed]).standard_normal(out[name].shape)
        drawn = base * np.exp(spread * noise) if base else spread * noise
        out[name] = jnp.asarray(drawn.astype(out[name].dtype))
    for name, factor in factors.items():
        out[name] = (out[name] * factor).astype(out[name].dtype)
    return out
```

```python
import numpy as np
import concourse.bass as bass
from concourse import mybir
from contextlib import ExitStack

D, SEQ, BATCH = 128, 256, 16
NT = 2 * SEQ
PAIRS = BATCH // 2
NTOK = BATCH * SEQ
HEADS, DH, WINDOW, DEPTH = 8, 64, 64, 2
INNER = HEADS * DH
HID = 341
HID_TILES = [(0, 128), (128, 128), (256, HID - 256)]
DI = 256
NS = 16
SSD_HEADS = 4
CONV = 4
MASKED = -1e30
QK_SCALE = 8.0
SS_SCALE = 2.0 ** 32
SS_FLOOR = 2.0 ** -63
LN_UNSCALE = 16 * float(np.log(2.0))
NORM_CLIP = 1e12
EPS = 1e-5


def layout(sizes):
    at, out = 0, {}
    for name, n in sizes:
        out[name] = (at, n)
        at += n
    return out, at


FIRST, N_FIRST = layout([
    ("ident", 128), ("mean128", 128), ("mean256", 128), ("ones", 128), ("le", 128), ("strict", 256),
    ("a_win", 548), ("a_convw", CONV * 288), ("a_convb", 2), ("a_convb_bc", 2), ("a_dtb", 16),
    ("a_alog", 16), ("a_d", 2), ("a_normw", 2), ("a_wout", 2 * 128)])
LAYER = [("wqkv", 3 * INNER), ("wrot", 2 * INNER), ("wo", 4 * 128), ("w1", 2 * HID), ("w2", 3 * 128),
         ("b1", 6), ("b2", 1), ("lg", 1), ("lb", 1), ("qs", 1), ("qsr", 1), ("ks", 1), ("ksr", 1)]
REST, N_REST = layout(
    [("head128", 128), ("head2", 2), ("cq", SEQ), ("sq", SEQ), ("ck", SEQ), ("sk", SEQ)]
    + [(f"{name}{l}", n) for l in range(DEPTH) for name, n in LAYER]
    + [("b_win", 4 * 128), ("b_wbc", 32), ("b_wdt", 2 * 128), ("b_alog", 2 * NS), ("b_bdt", 2), ("b_dtb", 2),
       ("b_gamma", 2), ("b_beta", 2), ("b_wout", 2 * 128)])
BF, N_BF = layout([("ident16", 128), ("band", 384), ("causal", 384), ("sel", 32 * 128)])


def program(nc, x_in, first_in, rest_in, bf_in, out):
    f32, bf16 = mybir.dt.float32, mybir.dt.bfloat16
    ACT, ALU, AX = mybir.ActivationFunctionType, mybir.AluOpType, mybir.AxisListType
    ctx = ExitStack()
    with ctx:
        def sb(name, shape, dt=f32):
            return ctx.enter_context(nc.sbuf_tensor(name, shape, dt))

        def sem(name):
            return ctx.enter_context(nc.semaphore(name))

        X = sb("X", [128, NTOK])
        first = sb("first", [128, N_FIRST])
        rest = sb("rest", [128, N_REST])
        tabs16 = sb("tabs16", [128, N_BF], bf16)

        def F(name, a=0, b=None, p=128):
            at, n = FIRST[name]
            return first[0:p, at + a:at + (n if b is None else b)]

        def W(name, a=0, b=None, p0=0, p=128):
            at, n = REST[name]
            return rest[p0:p, at + a:at + (n if b is None else b)]

        def T16(name, a=0, b=None, p=128):
            at, n = BF[name]
            return tabs16[0:p, at + a:at + (n if b is None else b)]

        ARENA = 19456
        arena = sb("arena", [128, ARENA])
        used = {}

        def shared(phase, shape):
            at = used.get(phase, 0)
            n = int(np.prod(shape[1:]))
            used[phase] = at + n
            assert used[phase] <= ARENA
            a = arena[0:shape[0], at:at + n]
            if len(shape) == 3:
                a = a.rearrange("p (a b) -> p a b", a=shape[1])
            if len(shape) == 4:
                a = a.rearrange("p (a b c) -> p a b c", a=shape[1], b=shape[2])
            return a

        bank = [ctx.enter_context(nc.psum_tensor(f"bank{k}", [128, 512], f32)) for k in range(8)]
        STAT = bank[7]

        XC = sb("XC", [128, NT])
        CEN = sb("CEN", [128, NT])
        LSQ = sb("LSQ", [128, NT])
        LLOG = sb("LLOG", [128, NT])
        LRS = sb("LRS", [128, NT])
        ln_in = sem("ln_in")
        ln_mean = sem("ln_mean")
        ln_cen = sem("ln_cen")
        ln_sq = sem("ln_sq")
        ln_var = sem("ln_var")
        ln_log = sem("ln_log")
        ln_rs = sem("ln_rs")
        ln_out = sem("ln_out")

        def ln_pe(pe, n, src):
            pe.wait_ge(ln_in, n + 1)
            nc.tensor.matmul(STAT[:, :], F("mean128"), src, start=True, stop=True).then_inc(ln_mean, 1)
            pe.wait_ge(ln_sq, n + 1)
            nc.tensor.matmul(STAT[:, :], F("mean128"), LSQ[:, :], start=True, stop=True).then_inc(ln_var, 1)

        def ln_act(act, n):
            act.wait_ge(ln_cen, n + 1)
            nc.scalar.activation(LSQ[:, :], CEN[:, :], ACT.Square).then_inc(ln_sq, 1)
            act.wait_ge(ln_var, n + 1)
            nc.scalar.activation(LLOG[:, :], STAT[:, :], ACT.Ln, bias=eps_col[:, :]).then_inc(ln_log, 1)
            act.wait_ge(ln_log, n + 1)
            nc.scalar.activation(LRS[:, :], LLOG[:, :], ACT.Exp, scale=-0.5).then_inc(ln_rs, 1)

        def ln_dve(dve, n, src, dst):
            dve.wait_ge(ln_mean, n + 1)
            nc.vector.tensor_tensor(CEN[:, :], src, STAT[:, :], ALU.subtract).then_inc(ln_cen, 1)
            dve.wait_ge(ln_rs, n + 1)
            dve.wait_ge(ln_cen, n + 1)
            nc.vector.tensor_tensor(dst, pair(CEN), pair(LRS), ALU.mult).then_inc(ln_out, 1)

        def pair(t):
            return t[:, :].rearrange("p (b t) -> p b t", b=2)

        eps_col = sb("eps_col", [128, 1])
        floor_col = sb("floor_col", [128, 1])
        unscale_col = sb("unscale_col", [128, 1])
        convW = sb("convW", [128, CONV, 288])
        a_exp = sb("a_exp", [128, 16])
        sg_bias = sb("sg_bias", [128, 2 * NS])
        th_bias = sb("th_bias", [128, 2 * NS])
        dt_bias_b = sb("dt_bias_b", [128, 2])
        out_bias_b = sb("out_bias_b", [128, 1])
        tab = sb("tab", [128, DEPTH, 4, SEQ])
        b1f = sb("b1f", [128, DEPTH, 6])
        in_first = sem("in_first")
        in_x = sem("in_x")
        in_rest = sem("in_rest")
        pre_a = sem("pre_a")
        pre_aexp = sem("pre_aexp")
        pre_ps = sem("pre_ps")
        pre_fold = sem("pre_fold")
        pre_b = sem("pre_b")

        XN = sb("XN", [128, 2, SEQ + CONV - 1])
        ZS = shared("ssd", [128, 2, NT])
        XA = shared("ssd", [128, 2, NT])
        BA = shared("ssd", [NS, NT])
        CA = shared("ssd", [NS, NT])
        sp = sb("sp", [128, 10, 16])
        adt = sb("adt", [128, 16])
        AM = sb("AM", [128, 2, 3, 128])
        LM = shared("ssd", [128, 2, 384])
        MM = shared("ssd", [128, 2, 384])
        XT = shared("ssd", [128, 4, DI])
        Y = shared("ssd", [128, 2, NT])
        YS = shared("ssd", [128, 2, NT])
        a_z = sem("a_z")
        a_dt = sem("a_dt")
        a_act = sem("a_act")
        a_sp = sem("a_sp")
        a_spd = sem("a_spd")
        a_adt1 = sem("a_adt1")
        a_adt = sem("a_adt")
        a_xtp = sem("a_xtp")
        a_xt = sem("a_xt")
        a_cb = sem("a_cb")
        a_am = sem("a_am")
        a_seg = sem("a_seg")
        a_lm = sem("a_lm")
        a_mm = sem("a_mm")
        a_y = sem("a_y")
        a_yd = sem("a_yd")
        a_yg = sem("a_yg")
        a_ysq = sem("a_ysq")
        a_ms = sem("a_ms")
        a_log = sem("a_log")
        a_rs = sem("a_rs")
        a_yn = sem("a_yn")
        a_out = sem("a_out")
        a_x = sem("a_x")

        R = shared("layers", [128, NT])
        HA = sb("HA", [128, NT])
        HF = sb("HF", [128, NT])
        HN = sb("HN", [128, NT])
        SQ = shared("layers", [128, 2, NT])
        T1 = shared("layers", [128, 2, NT])
        T2 = shared("layers", [128, 2, NT])
        KS = shared("layers", [128, 2, NT])
        KL = shared("layers", [128, 2, NT])
        KR = shared("layers", [128, 2, NT])
        QT = shared("layers", [128, 4, NT])
        KT = shared("layers", [128, 4, NT])
        QL = sb("QL", [128, 32])
        QR = sb("QR", [128, 32])
        QS = sb("QS", [128, 32])
        NQ = sb("NQ", [128, 32])
        VT = sb("VT", [128, 4, HEADS, DH + 1])
        MX = sb("MX", [128, 2, 4])
        NB = sb("NB", [128, 2, 4])
        P = sb("P", [128, 2, 2, 384])
        PT = shared("layers", [128, 2, 2, 384])
        RC = sb("RC", [128, 2, 4])
        OS = shared("layers", [128, 4, HEADS, DH])
        OT = shared("layers", [128, 4, NT])
        GE = shared("layers", [128, 2, NT])
        GA = shared("layers", [128, 3, NT])
        f_h = sem("f_h")
        f_qk = sem("f_qk")
        f_prod = sem("f_prod")
        f_sq = sem("f_sq")
        f_rope = sem("f_rope")
        f_qss = sem("f_qss")
        f_kss = sem("f_kss")
        f_qlog = sem("f_qlog")
        f_qr = sem("f_qr")
        f_qs = sem("f_qs")
        f_nq = sem("f_nq")
        f_klog = sem("f_klog")
        f_kr = sem("f_kr")
        f_k = sem("f_k")
        f_vps = sem("f_vps")
        f_v = sem("f_v")
        f_sim = sem("f_sim")
        f_mx = sem("f_mx")
        f_nb = sem("f_nb")
        f_exp = sem("f_exp")
        f_ptp = sem("f_ptp")
        f_pta = sem("f_pta")
        f_ptd = sem("f_ptd")
        f_ops = sem("f_ops")
        f_rc = sem("f_rc")
        f_os = sem("f_os")
        f_otp = sem("f_otp")
        f_ot = sem("f_ot")
        f_at = sem("f_at")
        f_r1 = sem("f_r1")
        f_ag = sem("f_ag")
        f_ge = sem("f_ge")
        f_ga = sem("f_ga")
        f_ff = sem("f_ff")
        f_r2 = sem("f_r2")
        f_x = sem("f_x")

        used["mamba"] = used["ssd"]
        XI = shared("mamba", [128, 2, NT])
        SPB = shared("mamba", [128, 4, 2, NT])
        U = shared("mamba", [128, 2, NT])
        LD = shared("mamba", [128, 2, NT])
        BR = shared("mamba", [32, 2, NT])
        BS = sb("BS", [96, NT], bf16)
        RG = shared("mamba", [128, 2, NT])
        AB = shared("mamba", [128, 2, NT])
        WU = SPB[:, 0, :, :]
        VB = SPB[:, 1, :, :]
        HS = SPB[:, 2, :, :]
        PC = SPB[:, 3, :, :]
        m_pr = sem("m_pr")
        m_ev = sem("m_ev")
        m_a1 = sem("m_a1")
        m_a2 = sem("m_a2")
        m_a3 = sem("m_a3")
        m_d = sem("m_d")
        m_u = sem("m_u")
        m_ld = sem("m_ld")
        m_bs = sem("m_bs")
        m_bd = sem("m_bd")
        m_bc = sem("m_bc")
        m_rg = sem("m_rg")
        m_ab = sem("m_ab")
        m_wu = sem("m_wu")
        m_vb = sem("m_vb")
        m_hs = sem("m_hs")
        m_pc = sem("m_pc")
        m_acc = sem("m_acc")
        m_g = sem("m_g")
        m_mean = sem("m_mean")
        m_cen = sem("m_cen")
        m_sq = sem("m_sq")
        m_var = sem("m_var")
        m_log = sem("m_log")
        m_rs = sem("m_rs")
        m_n = sem("m_n")
        m_out = sem("m_out")
        m_x = sem("m_x")
        out_done = sem("out_done")

        block = ctx.enter_context(nc.Block())

        LN_A, LN_F, LN_M = 0, (8, 40), 32

        @block.sync
        def _(sp_):
            sp_.dma_start(first[:, :], first_in).then_inc(in_first, 16)
            sp_.dma_start(X[:, :], x_in).then_inc(in_x, 16)
            sp_.dma_start(tabs16[:, :], bf_in).then_inc(in_first, 16)
            sp_.dma_start(rest[:, :], rest_in).then_inc(in_rest, 16)
            with sp_.Fori(0, PAIRS) as i:
                sp_.wait_ge(f_x, i + (PAIRS + 1))
                sp_.dma_start(out[:, bass.ds(i * NT, NT)], X[:, bass.ds(i * NT, NT)]).then_inc(out_done, 16)
            sp_.wait_ge(out_done, 16 * PAIRS)

        @block.gpsimd
        def _(pool):
            pool.wait_ge(in_first, 32)
            with pool.Fori(0, PAIRS) as i:
                pool.wait_ge(a_adt, i + 1)
                for q in range(8):
                    b, h = divmod(q, SSD_HEADS)
                    if q >= 2:
                        pool.wait_ge(a_seg, i * 8 + (q - 1))
                    a = adt[:, :].rearrange("p (b t h) -> p b t h", b=2, t=2)[:, b, :, h:h + 1]
                    nc.gpsimd.tensor_tensor(AM[:, q % 2, 0:2, :], F("strict").rearrange("p (t s) -> p t s", t=2),
                                            a.to_broadcast([128, 2, 128]), ALU.mult)
                    nc.gpsimd.tensor_tensor(AM[:, q % 2, 2, :], F("ones"), a[:, 1, :].to_broadcast([128, 128]),
                                            ALU.mult).then_inc(a_am, 1)

            def layers_pool(ph):
                with pool.Fori(0, PAIRS) as i:
                    for l in range(DEPTH):
                        u8 = i * 16 + 8 * (2 * PAIRS * ph + l)
                        u4 = i * 8 + 4 * (2 * PAIRS * ph + l)
                        for j in range(8):
                            pool.wait_ge(f_prod, u8 + (j + 1))
                            if j >= 6:
                                pool.wait_ge(f_k, u4 + (j - 5))
                            dst = QT[:, j, :] if j < 4 else KS[:, j % 2, :]
                            nc.gpsimd.tensor_tensor(dst, T1[:, j % 2, :], T2[:, j % 2, :], ALU.add).then_inc(f_rope, 1)

            layers_pool(0)
            with pool.Fori(0, PAIRS) as i:
                for s in range(NS):
                    for hf in range(2):
                        k = 2 * s + hf
                        pool.wait_ge(m_rg, i * 32 + (k + 1))
                        if k == 0:
                            pool.wait_ge(m_u, i + 1)
                        if k >= 2:
                            pool.wait_ge(m_vb, i * 32 + (k - 1))
                        nc.gpsimd.tensor_tensor(WU[:, hf, :], RG[:, hf, :], U[:, hf, :], ALU.mult).then_inc(m_wu, 1)
            layers_pool(1)

        @block.tensor
        def _(pe):
            mm = nc.tensor.matmul
            pe.wait_ge(in_first, 32)
            pe.wait_ge(pre_a, 1)
            with pe.Fori(0, PAIRS) as i:
                ln_pe(pe, i + LN_A, XC[:, :])
                pe.wait_ge(ln_out, i + (LN_A + 1))
                for tt in range(4):
                    b, t = divmod(tt, 2)
                    last = mm(bank[5][:, 4 * tt:4 * tt + 4], XN[:, b, 3 + 128 * t:131 + 128 * t],
                              F("a_win", 544, 548), start=True, stop=True)
                last.then_inc(a_dt, 1)
                for k in range(2):
                    for c in range(CONV):
                        last = mm(bank[2 + k][:, :], convW[:, c, 128 * k:128 * k + 128], XN[:, :, c:c + SEQ],
                                  start=c == 0, stop=c == CONV - 1)
                    last.then_inc(a_z, 1)
                for k, dst in ((0, bank[4]), (1, bank[6])):
                    for c in range(CONV):
                        last = mm(dst[0:NS, :], convW[:, c, 256 + NS * k:256 + NS * (k + 1)], XN[:, :, c:c + SEQ],
                                  start=c == 0, stop=c == CONV - 1)
                    last.then_inc(a_z, 1)
                for k in range(2):
                    mm(bank[k][:, :], F("a_win", 128 * k, 128 * k + 128), XN[:, :, 3:3 + SEQ],
                       start=True, stop=True).then_inc(a_z, 1)
                pe.wait_ge(a_act, i * 6 + 4)
                for tt in range(4):
                    for k in range(2):
                        last = nc.tensor.transpose(bank[2 + tt // 2][:, 256 * (tt % 2) + 128 * k:256 * (tt % 2) + 128 * k + 128],
                                                   XA[:, k, 128 * tt:128 * tt + 128], F("ident"))
                    last.then_inc(a_xtp, 1)
                pe.wait_ge(a_act, i * 6 + 6)
                pe.wait_ge(a_xt, i * 4 + 4)

                def segsum(q):
                    seg = bank[q % 2]
                    pe.wait_ge(a_am, i * 8 + (q + 1))
                    if q >= 2:
                        pe.wait_ge(a_lm, i * 8 + (q - 1))
                    mm(seg[:, 0:384], T16("ident16"), T16("causal"), start=True, stop=False)
                    mm(seg[:, 0:128], AM[:, q % 2, 0, :], F("le"), start=False, stop=False)
                    mm(seg[:, 128:256], AM[:, q % 2, 0, :], F("ones"), start=False, stop=False)
                    mm(seg[:, 128:256], AM[:, q % 2, 2, :], F("le"), start=False, stop=False)
                    mm(seg[:, 256:384], AM[:, q % 2, 1, :], F("le"), start=False, stop=True).then_inc(a_seg, 1)

                def head_out(q):
                    b, h = divmod(q, SSD_HEADS)
                    pe.wait_ge(a_mm, i * 8 + (q + 1))
                    y = bank[2 + h // 2][64 * (h % 2):64 * (h % 2) + 64, :]
                    xh = XT[:, :, DH * h:DH * h + DH]
                    mm(y[:, SEQ * b:SEQ * b + SEQ], xh[:, 2 * b, :], MM[:, q % 2, 0:256], start=True, stop=False)
                    mm(y[:, SEQ * b + 128:SEQ * b + SEQ], xh[:, 2 * b + 1, :], MM[:, q % 2, 256:384],
                       start=False, stop=True).then_inc(a_y, 1)

                for b, cb in ((0, bank[4]), (1, bank[6])):
                    mm(cb[:, 0:256], BA[:, SEQ * b:SEQ * b + 128], CA[:, SEQ * b:SEQ * b + SEQ], start=True, stop=True)
                    mm(cb[:, 256:384], BA[:, SEQ * b + 128:SEQ * b + SEQ], CA[:, SEQ * b + 128:SEQ * b + SEQ],
                       start=True, stop=True).then_inc(a_cb, 1)
                segsum(0)
                for q in range(8):
                    if q < 7:
                        segsum(q + 1)
                    head_out(q)
                pe.wait_ge(a_ysq, i * 2 + 2)
                for k in range(2):
                    last = mm(STAT[:, :], F("mean256"), YS[:, k, :], start=k == 0, stop=k == 1)
                last.then_inc(a_ms, 1)
                pe.wait_ge(a_yn, i * 2 + 2)
                for k in range(2):
                    last = mm(STAT[:, :], F("a_wout", 128 * k, 128 * k + 128), Y[:, k, :], start=k == 0, stop=k == 1)
                last.then_inc(a_out, 1)

            pe.wait_ge(in_rest, 16)
            pe.wait_ge(a_x, PAIRS)
            for l in range(DEPTH):
                for g in range(2):
                    for m, (at, size) in enumerate(HID_TILES):
                        mm(bank[0][0:size, 8 * l + 3 * g + m:8 * l + 3 * g + m + 1],
                           W(f"w1{l}", HID * g + at, HID * g + at + size), W(f"lb{l}"), start=True, stop=True)
            for k in range(2):
                last = mm(bank[0][:, 16:17], W("b_wout", 128 * k, 128 * k + 128), W("b_beta", k, k + 1),
                          start=k == 0, stop=k == 1)
            last.then_inc(pre_ps, 1)
            pe.wait_ge(pre_b, 1)

            def layers_pe(ph):
                with pe.Fori(0, PAIRS) as i:
                    ln_pe(pe, i * 3 + LN_F[ph], XC[:, :])
                    for l in range(DEPTH):
                        u = i * 2 + (2 * PAIRS * ph + l)

                        def upto(per, n):
                            return i * (2 * per) + (per * (2 * PAIRS * ph + l) + n)

                        pe.wait_ge(f_h, upto(1, 1))

                        def project(j):
                            base = 128 * j
                            if j >= 2:
                                pe.wait_ge(f_prod, upto(8, j - 1))
                                pe.wait_ge(f_sq, upto(8, j - 1))
                            mm(bank[2 * (j % 2)][:, :], W(f"wqkv{l}", base, base + 128), HA[:, :], start=True, stop=True)
                            mm(bank[2 * (j % 2) + 1][:, :], W(f"wrot{l}", base, base + 128), HA[:, :],
                               start=True, stop=True).then_inc(f_qk, 1)

                        def sums(j):
                            pe.wait_ge(f_sq, upto(8, j + 1))
                            if j < 4:
                                cols = bank[6][:, 0:32].rearrange("p (h b k) -> p h b k", h=HEADS, b=2)
                                for tt in range(4):
                                    b, t = divmod(tt, 2)
                                    last = mm(cols[:, 2 * j:2 * j + 2, b, 1 - t], SQ[:, j % 2, 128 * tt:128 * tt + 128],
                                              W("head2"), start=True, stop=True)
                                last.then_inc(f_qss, 1)
                            else:
                                if j >= 6:
                                    pe.wait_ge(f_klog, upto(4, j - 5))
                                mm(bank[4 + j % 2][:, :], W("head128"), SQ[:, j % 2, :],
                                   start=True, stop=True).then_inc(f_kss, 1)

                        project(0)
                        for j in range(8):
                            if j < 7:
                                project(j + 1)
                            sums(j)
                        for tt in range(4):
                            if tt < 2:
                                pe.wait_ge(f_klog, upto(4, tt + 3))
                            else:
                                pe.wait_ge(f_v, upto(4, tt - 1))
                            mm(bank[4 + tt % 2][:, :], HA[:, 128 * tt:128 * tt + 128],
                               W(f"wqkv{l}", 2 * INNER, 3 * INNER), start=True, stop=True).then_inc(f_vps, 1)
                        pe.wait_ge(f_rope, upto(8, 8))
                        pe.wait_ge(f_k, upto(4, 4))

                        def scores(g):
                            b, j = divmod(g, 4)
                            if g >= 2:
                                pe.wait_ge(f_exp, upto(8, g - 1))
                            for hh in range(2):
                                s, rows = bank[2 * (g % 2) + hh], slice(64 * hh, 64 * hh + 64)
                                mm(s[:, 0:384], T16("ident16"), T16("band"), start=True, stop=False)
                                mm(s[:, 0:192], QT[rows, j, SEQ * b + 128:SEQ * b + 256],
                                   KT[rows, j, SEQ * b + 64:SEQ * b + 256], start=False, stop=False)
                                last = mm(s[:, 256:384], QT[rows, j, SEQ * b:SEQ * b + 128],
                                          KT[rows, j, SEQ * b:SEQ * b + 128], start=False, stop=True)
                            last.then_inc(f_sim, 1)

                        def attend(g):
                            b, j = divmod(g, 4)
                            pe.wait_ge(f_exp, upto(8, g + 1))
                            if g == 0:
                                pe.wait_ge(f_v, upto(4, 4))
                            if g >= 1:
                                pe.wait_ge(f_pta, upto(8, g))
                                pe.wait_ge(f_ptd, upto(8, g))
                            for hh in range(2):
                                for c in range(3):
                                    last = nc.tensor.transpose(bank[4 + hh][:, 128 * c:128 * c + 128],
                                                               P[:, g % 2, hh, 128 * c:128 * c + 128], F("ident"))
                            last.then_inc(f_ptp, 1)

                        def weigh(g):
                            b, j = divmod(g, 4)
                            pe.wait_ge(f_pta, upto(8, g + 1))
                            pe.wait_ge(f_ptd, upto(8, g + 1))
                            if g >= 2:
                                pe.wait_ge(f_os, upto(8, g - 1))
                            o = bank[6 + g % 2][:, 0:4 * (DH + 1)].rearrange("p (h k d) -> p h k d", h=2, k=2)
                            for hh in range(2):
                                h = 2 * j + hh
                                pt = PT[:, g % 2, hh, :]
                                mm(o[:, hh, 0, :], pt[:, 0:128], VT[:, 2 * b, h, :], start=True, stop=False)
                                mm(o[:, hh, 0, :], pt[:, 128:256], VT[:, 2 * b + 1, h, :], start=False, stop=True)
                                last = mm(o[:, hh, 1, :], pt[:, 256:384], VT[:, 2 * b, h, :], start=True, stop=True)
                            last.then_inc(f_ops, 1)

                        scores(0)
                        pe.wait_ge(f_qs, upto(1, 1))
                        for g in range(8):
                            if g < 7:
                                scores(g + 1)
                            attend(g)
                            if g >= 1:
                                weigh(g - 1)
                        weigh(7)
                        pe.wait_ge(f_os, upto(8, 8))

                        def back(j):
                            if j >= 2:
                                pe.wait_ge(f_ot, upto(4, j - 1))
                            for tt in range(4):
                                b, t = divmod(tt, 2)
                                last = nc.tensor.transpose(bank[4 + j % 2][:, 128 * tt:128 * tt + 128],
                                                           OS[:, 2 * b + 1 - t, 2 * j:2 * j + 2, :].rearrange("p h d -> p (h d)"),
                                                           F("ident"))
                            last.then_inc(f_otp, 1)

                        back(0)
                        for j in range(4):
                            if j < 3:
                                back(j + 1)
                            pe.wait_ge(f_ot, upto(4, j + 1))
                            last = mm(STAT[:, :], W(f"wo{l}", 128 * j, 128 * j + 128), OT[:, j, :],
                                      start=j == 0, stop=j == 3)
                        last.then_inc(f_at, 1)
                        ln_pe(pe, i * 3 + (LN_F[ph] + 1 + l), HF[:, :])
                        pe.wait_ge(ln_out, i * 3 + (LN_F[ph] + 2 + l))

                        def hidden(m):
                            at, size = HID_TILES[m]
                            if m >= 2:
                                pe.wait_ge(f_ga, upto(3, m - 1))
                            mm(bank[2 * (m % 2)][0:size, :], W(f"w1{l}", at, at + size), HN[:, :], start=True, stop=True)
                            mm(bank[2 * (m % 2) + 1][0:size, :], W(f"w1{l}", HID + at, HID + at + size), HN[:, :],
                               start=True, stop=True).then_inc(f_ag, 1)

                        hidden(0)
                        for m in range(3):
                            if m < 2:
                                hidden(m + 1)
                            size = HID_TILES[m][1]
                            pe.wait_ge(f_ga, upto(3, m + 1))
                            last = mm(STAT[:, :], W(f"w2{l}", 128 * m, 128 * m + 128, p=size), GA[0:size, m, :],
                                      start=m == 0, stop=m == 2)
                        last.then_inc(f_ff, 1)

            layers_pe(0)

            with pe.Fori(0, PAIRS) as i:
                ln_pe(pe, i + LN_M, XC[:, :])
                pe.wait_ge(ln_out, i + (LN_M + 1))
                for k in range(2):
                    mm(bank[k][:, :], W("b_wdt", 128 * k, 128 * k + 128), HN[:, :], start=True, stop=True).then_inc(m_pr, 1)
                for k in range(4):
                    mm(bank[2 + k][:, :], W("b_win", 128 * k, 128 * k + 128), HN[:, :], start=True, stop=True).then_inc(m_pr, 1)
                mm(bank[6][0:32, :], W("b_wbc"), HN[:, :], start=True, stop=True).then_inc(m_pr, 1)
                pe.wait_ge(m_bs, i * 3 + 3)
                pe.wait_ge(m_bd, i * 2 + 2)
                pe.wait_ge(m_ev, i * 4 + 4)
                pe.wait_ge(m_u, i + 1)

                def spread(s):
                    if s >= 2:
                        pe.wait_ge(m_pc, i * 32 + (2 * s - 2))
                    mm(bank[2 * (s % 2)][:, :], T16("sel", 128 * s, 128 * s + 128, p=96), BS[:, :], start=True, stop=True)
                    mm(bank[2 * (s % 2) + 1][:, :], T16("sel", 128 * (NS + s), 128 * (NS + s) + 128, p=96), BS[:, :],
                       start=True, stop=True).then_inc(m_bc, 1)

                spread(0)
                for s in range(NS):
                    if s + 1 < NS:
                        spread(s + 1)
                    for hf in range(2):
                        pe.wait_ge(m_pc, i * 32 + (2 * s + hf + 1))
                        mm(bank[4 + hf][:, :], F("ident"), PC[:, hf, :], start=s == 0, stop=s == NS - 1).then_inc(m_acc, 1)
                pe.wait_ge(m_g, i * 2 + 2)
                for k in range(2):
                    last = mm(STAT[:, :], F("mean256"), Y[:, k, :], start=k == 0, stop=k == 1)
                last.then_inc(m_mean, 1)
                pe.wait_ge(m_sq, i * 2 + 2)
                for k in range(2):
                    last = mm(STAT[:, :], F("mean256"), YS[:, k, :], start=k == 0, stop=k == 1)
                last.then_inc(m_var, 1)
                pe.wait_ge(m_n, i * 2 + 2)
                for k in range(2):
                    last = mm(STAT[:, :], W("b_wout", 128 * k, 128 * k + 128), Y[:, k, :], start=k == 0, stop=k == 1)
                last.then_inc(m_out, 1)
            layers_pe(1)

        @block.scalar
        def _(act):
            A = nc.scalar.activation
            act.wait_ge(in_first, 32)
            A(a_exp[:, :], F("a_alog"), ACT.Exp).then_inc(pre_aexp, 1)
            act.wait_ge(pre_a, 1)
            with act.Fori(0, PAIRS) as i:
                ln_act(act, i + LN_A)
                act.wait_ge(a_spd, i * 2 + 1)
                A(sp[:, 1, :], sp[:, 0, :], ACT.Abs).then_inc(a_sp, 1)
                act.wait_ge(a_sp, i * 3 + 1)
                A(sp[:, 2, :], sp[:, 1, :], ACT.Exp, scale=-1.0).then_inc(a_sp, 1)
                act.wait_ge(a_spd, i * 2 + 2)
                A(sp[:, 4, :], sp[:, 3, :], ACT.Ln).then_inc(a_sp, 1)
                for k in range(2):
                    act.wait_ge(a_z, i * 6 + (k + 1))
                    A(XA[:, k, :], bank[2 + k][:, :], ACT.Silu, bias=F("a_convb", k, k + 1)).then_inc(a_act, 1)
                for k, (dst, src) in enumerate(((BA, bank[4]), (CA, bank[6]))):
                    act.wait_ge(a_z, i * 6 + (k + 3))
                    A(dst[:, :], src[0:NS, :], ACT.Silu, bias=F("a_convb_bc", k, k + 1, p=NS)).then_inc(a_act, 1)
                for k in range(2):
                    act.wait_ge(a_z, i * 6 + (k + 5))
                    A(ZS[:, k, :], bank[k][:, :], ACT.Silu).then_inc(a_act, 1)
                for q in range(8):
                    act.wait_ge(a_seg, i * 8 + (q + 1))
                    if q >= 2:
                        act.wait_ge(a_mm, i * 8 + (q - 1))
                    A(LM[:, q % 2, :], bank[q % 2][:, 0:384], ACT.Exp).then_inc(a_lm, 1)
                for k in range(2):
                    act.wait_ge(a_yg, i * 2 + (k + 1))
                    A(YS[:, k, :], Y[:, k, :], ACT.Square).then_inc(a_ysq, 1)
                act.wait_ge(a_ms, i + 1)
                A(LLOG[:, :], STAT[:, :], ACT.Ln, bias=eps_col[:, :]).then_inc(a_log, 1)
                act.wait_ge(a_log, i + 1)
                A(LRS[:, :], LLOG[:, :], ACT.Exp, scale=-0.5).then_inc(a_rs, 1)

            act.wait_ge(pre_b, 1)

            def layers_act(ph):
                with act.Fori(0, PAIRS) as i:
                    ln_act(act, i * 3 + LN_F[ph])
                    for l in range(DEPTH):
                        def upto(per, n):
                            return i * (2 * per) + (per * (2 * PAIRS * ph + l) + n)

                        def squares(j):
                            act.wait_ge(f_qk, upto(8, j + 1))
                            if 2 <= j < 6:
                                act.wait_ge(f_qss, upto(4, j - 1))
                            elif j >= 6:
                                act.wait_ge(f_kss, upto(4, j - 5))
                            A(SQ[:, j % 2, :], bank[2 * (j % 2)][:, :], ACT.Square).then_inc(f_sq, 1)

                        def k_norm(k):
                            act.wait_ge(f_kss, upto(4, k + 1))
                            A(KL[:, k % 2, :], bank[4 + k % 2][:, :], ACT.Ln, bias=floor_col[:, :],
                              scale=SS_SCALE).then_inc(f_klog, 1)
                            act.wait_ge(f_klog, upto(4, k + 1))
                            if k >= 2:
                                act.wait_ge(f_k, upto(4, k - 1))
                            A(KR[:, k % 2, :], KL[:, k % 2, :], ACT.Exp, bias=unscale_col[:, :], scale=-0.5).then_inc(f_kr, 1)

                        for j in range(5):
                            squares(j)
                        act.wait_ge(f_qss, upto(4, 4))
                        A(QL[:, :], bank[6][:, 0:32], ACT.Ln, bias=floor_col[:, :], scale=SS_SCALE).then_inc(f_qlog, 1)
                        act.wait_ge(f_qlog, upto(1, 1))
                        A(QR[:, :], QL[:, :], ACT.Exp, bias=unscale_col[:, :], scale=-0.5).then_inc(f_qr, 1)
                        for j in range(5, 8):
                            squares(j)
                            k_norm(j - 5)
                        k_norm(3)
                        for tt in range(4):
                            act.wait_ge(f_vps, upto(4, tt + 1))
                            A(VT[:, tt, :, 0:DH], bank[4 + tt % 2][:, :].rearrange("p (h d) -> p h d", h=HEADS),
                              ACT.Copy).then_inc(f_v, 1)

                        def probabilities(g):
                            b, j = divmod(g, 4)
                            act.wait_ge(f_nb, upto(8, g + 1))
                            if g >= 2:
                                act.wait_ge(f_ptp, upto(8, g - 1))
                            for hh in range(2):
                                s = bank[2 * (g % 2) + hh]
                                col = (2 * j + hh) * 4 + 2 * b
                                A(P[:, g % 2, hh, 64:256], s[:, 0:192], ACT.Exp, bias=NB[:, g % 2, 2 * hh:2 * hh + 1],
                                  scale=QS[:, col:col + 1])
                                last = A(P[:, g % 2, hh, 256:384], s[:, 256:384], ACT.Exp,
                                         bias=NB[:, g % 2, 2 * hh + 1:2 * hh + 2], scale=QS[:, col + 1:col + 2])
                            last.then_inc(f_exp, 1)

                        def transposed(g):
                            act.wait_ge(f_ptp, upto(8, g + 1))
                            if g >= 2:
                                act.wait_ge(f_ops, upto(8, g - 1))
                            A(PT[:, g % 2, 0, :], bank[4][:, 0:384], ACT.Copy).then_inc(f_pta, 1)

                        probabilities(0)
                        for g in range(8):
                            if g < 7:
                                probabilities(g + 1)
                            transposed(g)
                        for j in range(4):
                            act.wait_ge(f_otp, upto(4, j + 1))
                            A(OT[:, j, :], bank[4 + j % 2][:, :], ACT.Copy).then_inc(f_ot, 1)
                        ln_act(act, i * 3 + (LN_F[ph] + 1 + l))
                        for m, (at, size) in enumerate(HID_TILES):
                            act.wait_ge(f_ag, upto(3, m + 1))
                            if m >= 2:
                                act.wait_ge(f_ga, upto(3, m - 1))
                            A(GE[0:size, m % 2, :], bank[2 * (m % 2) + 1][0:size, :], ACT.Gelu,
                              bias=b1f[0:size, l, 3 + m:4 + m]).then_inc(f_ge, 1)

            layers_act(0)
            with act.Fori(0, PAIRS) as i:
                ln_act(act, i + LN_M)
                for k in range(2):
                    act.wait_ge(m_pr, i * 7 + (k + 1))
                    A(SPB[:, 0, k, :], bank[k][:, :], ACT.Abs, bias=dt_bias_b[:, k:k + 1]).then_inc(m_a1, 1)
                act.wait_ge(m_a1, i * 2 + 2)
                A(SPB[:, 1, :, :], SPB[:, 0, :, :], ACT.Exp, scale=-1.0).then_inc(m_a2, 1)
                act.wait_ge(m_d, i * 8 + 1)
                A(SPB[:, 3, :, :], SPB[:, 2, :, :], ACT.Ln).then_inc(m_a3, 1)
                for k in range(2):
                    act.wait_ge(m_pr, i * 7 + (k + 3))
                    A(XI[:, k, :], bank[2 + k][:, :], ACT.Copy).then_inc(m_ev, 1)
                act.wait_ge(m_pr, i * 7 + 7)
                A(BS[0:32, :], bank[6][0:32, :], ACT.Copy).then_inc(m_bs, 1)
                act.wait_ge(m_bd, i * 2 + 1)
                A(BS[32:64, :], BR[:, 0, :], ACT.Copy).then_inc(m_bs, 1)
                act.wait_ge(m_bd, i * 2 + 2)
                A(BS[64:96, :], BR[:, 1, :], ACT.Copy).then_inc(m_bs, 1)
                act.wait_ge(m_d, i * 8 + 8)
                A(LD[:, :, :], SPB[:, 3, :, :], ACT.Ln).then_inc(m_ld, 1)
                for k in range(2):
                    act.wait_ge(m_pr, i * 7 + (k + 5))
                    A(ZS[:, k, :], bank[4 + k][:, :], ACT.Silu).then_inc(m_ev, 1)
                act.wait_ge(m_ld, i + 1)
                for s in range(NS):
                    for hf in range(2):
                        k = 2 * s + hf
                        c = NS * hf + s
                        if k >= 2:
                            act.wait_ge(m_wu, i * 32 + (k - 1))
                        A(RG[:, hf, :], LD[:, hf, :], ACT.Sigmoid, bias=sg_bias[:, c:c + 1], scale=-1.0).then_inc(m_rg, 1)
                        if k >= 2:
                            act.wait_ge(m_hs, i * 64 + (2 * k - 2))
                        A(AB[:, hf, :], LD[:, hf, :], ACT.Tanh, bias=th_bias[:, c:c + 1], scale=-0.5).then_inc(m_ab, 1)
                for k in range(2):
                    act.wait_ge(m_cen, i * 2 + (k + 1))
                    A(YS[:, k, :], Y[:, k, :], ACT.Square).then_inc(m_sq, 1)
                act.wait_ge(m_var, i + 1)
                A(LLOG[:, :], STAT[:, :], ACT.Ln, bias=eps_col[:, :]).then_inc(m_log, 1)
                act.wait_ge(m_log, i + 1)
                A(LRS[:, :], LLOG[:, :], ACT.Exp, scale=-0.5).then_inc(m_rs, 1)
            layers_act(1)

        @block.vector
        def _(dve):
            v = nc.vector
            TT, TS, STT = v.tensor_tensor, v.tensor_scalar, v.scalar_tensor_tensor
            v.memset(eps_col[:, :], EPS)
            v.memset(floor_col[:, :], SS_FLOOR)
            v.memset(unscale_col[:, :], LN_UNSCALE)
            v.memset(XN[:, :, 0:CONV - 1], 0.0)
            v.memset(HA[:, :], 0.0)
            v.memset(HF[:, :], 0.0)
            v.memset(P[:, :, :, :], 0.0)
            v.memset(VT[:, :, :, DH:DH + 1], 1.0)
            dve.wait_ge(in_first, 32)
            dve.wait_ge(pre_aexp, 1)
            for c in range(CONV):
                last = TT(convW[:, c, :], F("a_win", 256, 544), F("a_convw", 288 * c, 288 * c + 288), ALU.mult)
            for k in range(2):
                last = TS(F("a_wout", 128 * k, 128 * k + 128), F("a_wout", 128 * k, 128 * k + 128),
                          F("a_normw", k, k + 1), None, ALU.mult)
            last.then_inc(pre_a, 1)
            dve.wait_ge(in_x, 16)
            dve.wait_ge(pre_a, 1)

            with dve.Fori(0, PAIRS) as i:
                xs = X[:, bass.ds(i * NT, NT)]
                v.tensor_copy(XC[:, :], xs).then_inc(ln_in, 1)
                dve.wait_ge(ln_in, i + (LN_A + 1))
                ln_dve(dve, i + LN_A, XC[:, :], XN[:, :, CONV - 1:])
                dve.wait_ge(a_dt, i + 1)
                TT(sp[:, 0, :], bank[5][:, 0:16], F("a_dtb"), ALU.add).then_inc(a_spd, 1)
                dve.wait_ge(a_sp, i * 3 + 2)
                TS(sp[:, 3, :], sp[:, 2, :], 1.0, None, ALU.add).then_inc(a_spd, 1)
                dve.wait_ge(a_spd, i * 2 + 2)
                TS(sp[:, 5, :], sp[:, 3, :], -1.0, None, ALU.add).then_inc(a_adt1, 1)
                dve.wait_ge(a_adt1, i * 7 + 1)
                TS(sp[:, 6, :], sp[:, 5, :], 0.0, None, ALU.is_equal).then_inc(a_adt1, 1)
                dve.wait_ge(a_adt1, i * 7 + 2)
                dve.wait_ge(a_sp, i * 3 + 3)
                TT(sp[:, 5, :], sp[:, 5, :], sp[:, 6, :], ALU.add)
                TT(sp[:, 4, :], sp[:, 4, :], sp[:, 6, :], ALU.add).then_inc(a_adt1, 1)
                dve.wait_ge(a_adt1, i * 7 + 3)
                v.reciprocal(sp[:, 7, :], sp[:, 5, :])
                TT(sp[:, 4, :], sp[:, 4, :], sp[:, 2, :], ALU.mult).then_inc(a_adt1, 1)
                dve.wait_ge(a_adt1, i * 7 + 4)
                TT(sp[:, 4, :], sp[:, 4, :], sp[:, 7, :], ALU.mult).then_inc(a_adt1, 1)
                dve.wait_ge(a_adt1, i * 7 + 5)
                STT(sp[:, 8, :], sp[:, 0, :], 0.0, sp[:, 4, :], ALU.max, ALU.add).then_inc(a_adt1, 1)
                dve.wait_ge(a_adt1, i * 7 + 6)
                STT(adt[:, :], sp[:, 8, :], -1.0, a_exp[:, :], ALU.mult, ALU.mult).then_inc(a_adt, 1)
                v.tensor_copy(sp[:, 9, :], sp[:, 8, :]).then_inc(a_adt1, 1)
                dve.wait_ge(a_adt1, i * 7 + 7)
                for tt in range(4):
                    dve.wait_ge(a_xtp, i * 4 + (2 * (tt // 2) + 2))
                    TT(XT[:, tt, :].rearrange("p (h d) -> p h d", h=SSD_HEADS),
                       bank[2 + tt // 2][:, 256 * (tt % 2):256 * (tt % 2) + 256].rearrange("p (h d) -> p h d", h=SSD_HEADS),
                       sp[:, 9, 4 * tt:4 * tt + 4].unsqueeze(2).to_broadcast([128, SSD_HEADS, DH]), ALU.mult).then_inc(a_xt, 1)
                dve.wait_ge(a_cb, i * 2 + 2)
                for q in range(8):
                    dve.wait_ge(a_lm, i * 8 + (q + 1))
                    if q >= 2:
                        dve.wait_ge(a_y, i * 8 + (q - 1))
                    TT(MM[:, q % 2, :], LM[:, q % 2, :], bank[4 + 2 * (q // 4)][:, 0:384], ALU.mult).then_inc(a_mm, 1)
                dve.wait_ge(a_y, i * 8 + 8)
                for k in range(2):
                    STT(Y[:, k, :], XA[:, k, :], F("a_d", k, k + 1), bank[2 + k][:, :], ALU.mult, ALU.add).then_inc(a_yd, 1)
                for k in range(2):
                    dve.wait_ge(a_yd, i * 2 + (k + 1))
                    TT(Y[:, k, :], Y[:, k, :], ZS[:, k, :], ALU.mult).then_inc(a_yg, 1)
                dve.wait_ge(a_rs, i + 1)
                for k in range(2):
                    dve.wait_ge(a_yg, i * 2 + (k + 1))
                    TT(Y[:, k, :], Y[:, k, :], LRS[:, :], ALU.mult).then_inc(a_yn, 1)
                dve.wait_ge(a_out, i + 1)
                TT(xs, xs, STAT[:, :], ALU.add).then_inc(a_x, 1)

            dve.wait_ge(in_rest, 16)
            dve.wait_ge(pre_ps, 1)
            for l in range(DEPTH):
                for g in range(2):
                    for m, (at, size) in enumerate(HID_TILES):
                        c = 3 * g + m
                        TT(b1f[0:size, l, c:c + 1], bank[0][0:size, 8 * l + c:8 * l + c + 1],
                           W(f"b1{l}", c, c + 1, p=size), ALU.add)
                TS(W(f"w1{l}"), W(f"w1{l}"), W(f"lg{l}"), None, ALU.mult)
                for t, (table, scale) in enumerate((("cq", "qs"), ("sq", "qsr"), ("ck", "ks"), ("sk", "ksr"))):
                    TS(tab[:, l, t, :], W(table), W(f"{scale}{l}"), None, ALU.mult)
            v.tensor_copy(out_bias_b[:, :], bank[0][:, 16:17])
            for k in range(2):
                TS(W("b_wout", 128 * k, 128 * k + 128), W("b_wout", 128 * k, 128 * k + 128), W("b_gamma", k, k + 1),
                   None, ALU.mult)
            TT(dt_bias_b[:, :], W("b_bdt"), W("b_dtb"), ALU.add)
            TS(sg_bias[:, :], W("b_alog"), -1.0, float(np.log(2.0)), ALU.mult, ALU.add)
            TS(th_bias[:, :], W("b_alog"), -0.5, float(0.5 * np.log(2.0)), ALU.mult, ALU.add).then_inc(pre_b, 1)
            dve.wait_ge(pre_b, 1)
            dve.wait_ge(a_x, PAIRS)

            def shifted(src, dst, done):
                v.tensor_copy(dst[0:64, :], src[0:64, :])
                v.tensor_copy(dst[64:128, :].rearrange("p (b t) -> p b t", b=2)[:, :, 1:],
                              src[64:128, :].rearrange("p (b t) -> p b t", b=2)[:, :, 0:SEQ - 1]).then_inc(done, 1)

            def layers_dve(ph):
                with dve.Fori(0, PAIRS) as i:
                    xs = X[:, bass.ds(i * NT, NT)]
                    v.tensor_copy(XC[:, :], xs).then_inc(ln_in, 1)
                    dve.wait_ge(ln_in, i * 3 + (LN_F[ph] + 1))
                    ln_dve(dve, i * 3 + LN_F[ph], XC[:, :], pair(R))
                    for l in range(DEPTH):
                        def upto(per, n):
                            return i * (2 * per) + (per * (2 * PAIRS * ph + l) + n)

                        if l == 0:
                            dve.wait_ge(ln_out, i * 3 + (LN_F[ph] + 1))
                        else:
                            dve.wait_ge(f_r2, upto(1, 0))
                        shifted(R, HA, f_h)

                        def products(j):
                            dve.wait_ge(f_qk, upto(8, j + 1))
                            if j >= 2:
                                dve.wait_ge(f_rope, upto(8, j - 1))
                            t = 0 if j < 4 else 2
                            for part, dst in ((1, T2), (0, T1)):
                                if part == 0:
                                    dve.wait_ge(f_sq, upto(8, j + 1))
                                table = tab[:, l, t + part, :].unsqueeze(1).to_broadcast([128, 2, SEQ])
                                last = TT(dst[:, j % 2, :].rearrange("p (b t) -> p b t", b=2),
                                          bank[2 * (j % 2) + part][:, :].rearrange("p (b t) -> p b t", b=2), table, ALU.mult)
                            last.then_inc(f_prod, 1)

                        def k_scale(k):
                            dve.wait_ge(f_kr, upto(4, k + 1))
                            dve.wait_ge(f_rope, upto(8, k + 5))
                            STT(KT[:, k, :], KR[:, k % 2, :], NORM_CLIP, KS[:, k % 2, :], ALU.min, ALU.mult).then_inc(f_k, 1)

                        for j in range(6):
                            products(j)
                        dve.wait_ge(f_qr, upto(1, 1))
                        TS(QS[:, :], QR[:, :], NORM_CLIP, QK_SCALE, ALU.min, ALU.mult).then_inc(f_qs, 1)
                        TS(NQ[:, :], QR[:, :], NORM_CLIP, -QK_SCALE, ALU.min, ALU.mult).then_inc(f_nq, 1)
                        k_scale(0)
                        products(6)
                        k_scale(1)
                        products(7)
                        k_scale(2)
                        k_scale(3)
                        dve.wait_ge(f_nq, upto(1, 1))

                        def maxima(g):
                            b, j = divmod(g, 4)
                            dve.wait_ge(f_sim, upto(8, g + 1))
                            if g >= 2:
                                dve.wait_ge(f_exp, upto(8, g - 1))
                            for hh in range(2):
                                last = v.reduce_max(MX[:, g % 2, 2 * hh:2 * hh + 2],
                                                    bank[2 * (g % 2) + hh][:, 0:384].rearrange("p (k s) -> p k s", k=2), AX.X)
                            last.then_inc(f_mx, 1)
                            dve.wait_ge(f_mx, upto(8, g + 1))
                            nq = NQ[:, :].rearrange("p (h c) -> p h c", h=HEADS)[:, 2 * j:2 * j + 2, 2 * b:2 * b + 2]
                            TT(NB[:, g % 2, :].rearrange("p (h k) -> p h k", h=2),
                               MX[:, g % 2, :].rearrange("p (h k) -> p h k", h=2), nq, ALU.mult).then_inc(f_nb, 1)

                        def transposed(g):
                            dve.wait_ge(f_ptp, upto(8, g + 1))
                            if g >= 2:
                                dve.wait_ge(f_ops, upto(8, g - 1))
                            v.tensor_copy(PT[:, g % 2, 1, :], bank[5][:, 0:384]).then_inc(f_ptd, 1)

                        def normalise(g):
                            b, j = divmod(g, 4)
                            dve.wait_ge(f_ops, upto(8, g + 1))
                            o = bank[6 + g % 2][:, 0:4 * (DH + 1)].rearrange("p (q d) -> p q d", q=4)
                            v.reciprocal(RC[:, g % 2, :].unsqueeze(2), o[:, :, DH:DH + 1]).then_inc(f_rc, 1)
                            dve.wait_ge(f_rc, upto(8, g + 1))
                            for hh in range(2):
                                last = TT(OS[:, 2 * b:2 * b + 2, 2 * j + hh, :], o[:, 2 * hh:2 * hh + 2, 0:DH],
                                          RC[:, g % 2, 2 * hh:2 * hh + 2].unsqueeze(2).to_broadcast([128, 2, DH]), ALU.mult)
                            last.then_inc(f_os, 1)

                        maxima(0)
                        for g in range(8):
                            if g < 7:
                                maxima(g + 1)
                            transposed(g)
                            if g >= 1:
                                normalise(g - 1)
                        normalise(7)
                        dve.wait_ge(f_at, upto(1, 1))
                        TT(R[:, :], R[:, :], STAT[:, :], ALU.add).then_inc(f_r1, 1)
                        dve.wait_ge(f_r1, upto(1, 1))
                        shifted(R, HF, ln_in)
                        dve.wait_ge(ln_in, i * 3 + (LN_F[ph] + 2 + l))
                        ln_dve(dve, i * 3 + (LN_F[ph] + 1 + l), HF[:, :], pair(HN))
                        for m, (at, size) in enumerate(HID_TILES):
                            dve.wait_ge(f_ge, upto(3, m + 1))
                            STT(GA[0:size, m, :], bank[2 * (m % 2)][0:size, :], b1f[0:size, l, m:m + 1],
                                GE[0:size, m % 2, :], ALU.add, ALU.mult).then_inc(f_ga, 1)
                        dve.wait_ge(f_ff, upto(1, 1))
                        STT(R[:, :], STAT[:, :], W(f"b2{l}"), R[:, :], ALU.add, ALU.add).then_inc(f_r2, 1)
                    dve.wait_ge(f_r2, i * 2 + (2 * PAIRS * ph + 2))
                    TT(xs, xs, R[:, :], ALU.add).then_inc(f_x, 1)

            layers_dve(0)
            dve.wait_ge(f_x, PAIRS)
            with dve.Fori(0, PAIRS) as i:
                xs = X[:, bass.ds(i * NT, NT)]
                v.tensor_copy(XC[:, :], xs).then_inc(ln_in, 1)
                dve.wait_ge(ln_in, i + (LN_M + 1))
                ln_dve(dve, i + LN_M, XC[:, :], pair(HN))
                z, z1, lg, d = SPB[:, 1, :, :], SPB[:, 2, :, :], SPB[:, 3, :, :], SPB[:, 0, :, :]
                dve.wait_ge(m_a2, i + 1)
                TS(z1, z, 1.0, None, ALU.add).then_inc(m_d, 1)
                dve.wait_ge(m_d, i * 8 + 1)
                TS(d, z1, -1.0, None, ALU.add).then_inc(m_d, 1)
                dve.wait_ge(m_d, i * 8 + 2)
                dve.wait_ge(m_a3, i + 1)
                TS(z1, d, 0.0, None, ALU.is_equal).then_inc(m_d, 1)
                dve.wait_ge(m_d, i * 8 + 3)
                TT(d, d, z1, ALU.add)
                TT(lg, lg, z1, ALU.add).then_inc(m_d, 1)
                dve.wait_ge(m_d, i * 8 + 4)
                v.reciprocal(d, d)
                TT(lg, lg, z, ALU.mult).then_inc(m_d, 1)
                dve.wait_ge(m_d, i * 8 + 5)
                TT(lg, lg, d, ALU.mult)
                for k in range(2):
                    last = TS(z[:, k, :], bank[k][:, :], dt_bias_b[:, k:k + 1], 0.0, ALU.add, ALU.max)
                last.then_inc(m_d, 1)
                dve.wait_ge(m_d, i * 8 + 6)
                TT(d, lg, z, ALU.add).then_inc(m_d, 1)
                dve.wait_ge(m_d, i * 8 + 7)
                TS(lg, d, 1e-19, None, ALU.max).then_inc(m_d, 1)
                dve.wait_ge(m_ev, i * 4 + 2)
                TT(U[:, :, :], d, XI[:, :, :], ALU.mult).then_inc(m_u, 1)
                dve.wait_ge(m_bs, i * 3 + 1)
                TT(BR[:, 0, :], bank[6][0:32, :], BS[0:32, :], ALU.subtract).then_inc(m_bd, 1)
                dve.wait_ge(m_bs, i * 3 + 2)
                dve.wait_ge(m_bd, i * 2 + 1)
                TT(BR[:, 1, :], BR[:, 0, :], BS[32:64, :], ALU.subtract).then_inc(m_bd, 1)
                for s in range(NS):
                    for hf in range(2):
                        k = 2 * s + hf
                        if hf == 0:
                            dve.wait_ge(m_bc, i * 16 + (s + 1))
                        dve.wait_ge(m_wu, i * 32 + (k + 1))
                        TT(VB[:, hf, :], WU[:, hf, :], bank[2 * (s % 2)][:, :], ALU.mult).then_inc(m_vb, 1)
                        dve.wait_ge(m_vb, i * 32 + (k + 1))
                        dve.wait_ge(m_ab, i * 32 + (k + 1))
                        for b in range(2):
                            cols = slice(SEQ * b, SEQ * b + SEQ)
                            v.tensor_tensor_scan(HS[:, hf, cols], AB[:, hf, cols], VB[:, hf, cols], 0.0,
                                                 ALU.mult, ALU.add).then_inc(m_hs, 1)
                        dve.wait_ge(m_hs, i * 64 + (2 * k + 2))
                        if k >= 2:
                            dve.wait_ge(m_acc, i * 32 + (k - 1))
                        TT(PC[:, hf, :], HS[:, hf, :], bank[2 * (s % 2) + 1][:, :], ALU.mult).then_inc(m_pc, 1)
                for k in range(2):
                    dve.wait_ge(m_acc, i * 32 + (k + 31))
                    dve.wait_ge(m_ev, i * 4 + 4)
                    TT(Y[:, k, :], ZS[:, k, :], bank[4 + k][:, :], ALU.mult).then_inc(m_g, 1)
                dve.wait_ge(m_mean, i + 1)
                for k in range(2):
                    dve.wait_ge(m_g, i * 2 + (k + 1))
                    TT(Y[:, k, :], Y[:, k, :], STAT[:, :], ALU.subtract).then_inc(m_cen, 1)
                dve.wait_ge(m_rs, i + 1)
                for k in range(2):
                    dve.wait_ge(m_cen, i * 2 + (k + 1))
                    TT(Y[:, k, :], Y[:, k, :], LRS[:, :], ALU.mult).then_inc(m_n, 1)
                dve.wait_ge(m_out, i + 1)
                STT(xs, STAT[:, :], out_bias_b[:, :], xs, ALU.add, ALU.add).then_inc(m_x, 1)
            dve.wait_ge(m_x, PAIRS)
            layers_dve(1)


def shape_tables():
    p = np.arange(128)
    one = np.ones((128, 128), np.float32)
    le = (p[:, None] <= p[None, :]).astype(np.float32)
    strict = (p[:, None] > p[None, :]).astype(np.float32)
    half = np.arange(0, DH, 2, dtype=np.float32)
    inv_freq = (1.0 / 10000.0 ** (half / DH)).astype(np.float32)
    t = np.arange(SEQ, dtype=np.float32)
    freqs = (t[:, None] * inv_freq[None, :]).astype(np.float32).astype(np.float64)
    base = (half.astype(np.float64) + 0.4 * DH) / (1.4 * DH)
    scale = base[None, :] ** ((t.astype(np.float64) - SEQ // 2) / (WINDOW // 2))[:, None]
    cos, sin = np.cos(freqs), np.sin(freqs)

    def rows(a, sign):
        return np.concatenate([sign * a.T, a.T, sign * a.T, a.T]).astype(np.float32)

    f = {"ident": np.eye(128, dtype=np.float32), "mean128": one / 128, "mean256": one / 256, "ones": one,
         "le": le, "strict": np.concatenate([strict, strict], 1)}
    head = (p[:, None] // DH == p[None, :] // DH).astype(np.float32)
    r = {"head128": head, "head2": head[:, [0, DH]], "cq": rows(cos * scale, 1), "sq": rows(sin * scale, -1),
         "ck": rows(cos / scale, 1), "sk": rows(sin / scale, -1)}
    q, k = p[:, None], p[None, :]
    k1 = np.arange(192)[None, :] + 64
    ok1 = (k1 <= q + 128) & (k1 >= q + 128 - WINDOW)
    ok0 = (k <= q) & (k >= q - WINDOW)
    band = np.concatenate([ok1, np.zeros((128, 64), bool), ok0], 1)
    causal = np.concatenate([le > 0, np.ones((128, 128), bool), le > 0], 1)
    sel = np.zeros((128, 32, 128), np.float32)
    for s in range(32):
        for part in range(3):
            sel[32 * part + s, s, :] = 1.0
    b = {"ident16": np.eye(128), "band": np.where(band, 0.0, MASKED), "causal": np.where(causal, 0.0, MASKED),
         "sel": sel.reshape(128, 32 * 128)}
    return f, r, b


def pack(sizes, total, parts, dtype):
    out = np.zeros((128, total), dtype)
    for name, (at, n) in sizes.items():
        a = parts[name]
        out[:a.shape[0], at:at + n] = a
    return out


def kernel(**inputs):
    import concourse.bacc as _bacc
    import ml_dtypes
    from concourse.bass_utils import run_bass_kernel_spmd as _run
    g = {k: np.asarray(a) for k, a in inputs.items()}
    x = np.ascontiguousarray(g["L0_attn_a_u"].transpose(2, 0, 1).reshape(D, NTOK))
    f, r, b = shape_tables()
    A = {k[10:]: a for k, a in g.items() if k.startswith("L0_attn_a_")}
    B = {k[10:]: a for k, a in g.items() if k.startswith("L0_attn_b_")}
    L = {k[7:]: a for k, a in g.items() if k.startswith("L0_ffn_")}

    def cols(a, n):
        return a.reshape(n, 128, -1).transpose(1, 0, 2).reshape(128, -1)

    f.update({
        "a_win": A["W_in"].T, "a_convw": np.tile(A["conv_w"][:, 0, :].T.reshape(1, -1), (128, 1)),
        "a_convb": cols(A["conv_b"][:256, None], 2), "a_convb_bc": A["conv_b"][256:].reshape(2, NS).T,
        "a_dtb": np.tile(A["dt_bias"][None, :], (128, 4)), "a_alog": np.tile(A["A_log"][None, :], (128, 4)),
        "a_d": cols(np.repeat(A["D"], DH)[:, None], 2), "a_normw": cols(A["norm_w"][:, None], 2),
        "a_wout": cols(A["W_out"].T, 2)})
    for l in range(DEPTH):
        wqk = L["wqkv"][l][:, :2 * INNER].reshape(D, 2 * HEADS, 2, DH // 2)
        b1 = np.zeros((2, 3 * 128), np.float32)
        b1[:, :HID] = L["b1"][l].reshape(2, HID)
        w2 = np.zeros((3 * 128, D), np.float32)
        w2[:HID] = L["w2"][l]
        qs, ks = L["q_scale"][l], L["k_scale"][l]
        r.update({
            f"wqkv{l}": L["wqkv"][l], f"wrot{l}": wqk[:, :, ::-1, :].reshape(D, 2 * INNER), f"wo{l}": cols(L["wo"][l], 4),
            f"w1{l}": L["w1"][l], f"w2{l}": cols(w2, 3), f"b1{l}": b1.reshape(6, 128).T, f"b2{l}": L["b2"][l][:, None],
            f"lg{l}": L["ln_g"][l][:, None], f"lb{l}": L["ln_b"][l][:, None],
            f"qs{l}": np.tile(qs, 2)[:, None], f"qsr{l}": np.tile(np.roll(qs, DH // 2), 2)[:, None],
            f"ks{l}": np.tile(ks, 2)[:, None], f"ksr{l}": np.tile(np.roll(ks, DH // 2), 2)[:, None]})
    r.update({
        "b_win": B["Win"].T, "b_wbc": np.concatenate([B["WB"], B["WC"]]).T, "b_wdt": B["Wdt"].T,
        "b_alog": cols(B["A_log"], 2), "b_bdt": cols(B["bdt"][:, None], 2), "b_dtb": cols(B["dt_bias"][:, None], 2),
        "b_gamma": cols(B["gamma"][:, None], 2), "b_beta": cols(B["beta"][:, None], 2), "b_wout": cols(B["Wout"].T, 2)})
    arrays = {"x": x, "first": pack(FIRST, N_FIRST, f, np.float32), "rest": pack(REST, N_REST, r, np.float32),
              "tabs16": pack(BF, N_BF, b, ml_dtypes.bfloat16)}
    nc = _bacc.Bacc("TRN2", target_bir_lowering=False, num_devices=1)
    args = [nc.dram_tensor(f"in_{k}", a.shape, mybir.dt.from_np(a.dtype), kind="ExternalInput").ap()
            for k, a in arrays.items()]
    out = nc.dram_tensor("out", (D, NTOK), mybir.dt.float32, kind="ExternalOutput").ap()
    program(nc, *args, out)
    got = _run(nc, [{f"in_{k}": a for k, a in arrays.items()}], core_ids=[0]).results[0]["out"]
    return np.ascontiguousarray(got.reshape(D, BATCH, SEQ).transpose(1, 2, 0))
```

```python
import numpy as np
import concourse.bass as bass
from concourse import mybir
from contextlib import ExitStack

D, SEQ, BATCH = 128, 256, 16
NT = 2 * SEQ
PAIRS = BATCH // 2
NTOK = BATCH * SEQ
HEADS, DH, WINDOW, DEPTH = 8, 64, 64, 2
INNER = HEADS * DH
HID = 341
HID_TILES = [(0, 128), (128, 128), (256, HID - 256)]
DI = 256
NS = 16
SSD_HEADS = 4
CONV = 4
MASKED = -1e30
QK_SCALE = 8.0
SS_SCALE = 2.0 ** 32
SS_FLOOR = 2.0 ** -63
LN_UNSCALE = 16 * float(np.log(2.0))
NORM_CLIP = 1e12
EPS = 1e-5


def layout(sizes):
    at, out = 0, {}
    for name, n in sizes:
        out[name] = (at, n)
        at += n
    return out, at


FIRST, N_FIRST = layout([
    ("ident", 128), ("mean128", 128), ("mean256", 128), ("ones", 128), ("le", 128), ("strict", 256),
    ("a_win", 548), ("a_convw", CONV * 288), ("a_convb", 2), ("a_convb_bc", 2), ("a_dtb", 16),
    ("a_alog", 16), ("a_d", 2), ("a_normw", 2), ("a_wout", 2 * 128)])
LAYER = [("wqkv", 3 * INNER), ("wo", 4 * 128), ("w1", 2 * HID), ("w2", 3 * 128),
         ("b1", 6), ("b2", 1), ("lg", 1), ("lb", 1), ("qks", 4 * DH)]
REST, N_REST = layout(
    [("rotary", 2 * 4 * DH)]
    + [(f"{name}{l}", n) for l in range(DEPTH) for name, n in LAYER]
    + [("b_win", 4 * 128), ("b_wbc", 32), ("b_wdt", 2 * 128), ("b_alog", 2 * NS), ("b_bdt", 2), ("b_dtb", 2),
       ("b_gamma", 2), ("b_beta", 2), ("b_wout", 2 * 128)])
BF, N_BF = layout([("ident16", 128), ("band", 384), ("causal", 384), ("sel", 32 * 128)])


def program(nc, x_in, first_in, rest_in, bf_in, out):
    f32, bf16 = mybir.dt.float32, mybir.dt.bfloat16
    ACT, ALU, AX = mybir.ActivationFunctionType, mybir.AluOpType, mybir.AxisListType
    ctx = ExitStack()
    with ctx:
        def sb(name, shape, dt=f32):
            return ctx.enter_context(nc.sbuf_tensor(name, shape, dt))

        def sem(name):
            return ctx.enter_context(nc.semaphore(name))

        X = sb("X", [128, NTOK])
        first = sb("first", [128, N_FIRST])
        rest = sb("rest", [128, N_REST])
        tabs16 = sb("tabs16", [128, N_BF], bf16)

        def F(name, a=0, b=None, p=128):
            at, n = FIRST[name]
            return first[0:p, at + a:at + (n if b is None else b)]

        def W(name, a=0, b=None, p0=0, p=128):
            at, n = REST[name]
            return rest[p0:p, at + a:at + (n if b is None else b)]

        def T16(name, a=0, b=None, p=128):
            at, n = BF[name]
            return tabs16[0:p, at + a:at + (n if b is None else b)]

        ARENA = 24832
        arena = sb("arena", [128, ARENA])
        used = {}

        def shared(phase, shape):
            at = used.get(phase, 0)
            n = int(np.prod(shape[1:]))
            used[phase] = at + n
            assert used[phase] <= ARENA
            a = arena[0:shape[0], at:at + n]
            if len(shape) == 3:
                a = a.rearrange("p (a b) -> p a b", a=shape[1])
            if len(shape) == 4:
                a = a.rearrange("p (a b c) -> p a b c", a=shape[1], b=shape[2])
            return a

        psum = ctx.enter_context(nc.psum_tensor("psum", [128, 8, 512], f32))
        bank = [psum[:, k, :] for k in range(8)]
        STAT = bank[7]

        XC = sb("XC", [128, NT])
        CEN = sb("CEN", [128, NT])
        LSQ = sb("LSQ", [128, NT])
        LLOG = LRS = LSQ
        CEN2 = sb("CEN2", [128, NT])
        LSQ2 = sb("LSQ2", [128, NT])
        ln_in = sem("ln_in")
        ln_mean = sem("ln_mean")
        ln_cen = sem("ln_cen")
        ln_sq = sem("ln_sq")
        ln_var = sem("ln_var")
        ln_log = sem("ln_log")
        ln_rs = sem("ln_rs")
        ln_out = sem("ln_out")

        def ln_pe(pe, n, src):
            pe.wait_ge(ln_in, n + 1)
            nc.tensor.matmul(STAT, F("mean128"), src, start=True, stop=True).then_inc(ln_mean, 1)
            pe.wait_ge(ln_sq, n + 1)
            nc.tensor.matmul(STAT, F("mean128"), LSQ[:, :], start=True, stop=True).then_inc(ln_var, 1)

        def ln_act(act, n):
            act.wait_ge(ln_cen, n + 1)
            nc.scalar.activation(LSQ[:, :], CEN[:, :], ACT.Square).then_inc(ln_sq, 1)
            act.wait_ge(ln_var, n + 1)
            nc.scalar.activation(LLOG[:, :], STAT, ACT.Ln, bias=eps_col[:, :]).then_inc(ln_log, 1)
            act.wait_ge(ln_log, n + 1)
            nc.scalar.activation(LRS[:, :], LLOG[:, :], ACT.Exp, scale=-0.5).then_inc(ln_rs, 1)

        def ln_dve(dve, n, src, dst):
            dve.wait_ge(ln_mean, n + 1)
            nc.vector.tensor_tensor(CEN[:, :], src, STAT, ALU.subtract).then_inc(ln_cen, 1)
            dve.wait_ge(ln_rs, n + 1)
            dve.wait_ge(ln_cen, n + 1)
            nc.vector.tensor_tensor(dst, pair(CEN), pair(LRS), ALU.mult).then_inc(ln_out, 1)

        def pair(t):
            return t[:, :].rearrange("p (b t) -> p b t", b=2)

        eps_col = sb("eps_col", [128, 1])
        floor_col = sb("floor_col", [128, 1])
        unscale_col = sb("unscale_col", [128, 1])
        convW = sb("convW", [128, CONV, 288])
        a_exp = sb("a_exp", [128, 16])
        sg_bias = sb("sg_bias", [128, 2 * NS])
        th_bias = sb("th_bias", [128, 2 * NS])
        dt_bias_b = sb("dt_bias_b", [128, 2])
        out_bias_b = sb("out_bias_b", [128, 1])
        tab = sb("tab", [128, DEPTH, 2, 4, DH])
        b1f = sb("b1f", [128, DEPTH, 6])
        in_first = sem("in_first")
        in_x = sem("in_x")
        in_rest = sem("in_rest")
        pre_a = sem("pre_a")
        pre_aexp = sem("pre_aexp")
        pre_ps = sem("pre_ps")
        pre_fold = sem("pre_fold")
        pre_b = sem("pre_b")

        XN = sb("XN", [128, 2, SEQ + CONV - 1])
        ZS = shared("ssd", [128, 2, NT])
        XA = shared("ssd", [128, 2, NT])
        BA = shared("ssd", [NS, NT])
        CA = shared("ssd", [NS, NT])
        sp = sb("sp", [128, 10, 16])
        adt = sb("adt", [128, 16])
        AM = sb("AM", [128, 2, 3, 128])
        LM = shared("ssd", [128, 2, 384])
        MM = shared("ssd", [128, 2, 384])
        XT = shared("ssd", [128, 4, DI])
        Y = shared("ssd", [128, 2, NT])
        YS = shared("ssd", [128, 2, NT])
        a_z = sem("a_z")
        a_dt = sem("a_dt")
        a_act = sem("a_act")
        a_sp = sem("a_sp")
        a_spd = sem("a_spd")
        a_adt1 = sem("a_adt1")
        a_adt = sem("a_adt")
        a_xtp = sem("a_xtp")
        a_xt = sem("a_xt")
        a_cb = sem("a_cb")
        a_am = sem("a_am")
        a_seg = sem("a_seg")
        a_lm = sem("a_lm")
        a_mm = sem("a_mm")
        a_y = sem("a_y")
        a_yd = sem("a_yd")
        a_yg = sem("a_yg")
        a_ysq = sem("a_ysq")
        a_ms = sem("a_ms")
        a_log = sem("a_log")
        a_rs = sem("a_rs")
        a_yn = sem("a_yn")
        a_out = sem("a_out")
        a_x = sem("a_x")

        SLOTS = DEPTH * PAIRS
        R = shared("layers", [128, NTOK])
        QKT = [shared("layers", [128, 8, NT]) for _ in range(2)]
        VT = [shared("layers", [128, 4, INNER]) for _ in range(2)]
        OT = shared("layers", [128, 4, NT])
        HA = sb("HA", [128, NT])
        HF = sb("HF", [128, NT])
        HN = sb("HN", [128, NT])
        SQN = shared("layers", [128, 2, INNER])
        CQ = shared("layers", [128, 2, INNER])
        SS = sb("SS", [128, 2, HEADS])
        SL = sb("SL", [128, 2, HEADS])
        SR = sb("SR", [128, 2, HEADS])
        SC = sb("SC", [128, 2, HEADS])
        NB = sb("NB", [128, 2, 2])
        LS = sb("LS", [128, 2, 2])
        RC = sb("RC", [128, 2, 2])
        P = sb("P", [128, 2, 384])
        PT = shared("layers", [128, 2, 384])
        GE = shared("layers", [128, 3, NT])
        S_BANK, P_BANK, O_BANK = (0, 1), 2, 4
        QK_BANK = (5, 6)
        V_BANK = bank[3]
        HID_BANK = ((V_BANK, STAT, V_BANK), (STAT, V_BANK, STAT))
        f_sim = sem("f_sim")
        f_nb = sem("f_nb")
        f_exp = sem("f_exp")
        f_rc = sem("f_rc")
        f_p = sem("f_p")
        f_ptp = sem("f_ptp")
        f_pta = sem("f_pta")
        f_ptd = sem("f_ptd")
        f_pv = sem("f_pv")
        f_oe = sem("f_oe")
        f_at = sem("f_at")
        f_r1 = sem("f_r1")
        f_g = sem("f_g")
        f_ge = sem("f_ge")
        f_a = sem("f_a")
        f_ga = sem("f_ga")
        f_ff = sem("f_ff")
        f_r2 = sem("f_r2")
        f_x = sem("f_x")
        f_h = sem("f_h")
        f_pj = sem("f_pj")
        f_sq = sem("f_sq")
        f_ss = sem("f_ss")
        f_sl = sem("f_sl")
        f_sr = sem("f_sr")
        f_sc = sem("f_sc")
        f_prod = sem("f_prod")
        f_rope = sem("f_rope")
        f_qk = sem("f_qk")
        f_xp = sem("f_xp")
        f_qkt = sem("f_qkt")
        f_vp = sem("f_vp")
        f_v = sem("f_v")

        class Norm:
            def __init__(self, tag):
                (self.ready, self.mean, self.cen, self.sq, self.var, self.log, self.rs, self.out) = (
                    sem(f"{tag}_{x}") for x in ("ready", "mean", "cen", "sq", "var", "log", "rs", "out"))

        inner, outer = Norm("fi"), Norm("fo")

        used["mamba"] = used["ssd"]
        XI = shared("mamba", [128, 2, NT])
        SPB = shared("mamba", [128, 4, 2, NT])
        U = shared("mamba", [128, 2, NT])
        LD = shared("mamba", [128, 2, NT])
        BR = shared("mamba", [32, 2, NT])
        BS = sb("BS", [96, NT], bf16)
        RG = shared("mamba", [128, 2, NT])
        AB = shared("mamba", [128, 2, NT])
        WU = SPB[:, 0, :, :]
        VB = SPB[:, 1, :, :]
        HS = SPB[:, 2, :, :]
        PC = SPB[:, 3, :, :]
        spread_bank = [(bank[0], bank[1]), (bank[2], bank[3]), (bank[6], bank[7])]
        m_pr = sem("m_pr")
        m_ev = sem("m_ev")
        m_a1 = sem("m_a1")
        m_a2 = sem("m_a2")
        m_a3 = sem("m_a3")
        m_d = sem("m_d")
        m_u = sem("m_u")
        m_ld = sem("m_ld")
        m_bs = sem("m_bs")
        m_bd = sem("m_bd")
        m_bc = sem("m_bc")
        m_rg = sem("m_rg")
        m_ab = sem("m_ab")
        m_wu = sem("m_wu")
        m_vb = sem("m_vb")
        m_hs = sem("m_hs")
        m_pc = sem("m_pc")
        m_acc = sem("m_acc")
        m_g = sem("m_g")
        m_mean = sem("m_mean")
        m_cen = sem("m_cen")
        m_sq = sem("m_sq")
        m_var = sem("m_var")
        m_log = sem("m_log")
        m_rs = sem("m_rs")
        m_n = sem("m_n")
        m_out = sem("m_out")
        m_x = sem("m_x")
        out_done = sem("out_done")

        block = ctx.enter_context(nc.Block())

        LN_A, LN_M = 0, PAIRS

        class Slot:
            def __init__(self, eng, ph, i, j, last=None):
                self.eng, self.ph, self.i, self.j = eng, ph, i, j
                last = j if last is None else last
                self.looped = not isinstance(i, int)
                self.post = 1 <= j and last <= SLOTS
                self.pre = -1 <= j and last <= SLOTS - 2
                self.outer = last + 2 < PAIRS
                self.last = last

            def has(self, m):
                return 0 <= self.j + m and self.last + m < SLOTS

            def side(self, m=0):
                return (self.j + m) % 2

            def layer(self, m):
                assert (self.j + m) // PAIRS == (self.last + m) // PAIRS
                return (self.j + m) // PAIRS

            def tokens(self, m):
                at = (self.j + m) % PAIRS * NT
                return bass.ds(self.i * (2 * NT) + at, NT) if self.looped else slice(at, at + NT)

            def wait(self, semaphore, per, n, slot=0):
                self.count(semaphore, 2 * per, per * (SLOTS * self.ph + self.j + slot) + n)

            def wait_pair(self, semaphore, slot):
                self.count(semaphore, 2, PAIRS * self.ph + (self.j + slot) % PAIRS + 1)

            def count(self, semaphore, per_turn, const):
                if not self.looped:
                    if const > 0:
                        self.eng.wait_ge(semaphore, const)
                else:
                    assert const > 0
                    self.eng.wait_ge(semaphore, self.i * per_turn + const)

            def unit(self, u):
                m, u = u // 16, u % 16
                return (m, u) if self.has(m) else None

        def passes(eng, ph, slot):
            for n in (-2, -1, 0, 1):
                slot(Slot(eng, ph, 0, n))
            with eng.Fori(0, 2) as i:
                for j in (2, 3):
                    slot(Slot(eng, ph, i, j, j + 2))
            for n in range(6, PAIRS + 1):
                slot(Slot(eng, ph, 0, n))
            with eng.Fori(0, PAIRS // 2 - 1) as i:
                for j in (PAIRS + 1, PAIRS + 2):
                    slot(Slot(eng, ph, i, j, j + PAIRS - 4))
            for n in (SLOTS - 1, SLOTS):
                slot(Slot(eng, ph, 0, n))

        START = (1, 4, 8, 11, 15, 18, 22, 25)

        def item(h, behind):
            return START.index(h - behind) if h - behind in START else None

        @block.sync
        def _(sp_):
            sp_.dma_start(first[:, :], first_in).then_inc(in_first, 16)
            sp_.dma_start(X[:, :], x_in).then_inc(in_x, 16)
            sp_.dma_start(tabs16[:, :], bf_in).then_inc(in_first, 16)
            sp_.dma_start(rest[:, :], rest_in).then_inc(in_rest, 16)
            with sp_.Fori(0, PAIRS) as i:
                sp_.wait_ge(f_x, i + (PAIRS + 1))
                sp_.dma_start(out[:, bass.ds(i * NT, NT)], X[:, bass.ds(i * NT, NT)]).then_inc(out_done, 16)
            sp_.wait_ge(out_done, 16 * PAIRS)

        @block.gpsimd
        def _(pool):
            pool.wait_ge(in_first, 32)
            with pool.Fori(0, PAIRS) as i:
                pool.wait_ge(a_adt, i + 1)
                for q in range(8):
                    b, h = divmod(q, SSD_HEADS)
                    if q >= 2:
                        pool.wait_ge(a_seg, i * 8 + (q - 1))
                    a = adt[:, :].rearrange("p (b t h) -> p b t h", b=2, t=2)[:, b, :, h:h + 1]
                    nc.gpsimd.tensor_tensor(AM[:, q % 2, 0:2, :], F("strict").rearrange("p (t s) -> p t s", t=2),
                                            a.to_broadcast([128, 2, 128]), ALU.mult)
                    nc.gpsimd.tensor_tensor(AM[:, q % 2, 2, :], F("ones"), a[:, 1, :].to_broadcast([128, 128]),
                                            ALU.mult).then_inc(a_am, 1)

            def pool_slot(k):
                if k.outer:
                    if k.j > -2:
                        k.wait_pair(outer.cen, 1)
                    nc.gpsimd.tensor_copy(XC[:, :], X[:, k.tokens(2)]).then_inc(outer.ready, 1)
                if not k.pre:
                    return
                for n in range(8):
                    part = n % 2
                    k.wait(f_prod, 8, n + 1, slot=1)
                    nc.gpsimd.tensor_tensor(CQ[:, part, :], CQ[:, part, :], SQN[:, part, :], ALU.add).then_inc(f_rope, 1)
                    k.wait(f_rope, 8, n + 1, slot=1)
                    k.wait(f_sc, 8, n + 1, slot=1)
                    heads = CQ[:, part, :].rearrange("p (h d) -> p h d", d=DH)
                    nc.gpsimd.tensor_tensor(heads, heads, SC[:, part, :].unsqueeze(2).to_broadcast([128, HEADS, DH]),
                                            ALU.mult).then_inc(f_qk, 1)

            def layers_pool(ph):
                passes(pool, ph, pool_slot)

            pool.wait_ge(a_x, PAIRS)
            layers_pool(0)
            with pool.Fori(0, PAIRS) as i:
                for s in range(NS):
                    for hf in range(2):
                        k = 2 * s + hf
                        pool.wait_ge(m_rg, i * 32 + (k + 1))
                        if k == 0:
                            pool.wait_ge(m_u, i + 1)
                        if k >= 2:
                            pool.wait_ge(m_vb, i * 32 + (k - 1))
                        nc.gpsimd.tensor_tensor(WU[:, hf, :], RG[:, hf, :], U[:, hf, :], ALU.mult).then_inc(m_wu, 1)
            pool.wait_ge(m_x, PAIRS)
            layers_pool(1)

        @block.tensor
        def _(pe):
            mm = nc.tensor.matmul
            pe.wait_ge(in_first, 32)
            pe.wait_ge(pre_a, 1)
            with pe.Fori(0, PAIRS) as i:
                ln_pe(pe, i + LN_A, XC[:, :])
                pe.wait_ge(ln_out, i + (LN_A + 1))
                for tt in range(4):
                    b, t = divmod(tt, 2)
                    last = mm(bank[5][:, 4 * tt:4 * tt + 4], XN[:, b, 3 + 128 * t:131 + 128 * t],
                              F("a_win", 544, 548), start=True, stop=True)
                last.then_inc(a_dt, 1)
                for k in range(2):
                    for c in range(CONV):
                        last = mm(bank[2 + k][:, :], convW[:, c, 128 * k:128 * k + 128], XN[:, :, c:c + SEQ],
                                  start=c == 0, stop=c == CONV - 1)
                    last.then_inc(a_z, 1)
                for k, dst in ((0, bank[4]), (1, bank[6])):
                    for c in range(CONV):
                        last = mm(dst[0:NS, :], convW[:, c, 256 + NS * k:256 + NS * (k + 1)], XN[:, :, c:c + SEQ],
                                  start=c == 0, stop=c == CONV - 1)
                    last.then_inc(a_z, 1)
                for k in range(2):
                    mm(bank[k][:, :], F("a_win", 128 * k, 128 * k + 128), XN[:, :, 3:3 + SEQ],
                       start=True, stop=True).then_inc(a_z, 1)
                pe.wait_ge(a_act, i * 6 + 4)
                for tt in range(4):
                    for k in range(2):
                        last = nc.tensor.transpose(bank[2 + tt // 2][:, 256 * (tt % 2) + 128 * k:256 * (tt % 2) + 128 * k + 128],
                                                   XA[:, k, 128 * tt:128 * tt + 128], F("ident"))
                    last.then_inc(a_xtp, 1)
                pe.wait_ge(a_act, i * 6 + 6)
                pe.wait_ge(a_xt, i * 4 + 4)

                def segsum(q):
                    seg = bank[q % 2]
                    pe.wait_ge(a_am, i * 8 + (q + 1))
                    if q >= 2:
                        pe.wait_ge(a_lm, i * 8 + (q - 1))
                    mm(seg[:, 0:384], T16("ident16"), T16("causal"), start=True, stop=False)
                    mm(seg[:, 0:128], AM[:, q % 2, 0, :], F("le"), start=False, stop=False)
                    mm(seg[:, 128:256], AM[:, q % 2, 0, :], F("ones"), start=False, stop=False)
                    mm(seg[:, 128:256], AM[:, q % 2, 2, :], F("le"), start=False, stop=False)
                    mm(seg[:, 256:384], AM[:, q % 2, 1, :], F("le"), start=False, stop=True).then_inc(a_seg, 1)

                def head_out(q):
                    b, h = divmod(q, SSD_HEADS)
                    pe.wait_ge(a_mm, i * 8 + (q + 1))
                    y = bank[2 + h // 2][64 * (h % 2):64 * (h % 2) + 64, :]
                    xh = XT[:, :, DH * h:DH * h + DH]
                    mm(y[:, SEQ * b:SEQ * b + SEQ], xh[:, 2 * b, :], MM[:, q % 2, 0:256], start=True, stop=False)
                    mm(y[:, SEQ * b + 128:SEQ * b + SEQ], xh[:, 2 * b + 1, :], MM[:, q % 2, 256:384],
                       start=False, stop=True).then_inc(a_y, 1)

                for b, cb in ((0, bank[4]), (1, bank[6])):
                    mm(cb[:, 0:256], BA[:, SEQ * b:SEQ * b + 128], CA[:, SEQ * b:SEQ * b + SEQ], start=True, stop=True)
                    mm(cb[:, 256:384], BA[:, SEQ * b + 128:SEQ * b + SEQ], CA[:, SEQ * b + 128:SEQ * b + SEQ],
                       start=True, stop=True).then_inc(a_cb, 1)
                segsum(0)
                for q in range(8):
                    if q < 7:
                        segsum(q + 1)
                    head_out(q)
                pe.wait_ge(a_ysq, i * 2 + 2)
                for k in range(2):
                    last = mm(STAT, F("mean256"), YS[:, k, :], start=k == 0, stop=k == 1)
                last.then_inc(a_ms, 1)
                pe.wait_ge(a_yn, i * 2 + 2)
                for k in range(2):
                    last = mm(STAT, F("a_wout", 128 * k, 128 * k + 128), Y[:, k, :], start=k == 0, stop=k == 1)
                last.then_inc(a_out, 1)

            pe.wait_ge(in_rest, 16)
            pe.wait_ge(a_x, PAIRS)
            for l in range(DEPTH):
                for g in range(2):
                    for m, (at, size) in enumerate(HID_TILES):
                        mm(bank[0][0:size, 8 * l + 3 * g + m:8 * l + 3 * g + m + 1],
                           W(f"w1{l}", HID * g + at, HID * g + at + size), W(f"lb{l}"), start=True, stop=True)
            for k in range(2):
                last = mm(bank[0][:, 16:17], W("b_wout", 128 * k, 128 * k + 128), W("b_beta", k, k + 1),
                          start=k == 0, stop=k == 1)
            last.then_inc(pre_ps, 1)
            pe.wait_ge(pre_b, 1)

            def scores(k, m, u):
                h, b = u % HEADS, u // HEADS
                k.wait(f_exp, 16, u - 1, slot=m)
                k.wait(f_qkt, 8, 4 * b + 4, slot=m)
                s, rows = bank[S_BANK[u % 2]], slice(64 * (h % 2), 64 * (h % 2) + 64)
                q, key = QKT[k.side(m)][rows, h // 2, :], QKT[k.side(m)][rows, 4 + h // 2, :]
                mm(s[:, 0:384], T16("ident16"), T16("band"), start=True, stop=False)
                mm(s[:, 0:192], q[:, SEQ * b + 128:SEQ * b + 256], key[:, SEQ * b + 64:SEQ * b + 256],
                   start=False, stop=False)
                mm(s[:, 256:384], q[:, SEQ * b:SEQ * b + 128], key[:, SEQ * b:SEQ * b + 128],
                   start=False, stop=True).then_inc(f_sim, 1)

            def flip(k, m, u):
                k.wait(f_p, 16, u + 1, slot=m)
                k.wait(f_pta if u % 2 else f_ptd, 8, (u + 1) // 2, slot=m)
                for c in range(3):
                    last = nc.tensor.transpose(bank[P_BANK][:, 128 * c:128 * c + 128],
                                               P[:, u % 2, 128 * c:128 * c + 128], F("ident"))
                last.then_inc(f_ptp, 1)

            def weigh(k, m, u):
                h, b = u % HEADS, u // HEADS
                k.wait(f_ptd if u % 2 else f_pta, 8, u // 2 + 1, slot=m)
                if u % 2 == 0:
                    k.wait(f_oe, 8, u // 2, slot=m)
                if h == 0:
                    k.wait(f_v, 4, 2 * b + 2, slot=m)
                o = bank[O_BANK][64 * (h % 2):64 * (h % 2) + 64, :]
                value = VT[k.side(m)][:, :, DH * h:DH * h + DH]
                mm(o[:, 128:256], value[:, 2 * b + 1, :], PT[:, u % 2, 128:256], start=True, stop=False)
                mm(o[:, 128:256], value[:, 2 * b, :], PT[:, u % 2, 0:128], start=False, stop=True)
                mm(o[:, 0:128], value[:, 2 * b, :], PT[:, u % 2, 256:384], start=True, stop=True).then_inc(f_pv, 1)

            def out_projection(k, half):
                l = k.layer(-1)
                if half == 0:
                    k.wait(f_oe, 8, 8, slot=-1)
                    if k.outer:
                        k.wait_pair(outer.log, 2)
                for j in (2 * half, 2 * half + 1):
                    last = mm(STAT, W(f"wo{l}", 128 * j, 128 * j + 128), OT[:, j, :], start=j == 0, stop=j == 3)
                if half:
                    last.then_inc(f_at, 1)

            def inner_mean(k):
                k.wait(inner.ready, 1, 1, slot=-1)
                mm(STAT, F("mean128"), HF[:, :], start=True, stop=True).then_inc(inner.mean, 1)

            def inner_var(k):
                k.wait(inner.sq, 1, 1, slot=-1)
                mm(STAT, F("mean128"), LSQ[:, :], start=True, stop=True).then_inc(inner.var, 1)

            def hidden(k, half, m, done):
                at, size = HID_TILES[m]
                mm(HID_BANK[half][m][0:size, :], W(f"w1{k.layer(-1)}", half * HID + at, half * HID + at + size), HN[:, :],
                   start=True, stop=True).then_inc(done, 1)

            def gate_half(k, m):
                if m == 0:
                    k.wait(inner.out, 1, 1, slot=-1)
                elif m == 1:
                    if k.has(0):
                        k.wait(f_v, 4, 4)
                    if k.pre:
                        k.wait(f_v, 4, 3, slot=1)
                else:
                    k.wait(f_ge, 3, 1, slot=-1)
                hidden(k, 1, m, f_g)

            def other_half(k, m):
                if m < 2:
                    k.wait(f_ge, 3, m + 2, slot=-1)
                else:
                    k.wait(f_ga, 3, 1, slot=-1)
                hidden(k, 0, m, f_a)

            def down_projection(k, m):
                size = HID_TILES[m][1]
                k.wait(f_ga, 3, max(m, 1) + 1, slot=-1)
                last = mm(STAT, W(f"w2{k.layer(-1)}", 128 * m, 128 * m + 128, p=size), GE[0:size, m, :],
                          start=m == 0, stop=m == 2)
                if m == 2:
                    last.then_inc(f_ff, 1)

            def outer_mean(k):
                k.wait_pair(outer.ready, 2)
                if k.j > -2:
                    k.wait_pair(outer.log, 1)
                k.wait(f_r2, 1, 1, slot=-2)
                mm(STAT, F("mean128"), XC[:, :], start=True, stop=True).then_inc(outer.mean, 1)

            def outer_var(k):
                k.wait_pair(outer.sq, 2)
                mm(STAT, F("mean128"), LSQ2[:, :], start=True, stop=True).then_inc(outer.var, 1)

            def project(k, n):
                tt, part = divmod(n, 2)
                if n == 0:
                    k.wait(f_h, 1, 1, slot=1)
                k.wait(f_qkt, 8, n - 1, slot=1)
                mm(bank[QK_BANK[part]], HA[:, 128 * tt:128 * tt + 128],
                   W(f"wqkv{k.layer(1)}", INNER * part, INNER * part + INNER), start=True, stop=True).then_inc(f_pj, 1)

            def project_v(k, tt):
                k.wait(f_h, 1, 1, slot=1)
                k.wait(f_v, 4, tt, slot=1)
                if tt == 3 and k.post:
                    k.wait(f_ga, 3, 3, slot=-1)
                mm(V_BANK, HA[:, 128 * tt:128 * tt + 128], W(f"wqkv{k.layer(1)}", 2 * INNER, 3 * INNER),
                   start=True, stop=True).then_inc(f_vp, 1)

            def to_features(k, n):
                part = n % 2
                k.wait(f_qk, 8, n + 1, slot=1)
                for c in range(4):
                    last = nc.tensor.transpose(bank[QK_BANK[part]][:, 128 * c:128 * c + 128],
                                               CQ[:, part, 128 * c:128 * c + 128], F("ident"))
                last.then_inc(f_xp, 1)

            def pe_dense(k, h):
                if k.outer and h == 1:
                    outer_mean(k)
                if k.outer and h == 4:
                    outer_var(k)
                if k.post:
                    if h in (5, 6):
                        out_projection(k, h - 5)
                    elif h == 9:
                        inner_mean(k)
                    elif h == 13:
                        inner_var(k)
                    elif h == 17:
                        gate_half(k, 0)
                        gate_half(k, 1)
                    elif h == 18:
                        gate_half(k, 2)
                    elif h in (19, 20, 22):
                        other_half(k, (19, 20, 22).index(h))
                    elif h in (23, 24, 25):
                        down_projection(k, h - 23)
                if k.pre:
                    if item(h, 5) is not None:
                        to_features(k, item(h, 5))
                    if item(h, 0) is not None:
                        project(k, item(h, 0))
                    if h in (2, 8, 14, 27):
                        project_v(k, (2, 8, 14, 27).index(h))

            def pe_slot(k):
                for u in range(16):
                    if k.unit(u + 2):
                        scores(k, *k.unit(u + 2))
                    pe_dense(k, 2 * u)
                    if k.unit(u):
                        flip(k, *k.unit(u))
                    pe_dense(k, 2 * u + 1)
                    if k.unit(u - 1):
                        weigh(k, *k.unit(u - 1))

            def layers_pe(ph):
                passes(pe, ph, pe_slot)

            layers_pe(0)

            with pe.Fori(0, PAIRS) as i:
                ln_pe(pe, i + LN_M, XC[:, :])
                pe.wait_ge(ln_out, i + (LN_M + 1))
                for k in range(2):
                    mm(bank[k][:, :], W("b_wdt", 128 * k, 128 * k + 128), HN[:, :], start=True, stop=True).then_inc(m_pr, 1)
                for k in range(4):
                    mm(bank[2 + k][:, :], W("b_win", 128 * k, 128 * k + 128), HN[:, :], start=True, stop=True).then_inc(m_pr, 1)
                mm(bank[6][0:32, :], W("b_wbc"), HN[:, :], start=True, stop=True).then_inc(m_pr, 1)
                pe.wait_ge(m_bs, i * 3 + 3)
                pe.wait_ge(m_bd, i * 2 + 2)
                pe.wait_ge(m_ev, i * 4 + 4)
                pe.wait_ge(m_u, i + 1)

                def spread(s):
                    if s >= 3:
                        pe.wait_ge(m_pc, i * 32 + (2 * s - 4))
                    mm(spread_bank[s % 3][0][:, :], T16("sel", 128 * s, 128 * s + 128, p=96), BS[:, :], start=True, stop=True)
                    mm(spread_bank[s % 3][1][:, :], T16("sel", 128 * (NS + s), 128 * (NS + s) + 128, p=96), BS[:, :],
                       start=True, stop=True).then_inc(m_bc, 1)

                spread(0)
                spread(1)
                for s in range(NS):
                    if s + 2 < NS:
                        spread(s + 2)
                    for hf in range(2):
                        pe.wait_ge(m_pc, i * 32 + (2 * s + hf + 1))
                        mm(bank[4 + hf][:, :], F("ident"), PC[:, hf, :], start=s == 0, stop=s == NS - 1).then_inc(m_acc, 1)
                pe.wait_ge(m_g, i * 2 + 2)
                for k in range(2):
                    last = mm(STAT, F("mean256"), Y[:, k, :], start=k == 0, stop=k == 1)
                last.then_inc(m_mean, 1)
                pe.wait_ge(m_sq, i * 2 + 2)
                for k in range(2):
                    last = mm(STAT, F("mean256"), YS[:, k, :], start=k == 0, stop=k == 1)
                last.then_inc(m_var, 1)
                pe.wait_ge(m_n, i * 2 + 2)
                for k in range(2):
                    last = mm(STAT, W("b_wout", 128 * k, 128 * k + 128), Y[:, k, :], start=k == 0, stop=k == 1)
                last.then_inc(m_out, 1)
            layers_pe(1)

        @block.scalar
        def _(act):
            A = nc.scalar.activation
            EXP_LN = "natural_log_exp_and_others"
            nc.scalar.preload_act_table_set(EXP_LN)
            act.wait_ge(in_first, 32)
            A(a_exp[:, :], F("a_alog"), ACT.Exp).then_inc(pre_aexp, 1)
            act.wait_ge(pre_a, 1)
            with act.Fori(0, PAIRS) as i:
                nc.scalar.preload_act_table_set(EXP_LN)
                ln_act(act, i + LN_A)
                act.wait_ge(a_spd, i * 2 + 1)
                A(sp[:, 1, :], sp[:, 0, :], ACT.Abs).then_inc(a_sp, 1)
                act.wait_ge(a_sp, i * 3 + 1)
                A(sp[:, 2, :], sp[:, 1, :], ACT.Exp, scale=-1.0).then_inc(a_sp, 1)
                act.wait_ge(a_spd, i * 2 + 2)
                A(sp[:, 4, :], sp[:, 3, :], ACT.Ln).then_inc(a_sp, 1)
                for k in range(2):
                    act.wait_ge(a_z, i * 6 + (k + 1))
                    A(XA[:, k, :], bank[2 + k][:, :], ACT.Silu, bias=F("a_convb", k, k + 1)).then_inc(a_act, 1)
                for k, (dst, src) in enumerate(((BA, bank[4]), (CA, bank[6]))):
                    act.wait_ge(a_z, i * 6 + (k + 3))
                    A(dst[:, :], src[0:NS, :], ACT.Silu, bias=F("a_convb_bc", k, k + 1, p=NS)).then_inc(a_act, 1)
                for k in range(2):
                    act.wait_ge(a_z, i * 6 + (k + 5))
                    A(ZS[:, k, :], bank[k][:, :], ACT.Silu).then_inc(a_act, 1)
                nc.scalar.preload_act_table_set(EXP_LN)
                for q in range(8):
                    act.wait_ge(a_seg, i * 8 + (q + 1))
                    if q >= 2:
                        act.wait_ge(a_mm, i * 8 + (q - 1))
                    A(LM[:, q % 2, :], bank[q % 2][:, 0:384], ACT.Exp).then_inc(a_lm, 1)
                for k in range(2):
                    act.wait_ge(a_yg, i * 2 + (k + 1))
                    A(YS[:, k, :], Y[:, k, :], ACT.Square).then_inc(a_ysq, 1)
                act.wait_ge(a_ms, i + 1)
                A(LLOG[:, :], STAT, ACT.Ln, bias=eps_col[:, :]).then_inc(a_log, 1)
                act.wait_ge(a_log, i + 1)
                A(LRS[:, :], LLOG[:, :], ACT.Exp, scale=-0.5).then_inc(a_rs, 1)

            act.wait_ge(pre_b, 1)

            def exponentials(k, m, u):
                k.wait(f_nb, 16, u + 1, slot=m)
                k.wait(f_ptp, 16, u - 1, slot=m)
                s = bank[S_BANK[u % 2]]
                A(P[:, u % 2, 64:256], s[:, 0:192], ACT.Exp, bias=NB[:, u % 2, 0:1], accum_out=LS[:, u % 2, 0:1])
                A(P[:, u % 2, 256:384], s[:, 256:384], ACT.Exp, bias=NB[:, u % 2, 1:2],
                  accum_out=LS[:, u % 2, 1:2]).then_inc(f_exp, 1)

            def flipped_act(k, m, u):
                k.wait(f_ptp, 16, u + 1, slot=m)
                k.wait(f_pv, 16, u - 1, slot=m)
                A(PT[:, 0, :], bank[P_BANK][:, 0:384], ACT.Copy).then_inc(f_pta, 1)

            def output(k, m, u):
                b, j = divmod(u // 2, 4)
                k.wait(f_pv, 16, u + 2, slot=m)
                if u == 0:
                    k.wait(f_at, 1, 1, slot=m - 1)
                A(OT[:, j, SEQ * b:SEQ * b + SEQ], bank[O_BANK][:, 0:256], ACT.Copy).then_inc(f_oe, 1)

            def square_centred(norm, wait, centred, square):
                wait(norm.cen)
                A(square, centred, ACT.Square).then_inc(norm.sq, 1)

            def inverse_root(norm, wait, variance, root):
                wait(norm.var)
                A(root, variance, ACT.Ln, bias=eps_col[:, :]).then_inc(norm.log, 1)
                wait(norm.log)
                A(root, root, ACT.Exp, scale=-0.5).then_inc(norm.rs, 1)

            def gelus(k):
                for m, (at, size) in enumerate(HID_TILES):
                    k.wait(f_g, 3, m + 1, slot=-1)
                    A(GE[0:size, m, :], HID_BANK[1][m][0:size, :], ACT.Gelu,
                      bias=b1f[0:size, k.layer(-1), 3 + m:4 + m]).then_inc(f_ge, 1)
                nc.scalar.preload_act_table_set(EXP_LN)

            def squares(k, n):
                k.wait(f_pj, 8, n + 1, slot=1)
                k.wait(f_rope, 8, n - 1, slot=1)
                A(SQN[:, n % 2, :], bank[QK_BANK[n % 2]], ACT.Square).then_inc(f_sq, 1)

            def values(k, tt):
                k.wait(f_vp, 4, tt + 1, slot=1)
                A(VT[k.side(1)][:, tt, :], V_BANK, ACT.Copy).then_inc(f_v, 1)

            def norms(k, n):
                k.wait(f_ss, 8, n + 1, slot=1)
                A(SL[:, n % 2, :], SS[:, n % 2, :], ACT.Ln, bias=floor_col[:, :], scale=SS_SCALE).then_inc(f_sl, 1)
                k.wait(f_sl, 8, n + 1, slot=1)
                A(SR[:, n % 2, :], SL[:, n % 2, :], ACT.Exp, bias=unscale_col[:, :], scale=-0.5).then_inc(f_sr, 1)

            def features(k, n):
                tt, part = divmod(n, 2)
                k.wait(f_xp, 8, n + 1, slot=1)
                A(QKT[k.side(1)][:, 4 * part:4 * part + 4, 128 * tt:128 * tt + 128],
                  bank[QK_BANK[part]].rearrange("p (c t) -> p c t", t=128), ACT.Copy).then_inc(f_qkt, 1)

            def act_dense(k, h):
                def inner_at(semaphore):
                    k.wait(semaphore, 1, 1, slot=-1)

                def outer_at(semaphore):
                    k.wait_pair(semaphore, 2)

                if k.outer and h == 3:
                    square_centred(outer, outer_at, CEN2[:, :], LSQ2[:, :])
                if k.outer and h == 5:
                    inverse_root(outer, outer_at, STAT, LSQ2[:, :])
                if k.post and h == 12:
                    square_centred(inner, inner_at, CEN[:, :], LSQ[:, :])
                if k.post and h == 14:
                    inverse_root(inner, inner_at, STAT, LSQ[:, :])
                if k.post and h == 18:
                    gelus(k)
                if k.pre:
                    if item(h, 1) is not None:
                        squares(k, item(h, 1))
                    if item(h, 3) is not None:
                        norms(k, item(h, 3))
                    if item(h, 6) is not None:
                        features(k, item(h, 6))
                    if h in (3, 9, 15, 28):
                        values(k, (3, 9, 15, 28).index(h))

            def act_slot(k):
                for u in range(16):
                    if k.unit(u + 1):
                        exponentials(k, *k.unit(u + 1))
                    if u % 2 and k.unit(u - 3):
                        output(k, *k.unit(u - 3))
                    act_dense(k, 2 * u)
                    if u % 2 == 0 and k.unit(u):
                        flipped_act(k, *k.unit(u))
                    act_dense(k, 2 * u + 1)

            def layers_act(ph):
                nc.scalar.preload_act_table_set(EXP_LN)
                passes(act, ph, act_slot)

            layers_act(0)
            with act.Fori(0, PAIRS) as i:
                nc.scalar.preload_act_table_set(EXP_LN)
                ln_act(act, i + LN_M)
                for k in range(2):
                    act.wait_ge(m_pr, i * 7 + (k + 1))
                    A(SPB[:, 0, k, :], bank[k][:, :], ACT.Abs, bias=dt_bias_b[:, k:k + 1]).then_inc(m_a1, 1)
                act.wait_ge(m_a1, i * 2 + 2)
                A(SPB[:, 1, :, :], SPB[:, 0, :, :], ACT.Exp, scale=-1.0).then_inc(m_a2, 1)
                act.wait_ge(m_d, i * 8 + 1)
                A(SPB[:, 3, :, :], SPB[:, 2, :, :], ACT.Ln).then_inc(m_a3, 1)
                for k in range(2):
                    act.wait_ge(m_pr, i * 7 + (k + 3))
                    A(XI[:, k, :], bank[2 + k][:, :], ACT.Copy).then_inc(m_ev, 1)
                act.wait_ge(m_pr, i * 7 + 7)
                A(BS[0:32, :], bank[6][0:32, :], ACT.Copy).then_inc(m_bs, 1)
                act.wait_ge(m_bd, i * 2 + 1)
                A(BS[32:64, :], BR[:, 0, :], ACT.Copy).then_inc(m_bs, 1)
                act.wait_ge(m_bd, i * 2 + 2)
                A(BS[64:96, :], BR[:, 1, :], ACT.Copy).then_inc(m_bs, 1)
                act.wait_ge(m_d, i * 8 + 8)
                A(LD[:, :, :], SPB[:, 3, :, :], ACT.Ln).then_inc(m_ld, 1)
                for k in range(2):
                    act.wait_ge(m_pr, i * 7 + (k + 5))
                    A(ZS[:, k, :], bank[4 + k][:, :], ACT.Silu).then_inc(m_ev, 1)
                act.wait_ge(m_ld, i + 1)
                for s in range(NS):
                    for hf in range(2):
                        k = 2 * s + hf
                        c = NS * hf + s
                        if k >= 2:
                            act.wait_ge(m_wu, i * 32 + (k - 1))
                        A(RG[:, hf, :], LD[:, hf, :], ACT.Sigmoid, bias=sg_bias[:, c:c + 1], scale=-1.0).then_inc(m_rg, 1)
                        if k >= 2:
                            act.wait_ge(m_hs, i * 64 + (2 * k - 2))
                        A(AB[:, hf, :], LD[:, hf, :], ACT.Tanh, bias=th_bias[:, c:c + 1], scale=-0.5).then_inc(m_ab, 1)
                nc.scalar.preload_act_table_set(EXP_LN)
                for k in range(2):
                    act.wait_ge(m_cen, i * 2 + (k + 1))
                    A(YS[:, k, :], Y[:, k, :], ACT.Square).then_inc(m_sq, 1)
                act.wait_ge(m_var, i + 1)
                A(LLOG[:, :], STAT, ACT.Ln, bias=eps_col[:, :]).then_inc(m_log, 1)
                act.wait_ge(m_log, i + 1)
                A(LRS[:, :], LLOG[:, :], ACT.Exp, scale=-0.5).then_inc(m_rs, 1)
            layers_act(1)

        @block.vector
        def _(dve):
            v = nc.vector
            TT, TS, STT = v.tensor_tensor, v.tensor_scalar, v.scalar_tensor_tensor
            v.memset(eps_col[:, :], EPS)
            v.memset(floor_col[:, :], SS_FLOOR)
            v.memset(unscale_col[:, :], LN_UNSCALE)
            v.memset(XN[:, :, 0:CONV - 1], 0.0)
            v.memset(HA[:, :], 0.0)
            v.memset(HF[:, :], 0.0)
            v.memset(P[:, :, :], 0.0)
            dve.wait_ge(in_first, 32)
            dve.wait_ge(pre_aexp, 1)
            for c in range(CONV):
                last = TT(convW[:, c, :], F("a_win", 256, 544), F("a_convw", 288 * c, 288 * c + 288), ALU.mult)
            for k in range(2):
                last = TS(F("a_wout", 128 * k, 128 * k + 128), F("a_wout", 128 * k, 128 * k + 128),
                          F("a_normw", k, k + 1), None, ALU.mult)
            last.then_inc(pre_a, 1)
            dve.wait_ge(in_x, 16)
            dve.wait_ge(pre_a, 1)

            with dve.Fori(0, PAIRS) as i:
                xs = X[:, bass.ds(i * NT, NT)]
                v.tensor_copy(XC[:, :], xs).then_inc(ln_in, 1)
                dve.wait_ge(ln_in, i + (LN_A + 1))
                ln_dve(dve, i + LN_A, XC[:, :], XN[:, :, CONV - 1:])
                dve.wait_ge(a_dt, i + 1)
                TT(sp[:, 0, :], bank[5][:, 0:16], F("a_dtb"), ALU.add).then_inc(a_spd, 1)
                dve.wait_ge(a_sp, i * 3 + 2)
                TS(sp[:, 3, :], sp[:, 2, :], 1.0, None, ALU.add).then_inc(a_spd, 1)
                dve.wait_ge(a_spd, i * 2 + 2)
                TS(sp[:, 5, :], sp[:, 3, :], -1.0, None, ALU.add).then_inc(a_adt1, 1)
                dve.wait_ge(a_adt1, i * 7 + 1)
                TS(sp[:, 6, :], sp[:, 5, :], 0.0, None, ALU.is_equal).then_inc(a_adt1, 1)
                dve.wait_ge(a_adt1, i * 7 + 2)
                dve.wait_ge(a_sp, i * 3 + 3)
                TT(sp[:, 5, :], sp[:, 5, :], sp[:, 6, :], ALU.add)
                TT(sp[:, 4, :], sp[:, 4, :], sp[:, 6, :], ALU.add).then_inc(a_adt1, 1)
                dve.wait_ge(a_adt1, i * 7 + 3)
                v.reciprocal(sp[:, 7, :], sp[:, 5, :])
                TT(sp[:, 4, :], sp[:, 4, :], sp[:, 2, :], ALU.mult).then_inc(a_adt1, 1)
                dve.wait_ge(a_adt1, i * 7 + 4)
                TT(sp[:, 4, :], sp[:, 4, :], sp[:, 7, :], ALU.mult).then_inc(a_adt1, 1)
                dve.wait_ge(a_adt1, i * 7 + 5)
                STT(sp[:, 8, :], sp[:, 0, :], 0.0, sp[:, 4, :], ALU.max, ALU.add).then_inc(a_adt1, 1)
                dve.wait_ge(a_adt1, i * 7 + 6)
                STT(adt[:, :], sp[:, 8, :], -1.0, a_exp[:, :], ALU.mult, ALU.mult).then_inc(a_adt, 1)
                v.tensor_copy(sp[:, 9, :], sp[:, 8, :]).then_inc(a_adt1, 1)
                dve.wait_ge(a_adt1, i * 7 + 7)
                for tt in range(4):
                    dve.wait_ge(a_xtp, i * 4 + (2 * (tt // 2) + 2))
                    TT(XT[:, tt, :].rearrange("p (h d) -> p h d", h=SSD_HEADS),
                       bank[2 + tt // 2][:, 256 * (tt % 2):256 * (tt % 2) + 256].rearrange("p (h d) -> p h d", h=SSD_HEADS),
                       sp[:, 9, 4 * tt:4 * tt + 4].unsqueeze(2).to_broadcast([128, SSD_HEADS, DH]), ALU.mult).then_inc(a_xt, 1)
                dve.wait_ge(a_cb, i * 2 + 2)
                for q in range(8):
                    dve.wait_ge(a_lm, i * 8 + (q + 1))
                    if q >= 2:
                        dve.wait_ge(a_y, i * 8 + (q - 1))
                    TT(MM[:, q % 2, :], LM[:, q % 2, :], bank[4 + 2 * (q // 4)][:, 0:384], ALU.mult).then_inc(a_mm, 1)
                dve.wait_ge(a_y, i * 8 + 8)
                for k in range(2):
                    STT(Y[:, k, :], XA[:, k, :], F("a_d", k, k + 1), bank[2 + k][:, :], ALU.mult, ALU.add).then_inc(a_yd, 1)
                for k in range(2):
                    dve.wait_ge(a_yd, i * 2 + (k + 1))
                    TT(Y[:, k, :], Y[:, k, :], ZS[:, k, :], ALU.mult).then_inc(a_yg, 1)
                dve.wait_ge(a_rs, i + 1)
                for k in range(2):
                    dve.wait_ge(a_yg, i * 2 + (k + 1))
                    TT(Y[:, k, :], Y[:, k, :], LRS[:, :], ALU.mult).then_inc(a_yn, 1)
                dve.wait_ge(a_out, i + 1)
                TT(xs, xs, STAT, ALU.add).then_inc(a_x, 1)

            dve.wait_ge(in_rest, 16)
            dve.wait_ge(pre_ps, 1)
            for l in range(DEPTH):
                for g in range(2):
                    for m, (at, size) in enumerate(HID_TILES):
                        c = 3 * g + m
                        TT(b1f[0:size, l, c:c + 1], bank[0][0:size, 8 * l + c:8 * l + c + 1],
                           W(f"b1{l}", c, c + 1, p=size), ALU.add)
                TS(W(f"w1{l}"), W(f"w1{l}"), W(f"lg{l}"), None, ALU.mult)
                for t in range(2):
                    TT(tab[:, l, t, :, :].rearrange("p a d -> p (a d)"), W("rotary", 4 * DH * t, 4 * DH * t + 4 * DH),
                       W(f"qks{l}"), ALU.mult)
            v.tensor_copy(out_bias_b[:, :], bank[0][:, 16:17])
            for k in range(2):
                TS(W("b_wout", 128 * k, 128 * k + 128), W("b_wout", 128 * k, 128 * k + 128), W("b_gamma", k, k + 1),
                   None, ALU.mult)
            TT(dt_bias_b[:, :], W("b_bdt"), W("b_dtb"), ALU.add)
            TS(sg_bias[:, :], W("b_alog"), -1.0, float(np.log(2.0)), ALU.mult, ALU.add)
            TS(th_bias[:, :], W("b_alog"), -0.5, float(0.5 * np.log(2.0)), ALU.mult, ALU.add).then_inc(pre_b, 1)
            dve.wait_ge(pre_b, 1)
            dve.wait_ge(a_x, PAIRS)

            def shifted(src, dst, done):
                TS(dst[0:64, :], src[0:64, :], 1.0, None, ALU.mult)
                TS(dst[64:128, :].rearrange("p (b t) -> p b t", b=2)[:, :, 1:],
                   src[64:128, :].rearrange("p (b t) -> p b t", b=2)[:, :, 0:SEQ - 1], 1.0, None, ALU.mult).then_inc(done, 1)

            def maxima(k, m, u):
                k.wait(f_sim, 16, u + 1, slot=m)
                k.wait(f_exp, 16, u - 1, slot=m)
                v.reduce_max(NB[:, u % 2, :], bank[S_BANK[u % 2]][:, 0:384].rearrange("p (k s) -> p k s", k=2), AX.X,
                             negate=True).then_inc(f_nb, 1)

            def probabilities(k, m, u):
                k.wait(f_exp, 16, u + 1, slot=m)
                v.reciprocal(RC[:, u % 2, :], LS[:, u % 2, :]).then_inc(f_rc, 1)
                k.wait(f_rc, 16, u + 1, slot=m)
                TS(P[:, u % 2, 64:256], P[:, u % 2, 64:256], RC[:, u % 2, 0:1], None, ALU.mult)
                TS(P[:, u % 2, 256:384], P[:, u % 2, 256:384], RC[:, u % 2, 1:2], None, ALU.mult).then_inc(f_p, 1)

            def flipped_dve(k, m, u):
                k.wait(f_ptp, 16, u + 1, slot=m)
                k.wait(f_pv, 16, u - 1, slot=m)
                v.tensor_copy(PT[:, 1, :], bank[P_BANK][:, 0:384]).then_inc(f_ptd, 1)

            def after_attention(k):
                r = R[:, k.tokens(-1)]
                k.wait(f_at, 1, 1, slot=-1)
                TT(r, r, STAT, ALU.add).then_inc(f_r1, 1)
                k.wait(f_r1, 1, 1, slot=-1)
                shifted(r, HF, inner.ready)

            def centre(norm, wait, src, mean, dst):
                wait(norm.mean)
                TT(dst, src, mean, ALU.subtract).then_inc(norm.cen, 1)

            def normalise(norm, wait, centred, root, dst):
                wait(norm.rs)
                wait(norm.cen)
                TT(dst, centred, root, ALU.mult).then_inc(norm.out, 1)

            def gated(k, m):
                size = HID_TILES[m][1]
                k.wait(f_a, 3, m + 1, slot=-1)
                STT(GE[0:size, m, :], HID_BANK[0][m][0:size, :], b1f[0:size, k.layer(-1), m:m + 1],
                    GE[0:size, m, :], ALU.add, ALU.mult).then_inc(f_ga, 1)

            def after_feed_forward(k):
                r = R[:, k.tokens(-1)]
                k.wait(f_ff, 1, 1, slot=-1)
                STT(r, STAT, W(f"b2{k.layer(-1)}"), r, ALU.add, ALU.add).then_inc(f_r2, 1)
                if k.layer(-1) == DEPTH - 1:
                    k.wait(f_r2, 1, 1, slot=-1)
                    xs = X[:, k.tokens(-1)]
                    TT(xs, xs, r, ALU.add).then_inc(f_x, 1)

            def begin_slot(k):
                if k.layer(1):
                    k.wait(f_r2, 1, 1, slot=1 - PAIRS)
                else:
                    k.wait_pair(outer.out, 1)
                k.wait(f_pj, 8, 8)
                k.wait(f_vp, 4, 4)
                shifted(R[:, k.tokens(1)], HA, f_h)

            def products(k, n):
                tt, part = divmod(n, 2)
                k.wait(f_sq, 8, n + 1, slot=1)
                k.wait(f_ss, 8, n + 1, slot=1)
                k.wait(f_xp, 8, n - 1, slot=1)
                x = bank[QK_BANK[part]].rearrange("p (h r d) -> p h r d", h=HEADS, r=2)
                t = tab[:, k.layer(1), tt % 2, :, :]
                TT(CQ[:, part, :].rearrange("p (h d) -> p h d", h=HEADS), bank[QK_BANK[part]].rearrange("p (h d) -> p h d", h=HEADS),
                   t[:, part, :].unsqueeze(1).to_broadcast([128, HEADS, DH]), ALU.mult)
                y = SQN[:, part, :].rearrange("p (h r d) -> p h r d", h=HEADS, r=2)
                for r in range(2):
                    sin = t[:, 2 + part, 32 * r:32 * r + 32].unsqueeze(1).to_broadcast([128, HEADS, 32])
                    last = TT(y[:, :, r, :], x[:, :, 1 - r, :], sin, ALU.mult)
                last.then_inc(f_prod, 1)

            def sums(k, n):
                k.wait(f_sq, 8, n + 1, slot=1)
                k.wait(f_sl, 8, n - 1, slot=1)
                v.reduce_sum(SS[:, n % 2, :], SQN[:, n % 2, :].rearrange("p (h d) -> p h d", d=DH), AX.X).then_inc(f_ss, 1)

            def clipped(k, n):
                k.wait(f_sr, 8, n + 1, slot=1)
                k.wait(f_qk, 8, n - 1, slot=1)
                TS(SC[:, n % 2, :], SR[:, n % 2, :], NORM_CLIP, None, ALU.min).then_inc(f_sc, 1)

            def dve_dense(k, h):
                def inner_at(semaphore):
                    k.wait(semaphore, 1, 1, slot=-1)

                def outer_at(semaphore):
                    k.wait_pair(semaphore, 2)

                if k.pre and h == 0:
                    begin_slot(k)
                if k.outer and h == 2:
                    centre(outer, outer_at, XC[:, :], STAT, CEN2[:, :])
                if k.outer and h == 7:
                    normalise(outer, outer_at, CEN2[:, :], LSQ2[:, :], R[:, k.tokens(2)])
                if k.post:
                    if h == 7:
                        after_attention(k)
                    elif h == 11:
                        centre(inner, inner_at, HF[:, :], STAT, CEN[:, :])
                    elif h == 16:
                        normalise(inner, inner_at, CEN[:, :], LSQ[:, :], HN[:, :])
                    elif h in (21, 22, 23):
                        gated(k, h - 21)
                    elif h == 27:
                        after_feed_forward(k)
                if k.pre:
                    if item(h, 2) is not None:
                        sums(k, item(h, 2))
                        products(k, item(h, 2))
                    if item(h, 4) is not None:
                        clipped(k, item(h, 4))

            def dve_slot(k):
                for u in range(16):
                    if k.unit(u + 2):
                        maxima(k, *k.unit(u + 2))
                    dve_dense(k, 2 * u)
                    if k.unit(u + 1):
                        probabilities(k, *k.unit(u + 1))
                    dve_dense(k, 2 * u + 1)
                    if u % 2 and k.unit(u):
                        flipped_dve(k, *k.unit(u))

            def layers_dve(ph):
                passes(dve, ph, dve_slot)

            layers_dve(0)
            dve.wait_ge(f_x, PAIRS)
            with dve.Fori(0, PAIRS) as i:
                xs = X[:, bass.ds(i * NT, NT)]
                v.tensor_copy(XC[:, :], xs).then_inc(ln_in, 1)
                dve.wait_ge(ln_in, i + (LN_M + 1))
                ln_dve(dve, i + LN_M, XC[:, :], pair(HN))
                z, z1, lg, d = SPB[:, 1, :, :], SPB[:, 2, :, :], SPB[:, 3, :, :], SPB[:, 0, :, :]
                dve.wait_ge(m_a2, i + 1)
                TS(z1, z, 1.0, None, ALU.add).then_inc(m_d, 1)
                dve.wait_ge(m_d, i * 8 + 1)
                TS(d, z1, -1.0, None, ALU.add).then_inc(m_d, 1)
                dve.wait_ge(m_d, i * 8 + 2)
                dve.wait_ge(m_a3, i + 1)
                TS(z1, d, 0.0, None, ALU.is_equal).then_inc(m_d, 1)
                dve.wait_ge(m_d, i * 8 + 3)
                TT(d, d, z1, ALU.add)
                TT(lg, lg, z1, ALU.add).then_inc(m_d, 1)
                dve.wait_ge(m_d, i * 8 + 4)
                v.reciprocal(d, d)
                TT(lg, lg, z, ALU.mult).then_inc(m_d, 1)
                dve.wait_ge(m_d, i * 8 + 5)
                TT(lg, lg, d, ALU.mult)
                for k in range(2):
                    last = TS(z[:, k, :], bank[k][:, :], dt_bias_b[:, k:k + 1], 0.0, ALU.add, ALU.max)
                last.then_inc(m_d, 1)
                dve.wait_ge(m_d, i * 8 + 6)
                TT(d, lg, z, ALU.add).then_inc(m_d, 1)
                dve.wait_ge(m_d, i * 8 + 7)
                TS(lg, d, 1e-19, None, ALU.max).then_inc(m_d, 1)
                dve.wait_ge(m_ev, i * 4 + 2)
                TT(U[:, :, :], d, XI[:, :, :], ALU.mult).then_inc(m_u, 1)
                dve.wait_ge(m_bs, i * 3 + 1)
                TT(BR[:, 0, :], bank[6][0:32, :], BS[0:32, :], ALU.subtract).then_inc(m_bd, 1)
                dve.wait_ge(m_bs, i * 3 + 2)
                dve.wait_ge(m_bd, i * 2 + 1)
                TT(BR[:, 1, :], BR[:, 0, :], BS[32:64, :], ALU.subtract).then_inc(m_bd, 1)

                def times_b(k):
                    if k % 2 == 0:
                        dve.wait_ge(m_bc, i * 16 + (k // 2 + 1))
                    dve.wait_ge(m_wu, i * 32 + (k + 1))
                    if k >= 2:
                        dve.wait_ge(m_hs, i * 64 + (2 * k - 2))
                    TT(VB[:, k % 2, :], WU[:, k % 2, :], spread_bank[k // 2 % 3][0][:, :], ALU.mult).then_inc(m_vb, 1)

                def states(k):
                    dve.wait_ge(m_vb, i * 32 + (k + 1))
                    dve.wait_ge(m_ab, i * 32 + (k + 1))
                    if k >= 2:
                        dve.wait_ge(m_pc, i * 32 + (k - 1))
                    for b in range(2):
                        cols = slice(SEQ * b, SEQ * b + SEQ)
                        v.tensor_tensor_scan(HS[:, k % 2, cols], AB[:, k % 2, cols], VB[:, k % 2, cols], 0.0,
                                             ALU.mult, ALU.add).then_inc(m_hs, 1)

                def times_c(k):
                    dve.wait_ge(m_hs, i * 64 + (2 * k + 2))
                    if k >= 2:
                        dve.wait_ge(m_acc, i * 32 + (k - 1))
                    TT(PC[:, k % 2, :], HS[:, k % 2, :], spread_bank[k // 2 % 3][1][:, :], ALU.mult).then_inc(m_pc, 1)

                times_b(0)
                times_b(1)
                states(0)
                for k in range(2 * NS):
                    if k >= 1:
                        times_c(k - 1)
                    if k + 2 < 2 * NS:
                        times_b(k + 2)
                    if k + 1 < 2 * NS:
                        states(k + 1)
                times_c(2 * NS - 1)
                for k in range(2):
                    dve.wait_ge(m_acc, i * 32 + (k + 31))
                    dve.wait_ge(m_ev, i * 4 + 4)
                    TT(Y[:, k, :], ZS[:, k, :], bank[4 + k][:, :], ALU.mult).then_inc(m_g, 1)
                dve.wait_ge(m_mean, i + 1)
                for k in range(2):
                    dve.wait_ge(m_g, i * 2 + (k + 1))
                    TT(Y[:, k, :], Y[:, k, :], STAT, ALU.subtract).then_inc(m_cen, 1)
                dve.wait_ge(m_rs, i + 1)
                for k in range(2):
                    dve.wait_ge(m_cen, i * 2 + (k + 1))
                    TT(Y[:, k, :], Y[:, k, :], LRS[:, :], ALU.mult).then_inc(m_n, 1)
                dve.wait_ge(m_out, i + 1)
                STT(xs, STAT, out_bias_b[:, :], xs, ALU.add, ALU.add).then_inc(m_x, 1)
            dve.wait_ge(m_x, PAIRS)
            layers_dve(1)


def shape_tables():
    p = np.arange(128)
    one = np.ones((128, 128), np.float32)
    le = (p[:, None] <= p[None, :]).astype(np.float32)
    strict = (p[:, None] > p[None, :]).astype(np.float32)
    half = np.arange(0, DH, 2, dtype=np.float32)
    inv_freq = (1.0 / 10000.0 ** (half / DH)).astype(np.float32)
    t = np.arange(SEQ, dtype=np.float32)
    freqs = (t[:, None] * inv_freq[None, :]).astype(np.float32).astype(np.float64)
    base = (half.astype(np.float64) + 0.4 * DH) / (1.4 * DH)
    scale = base[None, :] ** ((t.astype(np.float64) - SEQ // 2) / (WINDOW // 2))[:, None]
    cos, sin = np.cos(freqs), np.sin(freqs)

    def halves(a, sign):
        return np.concatenate([sign * a, a], 1)

    kinds = [halves(QK_SCALE * cos * scale, 1), halves(cos / scale, 1), halves(QK_SCALE * sin * scale, -1),
             halves(sin / scale, -1)]
    rotary = np.stack(kinds, 1).reshape(2, 128, 4 * DH).transpose(1, 0, 2).reshape(128, 2 * 4 * DH)

    f = {"ident": np.eye(128, dtype=np.float32), "mean128": one / 128, "mean256": one / 256, "ones": one,
         "le": le, "strict": np.concatenate([strict, strict], 1)}
    r = {"rotary": rotary.astype(np.float32)}
    q, k = p[:, None], p[None, :]
    k1 = np.arange(192)[None, :] + 64
    ok1 = (k1 <= q + 128) & (k1 >= q + 128 - WINDOW)
    ok0 = (k <= q) & (k >= q - WINDOW)
    band = np.concatenate([ok1, np.zeros((128, 64), bool), ok0], 1)
    causal = np.concatenate([le > 0, np.ones((128, 128), bool), le > 0], 1)
    sel = np.zeros((128, 32, 128), np.float32)
    for s in range(32):
        for part in range(3):
            sel[32 * part + s, s, :] = 1.0
    b = {"ident16": np.eye(128), "band": np.where(band, 0.0, MASKED), "causal": np.where(causal, 0.0, MASKED),
         "sel": sel.reshape(128, 32 * 128)}
    return f, r, b


def pack(sizes, total, parts, dtype):
    out = np.zeros((128, total), dtype)
    for name, (at, n) in sizes.items():
        a = parts[name]
        out[:a.shape[0], at:at + n] = a
    return out


def kernel(**inputs):
    import concourse.bacc as _bacc
    import ml_dtypes
    from concourse.bass_utils import run_bass_kernel_spmd as _run
    g = {k: np.asarray(a) for k, a in inputs.items()}
    x = np.ascontiguousarray(g["L0_attn_a_u"].transpose(2, 0, 1).reshape(D, NTOK))
    f, r, b = shape_tables()
    A = {k[10:]: a for k, a in g.items() if k.startswith("L0_attn_a_")}
    B = {k[10:]: a for k, a in g.items() if k.startswith("L0_attn_b_")}
    L = {k[7:]: a for k, a in g.items() if k.startswith("L0_ffn_")}

    def cols(a, n):
        return a.reshape(n, 128, -1).transpose(1, 0, 2).reshape(128, -1)

    f.update({
        "a_win": A["W_in"].T, "a_convw": np.tile(A["conv_w"][:, 0, :].T.reshape(1, -1), (128, 1)),
        "a_convb": cols(A["conv_b"][:256, None], 2), "a_convb_bc": A["conv_b"][256:].reshape(2, NS).T,
        "a_dtb": np.tile(A["dt_bias"][None, :], (128, 4)), "a_alog": np.tile(A["A_log"][None, :], (128, 4)),
        "a_d": cols(np.repeat(A["D"], DH)[:, None], 2), "a_normw": cols(A["norm_w"][:, None], 2),
        "a_wout": cols(A["W_out"].T, 2)})
    for l in range(DEPTH):
        b1 = np.zeros((2, 3 * 128), np.float32)
        b1[:, :HID] = L["b1"][l].reshape(2, HID)
        w2 = np.zeros((3 * 128, D), np.float32)
        w2[:HID] = L["w2"][l]
        qs, ks = L["q_scale"][l], L["k_scale"][l]
        r.update({
            f"wqkv{l}": L["wqkv"][l], f"wo{l}": cols(L["wo"][l], 4),
            f"w1{l}": L["w1"][l], f"w2{l}": cols(w2, 3), f"b1{l}": b1.reshape(6, 128).T, f"b2{l}": L["b2"][l][:, None],
            f"lg{l}": L["ln_g"][l][:, None], f"lb{l}": L["ln_b"][l][:, None],
            f"qks{l}": np.tile(np.concatenate([qs, ks, np.roll(qs, DH // 2), np.roll(ks, DH // 2)])[None, :], (128, 1))})
    r.update({
        "b_win": B["Win"].T, "b_wbc": np.concatenate([B["WB"], B["WC"]]).T, "b_wdt": B["Wdt"].T,
        "b_alog": cols(B["A_log"], 2), "b_bdt": cols(B["bdt"][:, None], 2), "b_dtb": cols(B["dt_bias"][:, None], 2),
        "b_gamma": cols(B["gamma"][:, None], 2), "b_beta": cols(B["beta"][:, None], 2), "b_wout": cols(B["Wout"].T, 2)})
    arrays = {"x": x, "first": pack(FIRST, N_FIRST, f, np.float32), "rest": pack(REST, N_REST, r, np.float32),
              "tabs16": pack(BF, N_BF, b, ml_dtypes.bfloat16)}
    nc = _bacc.Bacc("TRN2", target_bir_lowering=False, num_devices=1)
    args = [nc.dram_tensor(f"in_{k}", a.shape, mybir.dt.from_np(a.dtype), kind="ExternalInput").ap()
            for k, a in arrays.items()]
    out = nc.dram_tensor("out", (D, NTOK), mybir.dt.float32, kind="ExternalOutput").ap()
    program(nc, *args, out)
    got = _run(nc, [{f"in_{k}": a for k, a in arrays.items()}], core_ids=[0]).results[0]["out"]
    return np.ascontiguousarray(got.reshape(D, BATCH, SEQ).transpose(1, 2, 0))
```

```python
import numpy as np
import concourse.bass as bass
from concourse import mybir
from contextlib import ExitStack

D, SEQ, BATCH = 128, 256, 16
NT = 2 * SEQ
PAIRS = BATCH // 2
NTOK = BATCH * SEQ
HEADS, DH, WINDOW, DEPTH = 8, 64, 64, 2
INNER = HEADS * DH
HID = 341
HID_TILES = [(0, 128), (128, 128), (256, HID - 256)]
DI = 256
NS = 16
SSD_HEADS = 4
CONV = 4
MASKED = -1e30
QK_SCALE = 8.0
SS_SCALE = 2.0 ** 32
SS_FLOOR = 2.0 ** -63
LN_UNSCALE = 16 * float(np.log(2.0))
NORM_CLIP = 1e12
EPS = 1e-5


def layout(sizes):
    at, out = 0, {}
    for name, n in sizes:
        out[name] = (at, n)
        at += n
    return out, at


FIRST, N_FIRST = layout([
    ("ident", 128), ("mean128", 128), ("mean256", 128), ("ones", 128), ("le", 128), ("strict", 256),
    ("a_win", 548), ("a_convw", CONV * 288), ("a_convb", 2), ("a_convb_bc", 1), ("a_dtb", 16),
    ("a_alog", 16), ("a_d", 2), ("a_normw", 2), ("a_wout", 2 * 128)])
LAYER = [("wqkv", 3 * INNER), ("wo", 4 * 128), ("w1", 2 * HID), ("w2", 3 * 128),
         ("b1", 6), ("b2", 1), ("lg", 1), ("lb", 1), ("qks", 4 * DH)]
REST, N_REST = layout(
    [("rotary", 2 * 4 * DH)]
    + [(f"{name}{l}", n) for l in range(DEPTH) for name, n in LAYER]
    + [("b_win", 4 * 128), ("b_wbc", 32), ("b_wdt", 2 * 128), ("b_alog", 2 * NS), ("b_bdt", 2), ("b_dtb", 2),
       ("b_gamma", 2), ("b_beta", 2), ("b_wout", 2 * 128)])
BF, N_BF = layout([("ident16", 128), ("band", 384), ("causal", 384), ("sel", 32 * 128)])


def program(nc, x_in, first_in, rest_in, bf_in, out):
    f32, bf16 = mybir.dt.float32, mybir.dt.bfloat16
    ACT, ALU, AX = mybir.ActivationFunctionType, mybir.AluOpType, mybir.AxisListType
    ctx = ExitStack()
    with ctx:
        def sb(name, shape, dt=f32):
            return ctx.enter_context(nc.sbuf_tensor(name, shape, dt))

        def sem(name):
            return ctx.enter_context(nc.semaphore(name))

        X = sb("X", [128, NTOK])
        first = sb("first", [128, N_FIRST])
        rest = sb("rest", [128, N_REST])
        tabs16 = sb("tabs16", [128, N_BF], bf16)

        def F(name, a=0, b=None, p=128):
            at, n = FIRST[name]
            return first[0:p, at + a:at + (n if b is None else b)]

        def W(name, a=0, b=None, p0=0, p=128):
            at, n = REST[name]
            return rest[p0:p, at + a:at + (n if b is None else b)]

        def T16(name, a=0, b=None, p=128):
            at, n = BF[name]
            return tabs16[0:p, at + a:at + (n if b is None else b)]

        ARENA = 24832
        arena = sb("arena", [128, ARENA])
        used = {}

        def shared(phase, shape):
            at = used.get(phase, 0)
            n = int(np.prod(shape[1:]))
            used[phase] = at + n
            assert used[phase] <= ARENA
            a = arena[0:shape[0], at:at + n]
            if len(shape) == 3:
                a = a.rearrange("p (a b) -> p a b", a=shape[1])
            if len(shape) == 4:
                a = a.rearrange("p (a b c) -> p a b c", a=shape[1], b=shape[2])
            return a

        psum = ctx.enter_context(nc.psum_tensor("psum", [128, 8, 512], f32))
        bank = [psum[:, k, :] for k in range(8)]
        STAT = bank[7]

        XC = sb("XC", [128, NT])
        CEN = sb("CEN", [128, NT])
        LSQ = sb("LSQ", [128, NT])
        LLOG = LRS = LSQ
        LRS2 = sb("LRS2", [128, NT])
        CEN2 = sb("CEN2", [128, NT])
        LSQ2 = sb("LSQ2", [128, NT])
        ln_in = sem("ln_in")
        ln_mean = sem("ln_mean")
        ln_cen = sem("ln_cen")
        ln_sq = sem("ln_sq")
        ln_var = sem("ln_var")
        ln_log = sem("ln_log")
        ln_rs = sem("ln_rs")
        ln_out = sem("ln_out")

        def pair(t):
            return t[:, :].rearrange("p (b t) -> p b t", b=2)

        eps_col = sb("eps_col", [128, 1])
        floor_col = sb("floor_col", [128, 1])
        unscale_col = sb("unscale_col", [128, 1])
        convW = sb("convW", [128, CONV, 304])
        a_exp = sb("a_exp", [128, 16])
        sg_bias = sb("sg_bias", [128, 2 * NS])
        th_bias = sb("th_bias", [128, 2 * NS])
        dt_bias_b = sb("dt_bias_b", [128, 2])
        out_bias_b = sb("out_bias_b", [128, 1])
        tab = sb("tab", [128, DEPTH, 2, 4, DH])
        b1f = sb("b1f", [128, DEPTH, 6])
        in_first = sem("in_first")
        in_x = sem("in_x")
        in_rest = sem("in_rest")
        pre_a = sem("pre_a")
        pre_aexp = sem("pre_aexp")
        pre_ps = sem("pre_ps")
        pre_b = sem("pre_b")

        XN = sb("XN", [128, 2, SEQ + CONV - 1])
        ZS = shared("ssd", [128, 2, NT])
        Y = shared("ssd", [128, 2, NT])
        YS = shared("ssd", [128, 2, NT])
        used["mamba"] = used["ssd"]
        ZA = [ZS, shared("ssd", [128, 2, NT])]
        XA = [shared("ssd", [128, 2, NT]) for _ in range(2)]
        BA = [shared("ssd", [NS, NT]) for _ in range(2)]
        CA = [shared("ssd", [NS, NT]) for _ in range(2)]
        sp = sb("sp", [128, 8, 16])
        adt = sb("adt", [128, 2, 16])
        SEG_BANK, Y_BANK, CB_BANK, X_BANK = (bank[0], bank[1]), (bank[2], bank[3]), bank[4], (bank[6], bank[5])
        AM = sb("AM", [128, 2, 3, 128])
        LM = shared("ssd", [128, 2, 384])
        MM = shared("ssd", [128, 2, 384])
        XT = [shared("ssd", [128, 4, DI]) for _ in range(2)]
        a_z = sem("a_z")
        a_dt = sem("a_dt")
        a_act = sem("a_act")
        a_sp = sem("a_sp")
        a_spd = sem("a_spd")
        a_adt1 = sem("a_adt1")
        a_adt = sem("a_adt")
        a_xtp = sem("a_xtp")
        a_xt = sem("a_xt")
        a_cb = sem("a_cb")
        a_am = sem("a_am")
        a_seg = sem("a_seg")
        a_lm = sem("a_lm")
        a_mm = sem("a_mm")
        a_y = sem("a_y")
        a_yd = sem("a_yd")
        a_yg = sem("a_yg")
        a_ysq = sem("a_ysq")
        a_ms = sem("a_ms")
        a_log = sem("a_log")
        a_rs = sem("a_rs")
        a_yn = sem("a_yn")
        a_out = sem("a_out")
        a_x = sem("a_x")

        SLOTS = DEPTH * PAIRS
        R = shared("layers", [128, NTOK])
        QKT = [shared("layers", [128, 8, NT]) for _ in range(2)]
        VT = [shared("layers", [128, 4, INNER]) for _ in range(2)]
        OT = shared("layers", [128, 4, NT])
        HA = sb("HA", [128, NT])
        HF = sb("HF", [128, NT])
        HN = sb("HN", [128, NT])
        SQN = shared("layers", [128, 2, INNER])
        CQ = shared("layers", [128, 2, INNER])
        SS = sb("SS", [128, 2, HEADS])
        SL = sb("SL", [128, 2, HEADS])
        SR = sb("SR", [128, 2, HEADS])
        SC = sb("SC", [128, 2, HEADS])
        NB = sb("NB", [128, 2, 2])
        LS = sb("LS", [128, 2, 2])
        RC = sb("RC", [128, 2, 2])
        P = sb("P", [128, 2, 384])
        PT = shared("layers", [128, 2, 384])
        GE = shared("layers", [128, 3, NT])
        S_BANK, P_BANK, O_BANK = (0, 1), 2, 4
        QK_BANK = (5, 6)
        V_BANK = bank[3]
        HID_BANK = ((V_BANK, STAT, V_BANK), (STAT, V_BANK, STAT))
        f_sim = sem("f_sim")
        f_nb = sem("f_nb")
        f_exp = sem("f_exp")
        f_rc = sem("f_rc")
        f_p = sem("f_p")
        f_ptp = sem("f_ptp")
        f_pta = sem("f_pta")
        f_ptd = sem("f_ptd")
        f_pv = sem("f_pv")
        f_oe = sem("f_oe")
        f_at = sem("f_at")
        f_r1 = sem("f_r1")
        f_g = sem("f_g")
        f_ge = sem("f_ge")
        f_a = sem("f_a")
        f_ga = sem("f_ga")
        f_ff = sem("f_ff")
        f_r2 = sem("f_r2")
        f_x = sem("f_x")
        f_h = sem("f_h")
        f_pj = sem("f_pj")
        f_sq = sem("f_sq")
        f_ss = sem("f_ss")
        f_sl = sem("f_sl")
        f_sr = sem("f_sr")
        f_sc = sem("f_sc")
        f_prod = sem("f_prod")
        f_rope = sem("f_rope")
        f_qk = sem("f_qk")
        f_xp = sem("f_xp")
        f_qkt = sem("f_qkt")
        f_vp = sem("f_vp")
        f_v = sem("f_v")

        class Norm:
            def __init__(self, tag):
                (self.ready, self.mean, self.cen, self.sq, self.var, self.log, self.rs, self.out) = (
                    sem(f"{tag}_{x}") for x in ("ready", "mean", "cen", "sq", "var", "log", "rs", "out"))

        inner, outer = Norm("fi"), Norm("fo")

        DEEP = 4
        ZM = [ZS, shared("mamba", [128, 2, NT])]
        XI = shared("mamba", [128, 2, NT])
        AV = shared("mamba", [128, 2, NT])
        WV = shared("mamba", [128, 2, NT])
        LV = shared("mamba", [128, 2, NT])
        PV = shared("mamba", [128, 2, NT])
        U = [shared("mamba", [128, 2, NT]) for _ in range(2)]
        LD = [shared("mamba", [128, 2, NT]) for _ in range(2)]
        BR = shared("mamba", [96, NT])
        BS = [sb(f"BS{k}", [96, NT], bf16) for k in range(2)]
        RG = shared("mamba", [128, DEEP, NT])
        AB = shared("mamba", [128, DEEP, NT])
        WU = shared("mamba", [128, DEEP, NT])
        VB = shared("mamba", [128, 2, NT])
        HS = shared("mamba", [128, 2, NT])
        PC = shared("mamba", [128, DEEP, NT])
        B_BANK, C_BANK, ACC_BANK = (bank[0], bank[2]), (bank[1], bank[3]), (bank[4], bank[5])
        SIDE = bank[6]
        STEPS = 2 * NS
        m_bb = sem("m_bb")
        m_bc = sem("m_bc")
        m_rg = sem("m_rg")
        m_ab = sem("m_ab")
        m_wu = sem("m_wu")
        m_vb = sem("m_vb")
        m_hs = sem("m_hs")
        m_pc = sem("m_pc")
        m_acc = sem("m_acc")
        m_in = sem("m_in")
        m_zp = sem("m_zp")
        m_zg = sem("m_zg")
        m_zs = sem("m_zs")
        m_vp = sem("m_vp")
        m_abs = sem("m_abs")
        m_exp = sem("m_exp")
        m_w = sem("m_w")
        m_lost = sem("m_lost")
        m_ln = sem("m_ln")
        m_max = sem("m_max")
        m_l1p = sem("m_l1p")
        m_dt = sem("m_dt")
        m_dc = sem("m_dc")
        m_ld = sem("m_ld")
        m_xp = sem("m_xp")
        m_xi = sem("m_xi")
        m_u = sem("m_u")
        m_bp = sem("m_bp")
        m_bs = sem("m_bs")
        m_bd = sem("m_bd")
        m_g = sem("m_g")
        m_mean = sem("m_mean")
        m_cen = sem("m_cen")
        m_sq = sem("m_sq")
        m_var = sem("m_var")
        m_log = sem("m_log")
        m_rs = sem("m_rs")
        m_n = sem("m_n")
        m_out = sem("m_out")
        m_x = sem("m_x")

        out_done = sem("out_done")

        block = ctx.enter_context(nc.Block())

        LN_M = PAIRS

        class Slot:
            def __init__(self, eng, ph, i, j, last=None):
                self.eng, self.ph, self.i, self.j = eng, ph, i, j
                last = j if last is None else last
                self.looped = not isinstance(i, int)
                self.post = 1 <= j and last <= SLOTS
                self.pre = -1 <= j and last <= SLOTS - 2
                self.outer = last + 2 < PAIRS
                self.last = last

            def has(self, m):
                return 0 <= self.j + m and self.last + m < SLOTS

            def side(self, m=0):
                return (self.j + m) % 2

            def layer(self, m):
                assert (self.j + m) // PAIRS == (self.last + m) // PAIRS
                return (self.j + m) // PAIRS

            def tokens(self, m):
                at = (self.j + m) % PAIRS * NT
                return bass.ds(self.i * (2 * NT) + at, NT) if self.looped else slice(at, at + NT)

            def wait_ge(self, semaphore, per, n, slot=0):
                self.count(semaphore, 2 * per, per * (SLOTS * self.ph + self.j + slot) + n)

            def wait_pair(self, semaphore, slot):
                self.count(semaphore, 2, PAIRS * self.ph + (self.j + slot) % PAIRS + 1)

            def count(self, semaphore, per_turn, const):
                if not self.looped:
                    if const > 0:
                        self.eng.wait_ge(semaphore, const)
                else:
                    assert const > 0
                    self.eng.wait_ge(semaphore, self.i * per_turn + const)

            def unit(self, u):
                m, u = u // 16, u % 16
                return (m, u) if self.has(m) else None

        def passes(eng, ph, slot):
            for n in (-2, -1, 0, 1):
                slot(Slot(eng, ph, 0, n))
            with eng.Fori(0, 2) as i:
                for j in (2, 3):
                    slot(Slot(eng, ph, i, j, j + 2))
            for n in range(6, PAIRS + 1):
                slot(Slot(eng, ph, 0, n))
            with eng.Fori(0, PAIRS // 2 - 1) as i:
                for j in (PAIRS + 1, PAIRS + 2):
                    slot(Slot(eng, ph, i, j, j + PAIRS - 4))
            for n in (SLOTS - 1, SLOTS):
                slot(Slot(eng, ph, 0, n))

        class Turn:
            def __init__(self, eng, i, j):
                self.eng, self.i, self.j = eng, i, j
                self.looped = not isinstance(i, int)
                self.states = 0 <= j < PAIRS
                self.before = 1 <= j
                self.after = j < PAIRS - 1

            def wait_ge(self, semaphore, per, n, pair=0):
                const = per * (self.j + pair) + n
                if self.looped:
                    assert const > 0
                    self.eng.wait_ge(semaphore, self.i * (2 * per) + const)
                elif const > 0:
                    self.eng.wait_ge(semaphore, const)

            def tokens(self, m):
                at = (self.j + m) * NT
                return bass.ds(self.i * (2 * NT) + at, NT) if self.looped else slice(at, at + NT)

        def pairs(eng, turn):
            turn(Turn(eng, 0, -1))
            turn(Turn(eng, 0, 0))
            with eng.Fori(0, PAIRS // 2 - 1) as i:
                for j in (1, 2):
                    turn(Turn(eng, i, j))
            turn(Turn(eng, 0, PAIRS - 1))
            turn(Turn(eng, 0, PAIRS))

        FIRST_ITEM, SPACING = 2, 4

        def item(k, h, behind):
            h -= behind + FIRST_ITEM
            m, h = (1, h) if h >= 0 else (0, h + 8 * SPACING)
            exists = k.pre if m else k.has(0)
            return (m, h // SPACING) if exists and h % SPACING == 0 else None

        @block.sync
        def _(sp_):
            sp_.dma_start(first[:, :], first_in).then_inc(in_first, 16)
            sp_.dma_start(X[:, :], x_in).then_inc(in_x, 16)
            sp_.dma_start(tabs16[:, :], bf_in).then_inc(in_first, 16)
            sp_.dma_start(rest[:, :], rest_in).then_inc(in_rest, 16)
            with sp_.Fori(0, PAIRS) as i:
                sp_.wait_ge(f_x, i + (PAIRS + 1))
                sp_.dma_start(out[:, bass.ds(i * NT, NT)], X[:, bass.ds(i * NT, NT)]).then_inc(out_done, 16)
            sp_.wait_ge(out_done, 16 * PAIRS)

        @block.gpsimd
        def _(pool):
            pool.wait_ge(in_first, 32)

            def pool_heads(t):
                if not t.states:
                    return
                t.wait_ge(a_adt, 1, 1)
                for q in range(8):
                    b, h = divmod(q, SSD_HEADS)
                    t.wait_ge(a_seg, 8, q - 1)
                    a = adt[:, t.j % 2, :].rearrange("p (b t h) -> p b t h", b=2, t=2)[:, b, :, h:h + 1]
                    nc.gpsimd.tensor_tensor(AM[:, q % 2, 0:2, :], F("strict").rearrange("p (t s) -> p t s", t=2),
                                            a.to_broadcast([128, 2, 128]), ALU.mult)
                    nc.gpsimd.tensor_tensor(AM[:, q % 2, 2, :], F("ones"), a[:, 1, :].to_broadcast([128, 128]),
                                            ALU.mult).then_inc(a_am, 1)

            pairs(pool, pool_heads)

            def pool_slot(k):
                if not k.pre:
                    return
                for n in range(8):
                    part = n % 2
                    k.wait_ge(f_prod, 8, n + 1, slot=1)
                    nc.gpsimd.tensor_tensor(CQ[:, part, :], CQ[:, part, :], SQN[:, part, :], ALU.add).then_inc(f_rope, 1)
                    k.wait_ge(f_rope, 8, n + 1, slot=1)
                    k.wait_ge(f_sc, 8, n + 1, slot=1)
                    heads = CQ[:, part, :].rearrange("p (h d) -> p h d", d=DH)
                    nc.gpsimd.tensor_tensor(heads, heads, SC[:, part, :].unsqueeze(2).to_broadcast([128, HEADS, DH]),
                                            ALU.mult).then_inc(f_qk, 1)

            def layers_pool(ph):
                passes(pool, ph, pool_slot)

            pool.wait_ge(a_x, PAIRS)
            layers_pool(0)
            def pool_turn(t):
                for k in range(STEPS):
                    if t.states:
                        t.wait_ge(m_rg, STEPS, k + 1)
                        t.wait_ge(m_vb, STEPS, k + 1 - DEEP)
                        if k == 0:
                            t.wait_ge(m_u, 1, 1)
                        nc.gpsimd.tensor_tensor(WU[:, k % DEEP, :], RG[:, k % DEEP, :], U[t.j % 2][:, k % 2, :],
                                                ALU.mult).then_inc(m_wu, 1)
                    if not t.after:
                        continue
                    if k == 20:
                        t.wait_ge(m_ln, 1, 1, pair=1)
                        t.wait_ge(m_lost, 1, 1, pair=1)
                        nc.gpsimd.tensor_tensor(LV[:, :, :], LV[:, :, :], AV[:, :, :], ALU.subtract).then_inc(m_l1p, 1)
                    if k == 22:
                        t.wait_ge(m_l1p, 1, 1, pair=1)
                        t.wait_ge(m_max, 2, 2, pair=1)
                        nc.gpsimd.tensor_tensor(LV[:, :, :], LV[:, :, :], PV[:, :, :], ALU.add).then_inc(m_dt, 1)
                    if k == 26:
                        t.wait_ge(m_dt, 1, 1, pair=1)
                        t.wait_ge(m_xi, 2, 2, pair=1)
                        t.wait_ge(m_wu, STEPS, STEPS, pair=-1)
                        nc.gpsimd.tensor_tensor(U[(t.j + 1) % 2][:, :, :], LV[:, :, :], XI[:, :, :], ALU.mult).then_inc(m_u, 1)

            pairs(pool, pool_turn)
            pool.wait_ge(m_x, PAIRS)
            layers_pool(1)

        @block.tensor
        def _(pe):
            mm = nc.tensor.matmul
            pe.wait_ge(in_first, 32)
            pe.wait_ge(pre_a, 1)

            def segsum(t, q):
                seg = SEG_BANK[q % 2]
                t.wait_ge(a_am, 8, q + 1)
                t.wait_ge(a_lm, 8, q - 1)
                mm(seg[:, 0:384], T16("ident16"), T16("causal"), start=True, stop=False)
                mm(seg[:, 0:128], AM[:, q % 2, 0, :], F("le"), start=False, stop=False)
                mm(seg[:, 128:256], AM[:, q % 2, 0, :], F("ones"), start=False, stop=False)
                mm(seg[:, 128:256], AM[:, q % 2, 2, :], F("le"), start=False, stop=False)
                mm(seg[:, 256:384], AM[:, q % 2, 1, :], F("le"), start=False, stop=True).then_inc(a_seg, 1)

            def c_times_b(t, b):
                ba, ca = BA[t.j % 2], CA[t.j % 2]
                t.wait_ge(a_act, 6, 4)
                t.wait_ge(a_mm, 8, 4 * b)
                mm(CB_BANK[:, 0:256], ba[:, SEQ * b:SEQ * b + 128], ca[:, SEQ * b:SEQ * b + SEQ], start=True, stop=True)
                mm(CB_BANK[:, 256:384], ba[:, SEQ * b + 128:SEQ * b + SEQ], ca[:, SEQ * b + 128:SEQ * b + SEQ],
                   start=True, stop=True).then_inc(a_cb, 1)

            def head_out(t, q):
                b, h = divmod(q, SSD_HEADS)
                t.wait_ge(a_mm, 8, q + 1)
                if q == 0:
                    t.wait_ge(a_xt, 4, 4)
                    t.wait_ge(a_yd, 2, 2, pair=-1)
                y = Y_BANK[h // 2][64 * (h % 2):64 * (h % 2) + 64, :]
                xh = XT[t.j % 2][:, :, DH * h:DH * h + DH]
                mm(y[:, SEQ * b:SEQ * b + SEQ], xh[:, 2 * b, :], MM[:, q % 2, 0:256], start=True, stop=False)
                mm(y[:, SEQ * b + 128:SEQ * b + SEQ], xh[:, 2 * b + 1, :], MM[:, q % 2, 256:384],
                   start=False, stop=True).then_inc(a_y, 1)

            def conv(t, columns, dst, first_tap):
                for c in (first_tap, first_tap + 1):
                    last = mm(dst, convW[:, c, columns], XN[:, :, c:c + SEQ], start=c == 0, stop=c == CONV - 1)
                if first_tap:
                    last.then_inc(a_z, 1)

            def a_pe_beginning(t, h):
                if h == 1:
                    t.wait_ge(ln_in, 1, 1, pair=1)
                    t.wait_ge(a_xt, 4, 4)
                    mm(X_BANK[1], F("mean128"), XC[:, :], start=True, stop=True).then_inc(ln_mean, 1)
                elif h == 3:
                    t.wait_ge(ln_sq, 1, 1, pair=1)
                    mm(X_BANK[1], F("mean128"), LSQ[:, :], start=True, stop=True).then_inc(ln_var, 1)
                elif h == 6:
                    t.wait_ge(ln_out, 1, 1, pair=1)
                    for tt in range(4):
                        b, tile = divmod(tt, 2)
                        last = mm(X_BANK[1][:, 4 * tt:4 * tt + 4], XN[:, b, 3 + 128 * tile:131 + 128 * tile],
                                  F("a_win", 544, 548), start=True, stop=True)
                    last.then_inc(a_dt, 1)
                    conv(t, slice(0, 128), X_BANK[0], 0)
                elif h == 7:
                    conv(t, slice(0, 128), X_BANK[0], 2)
                elif h == 8:
                    t.wait_ge(a_spd, 2, 1, pair=1)
                    conv(t, slice(128, 256), X_BANK[1], 0)
                elif h == 9:
                    conv(t, slice(128, 256), X_BANK[1], 2)
                elif h == 11:
                    t.wait_ge(a_act, 6, 1, pair=1)
                    conv(t, slice(256, 304), X_BANK[0][0:48, :], 0)
                    conv(t, slice(256, 304), X_BANK[0][0:48, :], 2)
                elif h == 12:
                    t.wait_ge(a_act, 6, 2, pair=1)
                    t.wait_ge(a_x, 1, 1, pair=-1)
                    for half, dst in enumerate((X_BANK[1], STAT)):
                        mm(dst, F("a_win", 128 * half, 128 * half + 128), XN[:, :, 3:3 + SEQ],
                           start=True, stop=True).then_inc(a_z, 1)
                elif h in (14, 15):
                    part = h - 14
                    t.wait_ge(a_act, 6, (4, 5)[part], pair=1)
                    for tt in (2 * part, 2 * part + 1):
                        for k in range(2):
                            at = 256 * (tt % 2) + 128 * k
                            last = nc.tensor.transpose(X_BANK[part][:, at:at + 128],
                                                       XA[(t.j + 1) % 2][:, k, 128 * tt:128 * tt + 128], F("ident"))
                    last.then_inc(a_xtp, 1)

            def a_pe_ending(t, h):
                if h in (3, 4):
                    half = h - 3
                    t.wait_ge(a_ysq, 2, half + 1, pair=-1)
                    if half == 0 and t.states:
                        t.wait_ge(a_act, 6, 6)
                    last = mm(STAT, F("mean256"), YS[:, half, :], start=half == 0, stop=half == 1)
                    if half:
                        last.then_inc(a_ms, 1)
                elif h in (8, 9):
                    half = h - 8
                    t.wait_ge(a_yn, 2, half + 1, pair=-1)
                    t.wait_ge(a_log, 1, 1, pair=-1)
                    last = mm(STAT, F("a_wout", 128 * half, 128 * half + 128), Y[:, half, :], start=half == 0, stop=half == 1)
                    if half:
                        last.then_inc(a_out, 1)

            def a_pe_turn(t):
                for h in range(16):
                    if t.states and h % 2 == 0:
                        if h == 0:
                            c_times_b(t, 0)
                            segsum(t, 0)
                        if h == 8:
                            c_times_b(t, 1)
                        if h < 14:
                            segsum(t, h // 2 + 1)
                    if t.before:
                        a_pe_ending(t, h)
                    if t.after:
                        a_pe_beginning(t, h)
                    if t.states and h % 2 and h >= 3:
                        head_out(t, (h - 3) // 2)
                if t.states:
                    head_out(t, 7)

            pairs(pe, a_pe_turn)

            pe.wait_ge(in_rest, 16)
            pe.wait_ge(a_x, PAIRS)
            for l in range(DEPTH):
                for g in range(2):
                    for m, (at, size) in enumerate(HID_TILES):
                        mm(bank[0][0:size, 8 * l + 3 * g + m:8 * l + 3 * g + m + 1],
                           W(f"w1{l}", HID * g + at, HID * g + at + size), W(f"lb{l}"), start=True, stop=True)
            for k in range(2):
                last = mm(bank[0][:, 16:17], W("b_wout", 128 * k, 128 * k + 128), W("b_beta", k, k + 1),
                          start=k == 0, stop=k == 1)
            last.then_inc(pre_ps, 1)
            pe.wait_ge(pre_b, 1)

            def scores(k, m, u):
                h, b = u % HEADS, u // HEADS
                k.wait_ge(f_exp, 16, u - 1, slot=m)
                k.wait_ge(f_qkt, 8, 4 * b + 4, slot=m)
                s, rows = bank[S_BANK[u % 2]], slice(64 * (h % 2), 64 * (h % 2) + 64)
                q, key = QKT[k.side(m)][rows, h // 2, :], QKT[k.side(m)][rows, 4 + h // 2, :]
                mm(s[:, 0:384], T16("ident16"), T16("band"), start=True, stop=False)
                mm(s[:, 0:192], q[:, SEQ * b + 128:SEQ * b + 256], key[:, SEQ * b + 64:SEQ * b + 256],
                   start=False, stop=False)
                mm(s[:, 256:384], q[:, SEQ * b:SEQ * b + 128], key[:, SEQ * b:SEQ * b + 128],
                   start=False, stop=True).then_inc(f_sim, 1)

            def flip(k, m, u):
                k.wait_ge(f_p, 16, u + 1, slot=m)
                k.wait_ge(f_pta if u % 2 else f_ptd, 8, (u + 1) // 2, slot=m)
                for c in range(3):
                    last = nc.tensor.transpose(bank[P_BANK][:, 128 * c:128 * c + 128],
                                               P[:, u % 2, 128 * c:128 * c + 128], F("ident"))
                last.then_inc(f_ptp, 1)

            def weigh(k, m, u):
                h, b = u % HEADS, u // HEADS
                k.wait_ge(f_ptd if u % 2 else f_pta, 8, u // 2 + 1, slot=m)
                if u % 2 == 0:
                    k.wait_ge(f_oe, 8, u // 2, slot=m)
                if h == 0:
                    k.wait_ge(f_v, 4, 2 * b + 2, slot=m)
                o = bank[O_BANK][64 * (h % 2):64 * (h % 2) + 64, :]
                value = VT[k.side(m)][:, :, DH * h:DH * h + DH]
                mm(o[:, 128:256], value[:, 2 * b + 1, :], PT[:, u % 2, 128:256], start=True, stop=False)
                mm(o[:, 128:256], value[:, 2 * b, :], PT[:, u % 2, 0:128], start=False, stop=True)
                mm(o[:, 0:128], value[:, 2 * b, :], PT[:, u % 2, 256:384], start=True, stop=True).then_inc(f_pv, 1)

            def out_projection(k, half):
                l = k.layer(-1)
                if half == 0:
                    k.wait_ge(f_oe, 8, 8, slot=-1)
                    if k.outer:
                        k.wait_pair(outer.log, 2)
                for j in (2 * half, 2 * half + 1):
                    last = mm(STAT, W(f"wo{l}", 128 * j, 128 * j + 128), OT[:, j, :], start=j == 0, stop=j == 3)
                if half:
                    last.then_inc(f_at, 1)

            def inner_mean(k):
                k.wait_ge(inner.ready, 1, 1, slot=-1)
                mm(STAT, F("mean128"), HF[:, :], start=True, stop=True).then_inc(inner.mean, 1)

            def inner_var(k):
                k.wait_ge(inner.sq, 1, 1, slot=-1)
                mm(STAT, F("mean128"), LSQ[:, :], start=True, stop=True).then_inc(inner.var, 1)

            def hidden(k, half, m, done):
                at, size = HID_TILES[m]
                mm(HID_BANK[half][m][0:size, :], W(f"w1{k.layer(-1)}", half * HID + at, half * HID + at + size), HN[:, :],
                   start=True, stop=True).then_inc(done, 1)

            def gate_half(k, m):
                if m == 0:
                    k.wait_ge(inner.out, 1, 1, slot=-1)
                elif m == 1:
                    if k.has(0):
                        k.wait_ge(f_v, 4, 4)
                    if k.pre:
                        k.wait_ge(f_v, 4, 3, slot=1)
                else:
                    k.wait_ge(f_ge, 3, 1, slot=-1)
                hidden(k, 1, m, f_g)

            def other_half(k, m):
                if m < 2:
                    k.wait_ge(f_ge, 3, m + 2, slot=-1)
                else:
                    k.wait_ge(f_ga, 3, 1, slot=-1)
                hidden(k, 0, m, f_a)

            def down_projection(k, m):
                size = HID_TILES[m][1]
                k.wait_ge(f_ga, 3, max(m, 1) + 1, slot=-1)
                last = mm(STAT, W(f"w2{k.layer(-1)}", 128 * m, 128 * m + 128, p=size), GE[0:size, m, :],
                          start=m == 0, stop=m == 2)
                if m == 2:
                    last.then_inc(f_ff, 1)

            def outer_mean(k):
                k.wait_pair(outer.ready, 2)
                if k.j > -2:
                    k.wait_pair(outer.log, 1)
                k.wait_ge(f_r2, 1, 1, slot=-2)
                mm(STAT, F("mean128"), XC[:, :], start=True, stop=True).then_inc(outer.mean, 1)

            def outer_var(k):
                k.wait_pair(outer.sq, 2)
                mm(STAT, F("mean128"), LSQ2[:, :], start=True, stop=True).then_inc(outer.var, 1)

            def project(k, m, n):
                tt, part = divmod(n, 2)
                if n == 0:
                    k.wait_ge(f_h, 1, 1, slot=m)
                k.wait_ge(f_qkt, 8, n - 1, slot=m)
                mm(bank[QK_BANK[part]], HA[:, 128 * tt:128 * tt + 128],
                   W(f"wqkv{k.layer(m)}", INNER * part, INNER * part + INNER), start=True, stop=True).then_inc(f_pj, 1)

            def project_v(k, tt):
                k.wait_ge(f_h, 1, 1, slot=1)
                k.wait_ge(f_v, 4, tt, slot=1)
                if tt == 3 and k.post:
                    k.wait_ge(f_ga, 3, 3, slot=-1)
                mm(V_BANK, HA[:, 128 * tt:128 * tt + 128], W(f"wqkv{k.layer(1)}", 2 * INNER, 3 * INNER),
                   start=True, stop=True).then_inc(f_vp, 1)

            def to_features(k, m, n):
                part = n % 2
                k.wait_ge(f_qk, 8, n + 1, slot=m)
                for c in range(4):
                    last = nc.tensor.transpose(bank[QK_BANK[part]][:, 128 * c:128 * c + 128],
                                               CQ[:, part, 128 * c:128 * c + 128], F("ident"))
                last.then_inc(f_xp, 1)

            def pe_dense(k, h):
                if k.outer and h == 1:
                    outer_mean(k)
                if k.outer and h == 4:
                    outer_var(k)
                if k.post:
                    if h in (5, 6):
                        out_projection(k, h - 5)
                    elif h == 9:
                        inner_mean(k)
                    elif h == 13:
                        inner_var(k)
                    elif h == 18:
                        gate_half(k, 0)
                        gate_half(k, 1)
                    elif h == 20:
                        gate_half(k, 2)
                    elif h in (21, 22, 24):
                        other_half(k, (21, 22, 24).index(h))
                    elif h in (25, 26, 27):
                        down_projection(k, h - 25)
                if item(k, h, 6):
                    to_features(k, *item(k, h, 6))
                if item(k, h, 0):
                    project(k, *item(k, h, 0))
                if k.pre and h in (3, 7, 13, 29):
                    project_v(k, (3, 7, 13, 29).index(h))

            def pe_slot(k):
                for u in range(16):
                    if k.unit(u + 2):
                        scores(k, *k.unit(u + 2))
                    pe_dense(k, 2 * u)
                    if k.unit(u):
                        flip(k, *k.unit(u))
                    pe_dense(k, 2 * u + 1)
                    if k.unit(u - 1):
                        weigh(k, *k.unit(u - 1))

            def layers_pe(ph):
                passes(pe, ph, pe_slot)

            layers_pe(0)

            def spread(t, s, column, dst, done):
                mm(dst, T16("sel", 128 * column, 128 * column + 128, p=96), BS[t.j % 2][:, :],
                   start=True, stop=True).then_inc(done, 1)

            def spread_b(t, s):
                t.wait_ge(m_vb, STEPS, 2 * s - 2)
                if s == 0:
                    t.wait_ge(m_bs, 3, 3)
                spread(t, s, s, B_BANK[s % 2], m_bb)

            def spread_c(t, s):
                t.wait_ge(m_pc, STEPS, 2 * s - 2)
                spread(t, s, NS + s, C_BANK[s % 2], m_bc)

            def half_sum(k, weight, source, done):
                last = mm(STAT, weight(k), source[:, k, :], start=k == 0, stop=k == 1)
                if k:
                    last.then_inc(done, 1)

            def pe_ending(t, k):
                if k in (2, 3):
                    t.wait_ge(m_g, 2, k - 1, pair=-1)
                    half_sum(k - 2, lambda half: F("mean256"), Y, m_mean)
                elif k in (8, 9):
                    t.wait_ge(m_sq, 2, k - 7, pair=-1)
                    t.wait_ge(m_cen, 2, 2, pair=-1)
                    half_sum(k - 8, lambda half: F("mean256"), YS, m_var)
                elif k in (18, 19):
                    t.wait_ge(m_n, 2, k - 17, pair=-1)
                    if t.after and k == 18:
                        t.wait_ge(m_abs, 2, 2, pair=1)
                        t.wait_ge(m_max, 2, 2, pair=1)
                    half_sum(k - 18, lambda half: W("b_wout", 128 * half, 128 * half + 128), Y, m_out)

            def pe_beginning(t, k):
                if k == 1:
                    t.wait_ge(m_in, 1, 1, pair=1)
                    t.wait_ge(m_zs, 2, 2)
                    mm(SIDE, F("mean128"), XC[:, :], start=True, stop=True).then_inc(ln_mean, 1)
                elif k == 6:
                    pe_wait_ln(t, ln_sq)
                    mm(SIDE, F("mean128"), LSQ[:, :], start=True, stop=True).then_inc(ln_var, 1)
                elif k in (13, 14):
                    half = k - 13
                    if half == 0:
                        pe_wait_ln(t, ln_out)
                    else:
                        t.wait_ge(m_log, 1, 1, pair=-1)
                    mm((SIDE, STAT)[half], W("b_wdt", 128 * half, 128 * half + 128), HN[:, :],
                       start=True, stop=True).then_inc(m_vp, 1)
                elif k in (18, 20):
                    half = (k - 18) // 2
                    if half:
                        t.wait_ge(m_xi, 2, 1, pair=1)
                    else:
                        t.wait_ge(m_abs, 2, 1, pair=1)
                        t.wait_ge(m_max, 2, 1, pair=1)
                    mm(SIDE, W("b_win", 128 * half, 128 * half + 128), HN[:, :], start=True, stop=True).then_inc(m_xp, 1)
                elif k == 22:
                    t.wait_ge(m_xi, 2, 2, pair=1)
                    mm(SIDE[0:32, :], W("b_wbc"), HN[:, :], start=True, stop=True).then_inc(m_bp, 1)
                elif k in (25, 28):
                    half = (k - 25) // 3
                    t.wait_ge(m_zs if half else m_bd, 2, 1, pair=1)
                    mm(SIDE, W("b_win", 256 + 128 * half, 384 + 128 * half), HN[:, :], start=True, stop=True).then_inc(m_zp, 1)

            def pe_wait_ln(t, semaphore):
                t.wait_ge(semaphore, 1, LN_M + 1, pair=1)

            def pe_turn(t):
                if t.states:
                    spread_b(t, 0)
                    spread_c(t, 0)
                    spread_b(t, 1)
                    spread_c(t, 1)
                for k in range(STEPS):
                    if t.states:
                        if k % 2 == 0 and k // 2 + 2 < NS:
                            spread_b(t, k // 2 + 2)
                        if k % 2 == 0 and 2 <= k < STEPS - 2:
                            spread_c(t, k // 2 + 1)
                    if t.before:
                        pe_ending(t, k)
                    if t.after:
                        pe_beginning(t, k)
                    if t.states:
                        t.wait_ge(m_pc, STEPS, k + 1)
                        if k < 2:
                            t.wait_ge(m_g, 2, k + 1, pair=-1)
                        mm(ACC_BANK[k % 2], F("ident"), PC[:, k % DEEP, :], start=k < 2, stop=k >= STEPS - 2).then_inc(m_acc, 1)

            pairs(pe, pe_turn)
            layers_pe(1)

        @block.scalar
        def _(act):
            A = nc.scalar.activation
            EXP_LN = "natural_log_exp_and_others"
            nc.scalar.preload_act_table_set(EXP_LN)
            act.wait_ge(in_first, 32)
            A(a_exp[:, :], F("a_alog"), ACT.Exp).then_inc(pre_aexp, 1)
            act.wait_ge(pre_a, 1)

            def a_act_ending(t, h):
                if h == 2:
                    for half in range(2):
                        t.wait_ge(a_yg, 2, half + 1, pair=-1)
                        A(YS[:, half, :], Y[:, half, :], ACT.Square).then_inc(a_ysq, 1)
                elif h == 6:
                    t.wait_ge(a_ms, 1, 1, pair=-1)
                    A(LRS2[:, :], STAT, ACT.Ln, bias=eps_col[:, :]).then_inc(a_log, 1)
                    t.wait_ge(a_log, 1, 1, pair=-1)
                    A(LRS2[:, :], LRS2[:, :], ACT.Exp, scale=-0.5).then_inc(a_rs, 1)

            def a_act_beginning(t, h):
                side = (t.j + 1) % 2
                if h == 2:
                    t.wait_ge(ln_cen, 1, 1, pair=1)
                    A(LSQ[:, :], CEN[:, :], ACT.Square).then_inc(ln_sq, 1)
                elif h == 4:
                    t.wait_ge(ln_var, 1, 1, pair=1)
                    A(LLOG[:, :], X_BANK[1], ACT.Ln, bias=eps_col[:, :]).then_inc(ln_log, 1)
                    t.wait_ge(ln_log, 1, 1, pair=1)
                    A(LRS[:, :], LLOG[:, :], ACT.Exp, scale=-0.5).then_inc(ln_rs, 1)
                elif h == 8:
                    t.wait_ge(a_spd, 2, 1, pair=1)
                    A(sp[:, 1, :], sp[:, 0, :], ACT.Abs).then_inc(a_sp, 1)
                    t.wait_ge(a_sp, 3, 1, pair=1)
                    A(sp[:, 2, :], sp[:, 1, :], ACT.Exp, scale=-1.0).then_inc(a_sp, 1)
                elif h == 10:
                    t.wait_ge(a_spd, 2, 2, pair=1)
                    A(sp[:, 4, :], sp[:, 3, :], ACT.Ln).then_inc(a_sp, 1)
                    for k in range(2):
                        t.wait_ge(a_z, 5, k + 1, pair=1)
                        A(XA[side][:, k, :], X_BANK[k], ACT.Silu, bias=F("a_convb", k, k + 1)).then_inc(a_act, 1)
                    nc.scalar.preload_act_table_set(EXP_LN)
                elif h == 13:
                    for k, dst in enumerate((BA, CA)):
                        t.wait_ge(a_z, 5, 3, pair=1)
                        rows = slice(32 * k, 32 * k + NS)
                        A(dst[side][:, :], X_BANK[0][rows, :], ACT.Silu, bias=F("a_convb_bc")[rows, :]).then_inc(a_act, 1)
                    for k in range(2):
                        t.wait_ge(a_z, 5, k + 4, pair=1)
                        A(ZA[side][:, k, :], (X_BANK[1], STAT)[k], ACT.Silu).then_inc(a_act, 1)
                    nc.scalar.preload_act_table_set(EXP_LN)

            def a_act_turn(t):
                for h in range(16):
                    if t.states and h % 2 == 0:
                        q = h // 2
                        t.wait_ge(a_seg, 8, q + 1)
                        t.wait_ge(a_mm, 8, q - 1)
                        A(LM[:, q % 2, :], SEG_BANK[q % 2][:, 0:384], ACT.Exp).then_inc(a_lm, 1)
                    if t.before:
                        a_act_ending(t, h)
                    if t.after:
                        a_act_beginning(t, h)

            nc.scalar.preload_act_table_set(EXP_LN)
            pairs(act, a_act_turn)

            act.wait_ge(pre_b, 1)

            def exponentials(k, m, u):
                k.wait_ge(f_nb, 16, u + 1, slot=m)
                k.wait_ge(f_ptp, 16, u - 1, slot=m)
                s = bank[S_BANK[u % 2]]
                A(P[:, u % 2, 64:256], s[:, 0:192], ACT.Exp, bias=NB[:, u % 2, 0:1], accum_out=LS[:, u % 2, 0:1])
                A(P[:, u % 2, 256:384], s[:, 256:384], ACT.Exp, bias=NB[:, u % 2, 1:2],
                  accum_out=LS[:, u % 2, 1:2]).then_inc(f_exp, 1)

            def flipped_act(k, m, u):
                k.wait_ge(f_ptp, 16, u + 1, slot=m)
                k.wait_ge(f_pv, 16, u - 1, slot=m)
                A(PT[:, 0, :], bank[P_BANK][:, 0:384], ACT.Copy).then_inc(f_pta, 1)

            def output(k, m, u):
                b, j = divmod(u // 2, 4)
                k.wait_ge(f_pv, 16, u + 2, slot=m)
                if u == 0:
                    k.wait_ge(f_at, 1, 1, slot=m - 1)
                A(OT[:, j, SEQ * b:SEQ * b + SEQ], bank[O_BANK][:, 0:256], ACT.Copy).then_inc(f_oe, 1)

            def square_centred(norm, wait, centred, square):
                wait(norm.cen)
                A(square, centred, ACT.Square).then_inc(norm.sq, 1)

            def inverse_root(norm, wait, variance, root):
                wait(norm.var)
                A(root, variance, ACT.Ln, bias=eps_col[:, :]).then_inc(norm.log, 1)
                wait(norm.log)
                A(root, root, ACT.Exp, scale=-0.5).then_inc(norm.rs, 1)

            def gelus(k):
                for m, (at, size) in enumerate(HID_TILES):
                    k.wait_ge(f_g, 3, m + 1, slot=-1)
                    A(GE[0:size, m, :], HID_BANK[1][m][0:size, :], ACT.Gelu,
                      bias=b1f[0:size, k.layer(-1), 3 + m:4 + m]).then_inc(f_ge, 1)
                nc.scalar.preload_act_table_set(EXP_LN)

            def squares(k, m, n):
                k.wait_ge(f_pj, 8, n + 1, slot=m)
                k.wait_ge(f_rope, 8, n - 1, slot=m)
                A(SQN[:, n % 2, :], bank[QK_BANK[n % 2]], ACT.Square).then_inc(f_sq, 1)

            def values(k, tt):
                k.wait_ge(f_vp, 4, tt + 1, slot=1)
                A(VT[k.side(1)][:, tt, :], V_BANK, ACT.Copy).then_inc(f_v, 1)

            def norms(k, m, n):
                k.wait_ge(f_ss, 8, n + 1, slot=m)
                A(SL[:, n % 2, :], SS[:, n % 2, :], ACT.Ln, bias=floor_col[:, :], scale=SS_SCALE).then_inc(f_sl, 1)
                k.wait_ge(f_sl, 8, n + 1, slot=m)
                A(SR[:, n % 2, :], SL[:, n % 2, :], ACT.Exp, bias=unscale_col[:, :], scale=-0.5).then_inc(f_sr, 1)

            def features(k, m, n):
                tt, part = divmod(n, 2)
                k.wait_ge(f_xp, 8, n + 1, slot=m)
                A(QKT[k.side(m)][:, 4 * part:4 * part + 4, 128 * tt:128 * tt + 128],
                  bank[QK_BANK[part]].rearrange("p (c t) -> p c t", t=128), ACT.Copy).then_inc(f_qkt, 1)

            def act_dense(k, h):
                def inner_at(semaphore):
                    k.wait_ge(semaphore, 1, 1, slot=-1)

                def outer_at(semaphore):
                    k.wait_pair(semaphore, 2)

                if k.outer and h == 3:
                    square_centred(outer, outer_at, CEN2[:, :], LSQ2[:, :])
                if k.outer and h == 5:
                    inverse_root(outer, outer_at, STAT, LSQ2[:, :])
                if k.post and h == 12:
                    square_centred(inner, inner_at, CEN[:, :], LSQ[:, :])
                if k.post and h == 14:
                    inverse_root(inner, inner_at, STAT, LSQ[:, :])
                if k.post and h == 19:
                    gelus(k)
                if item(k, h, 1):
                    squares(k, *item(k, h, 1))
                if item(k, h, 3):
                    norms(k, *item(k, h, 3))
                if item(k, h, 7):
                    features(k, *item(k, h, 7))
                if k.pre and h in (4, 8, 14, 30):
                    values(k, (4, 8, 14, 30).index(h))

            def act_slot(k):
                for u in range(16):
                    if k.unit(u + 1):
                        exponentials(k, *k.unit(u + 1))
                    if u % 2 and k.unit(u - 3):
                        output(k, *k.unit(u - 3))
                    act_dense(k, 2 * u)
                    if u % 2 == 0 and k.unit(u):
                        flipped_act(k, *k.unit(u))
                    act_dense(k, 2 * u + 1)

            def layers_act(ph):
                nc.scalar.preload_act_table_set(EXP_LN)
                passes(act, ph, act_slot)

            layers_act(0)
            SIG_TANH = "sigmoid_and_others"

            def act_ending(t, k):
                if k == 9:
                    for half in range(2):
                        t.wait_ge(m_cen, 2, half + 1, pair=-1)
                        A(YS[:, half, :], Y[:, half, :], ACT.Square).then_inc(m_sq, 1)
                elif k == 14:
                    t.wait_ge(m_var, 1, 1, pair=-1)
                    A(LRS2[:, :], STAT, ACT.Ln, bias=eps_col[:, :]).then_inc(m_log, 1)
                    t.wait_ge(m_log, 1, 1, pair=-1)
                    A(LRS2[:, :], LRS2[:, :], ACT.Exp, scale=-0.5).then_inc(m_rs, 1)

            def act_beginning(t, k):
                if k == 7:
                    t.wait_ge(ln_cen, 1, LN_M + 1, pair=1)
                    A(LSQ[:, :], CEN[:, :], ACT.Square).then_inc(ln_sq, 1)
                elif k == 14:
                    t.wait_ge(ln_var, 1, LN_M + 1, pair=1)
                    A(LLOG[:, :], SIDE, ACT.Ln, bias=eps_col[:, :]).then_inc(ln_log, 1)
                    t.wait_ge(ln_log, 1, LN_M + 1, pair=1)
                    A(LRS[:, :], LLOG[:, :], ACT.Exp, scale=-0.5).then_inc(ln_rs, 1)
                elif k == 18:
                    nc.scalar.preload_act_table_set(EXP_LN)
                    t.wait_ge(m_dc, 1, 1)
                    t.wait_ge(m_u, 1, 1)
                    for half in range(2):
                        t.wait_ge(m_vp, 2, half + 1, pair=1)
                        A(AV[:, half, :], (SIDE, STAT)[half], ACT.Abs, bias=dt_bias_b[:, half:half + 1]).then_inc(m_abs, 1)
                    t.wait_ge(m_abs, 2, 2, pair=1)
                    A(AV[:, :, :], AV[:, :, :], ACT.Exp, scale=-1.0).then_inc(m_exp, 1)
                    t.wait_ge(m_w, 1, 1, pair=1)
                    A(LV[:, :, :], WV[:, :, :], ACT.Ln).then_inc(m_ln, 1)
                    nc.scalar.preload_act_table_set(SIG_TANH)
                elif k in (22, 24):
                    half = (k - 22) // 2
                    t.wait_ge(m_xp, 2, half + 1, pair=1)
                    A(XI[:, half, :], SIDE, ACT.Copy).then_inc(m_xi, 1)
                elif k == 26:
                    t.wait_ge(m_bp, 1, 1, pair=1)
                    t.wait_ge(m_bc, NS, NS, pair=-1)
                    A(BS[(t.j + 1) % 2][0:32, :], SIDE[0:32, :], ACT.Copy).then_inc(m_bs, 1)
                elif k in (28, 30):
                    part = (k - 26) // 2
                    t.wait_ge(m_bd, 2, part, pair=1)
                    A(BS[(t.j + 1) % 2][32 * part:32 * part + 32, :], BR[32 * part:32 * part + 32, :],
                      ACT.Copy).then_inc(m_bs, 1)
                if k in (29, 31):
                    half = (k - 29) // 2
                    t.wait_ge(m_zp, 2, half + 1, pair=1)
                    A(ZM[(t.j + 1) % 2][:, half, :], SIDE, ACT.Sigmoid).then_inc(m_zg, 1)
                if k == 29:
                    nc.scalar.preload_act_table_set(EXP_LN)
                    t.wait_ge(m_dc, 1, 1, pair=1)
                    A(LD[(t.j + 1) % 2][:, :, :], WV[:, :, :], ACT.Ln).then_inc(m_ld, 1)
                    nc.scalar.preload_act_table_set(SIG_TANH)

            def act_turn(t):
                for k in range(STEPS):
                    if t.states:
                        c = NS * (k % 2) + k // 2
                        d = LD[t.j % 2][:, k % 2, :]
                        if k == 0:
                            t.wait_ge(m_ld, 1, 1)
                        t.wait_ge(m_wu, STEPS, k + 1 - DEEP)
                        A(RG[:, k % DEEP, :], d, ACT.Sigmoid, bias=sg_bias[:, c:c + 1], scale=-1.0).then_inc(m_rg, 1)
                        t.wait_ge(m_hs, 2 * STEPS, 2 * (k + 1 - DEEP))
                        A(AB[:, k % DEEP, :], d, ACT.Tanh, bias=th_bias[:, c:c + 1], scale=-0.5).then_inc(m_ab, 1)
                    if k == 14:
                        nc.scalar.preload_act_table_set(EXP_LN)
                    if t.before:
                        act_ending(t, k)
                    if t.after:
                        act_beginning(t, k)
                    if k == 14:
                        nc.scalar.preload_act_table_set(SIG_TANH)

            pairs(act, act_turn)
            nc.scalar.preload_act_table_set(EXP_LN)
            layers_act(1)

        @block.vector
        def _(dve):
            v = nc.vector
            TT, TS, STT = v.tensor_tensor, v.tensor_scalar, v.scalar_tensor_tensor
            v.memset(eps_col[:, :], EPS)
            v.memset(floor_col[:, :], SS_FLOOR)
            v.memset(unscale_col[:, :], LN_UNSCALE)
            v.memset(XN[:, :, 0:CONV - 1], 0.0)
            v.memset(HA[:, :], 0.0)
            v.memset(HF[:, :], 0.0)
            v.memset(P[:, :, :], 0.0)
            dve.wait_ge(in_first, 32)
            dve.wait_ge(pre_aexp, 1)
            for c in range(CONV):
                TT(convW[:, c, 0:272], F("a_win", 256, 528), F("a_convw", 288 * c, 288 * c + 272), ALU.mult)
                TT(convW[:, c, 288:304], F("a_win", 528, 544), F("a_convw", 288 * c + 272, 288 * c + 288), ALU.mult)
                v.memset(convW[:, c, 272:288], 0.0)
            for k in range(2):
                last = TS(F("a_wout", 128 * k, 128 * k + 128), F("a_wout", 128 * k, 128 * k + 128),
                          F("a_normw", k, k + 1), None, ALU.mult)
            last.then_inc(pre_a, 1)
            dve.wait_ge(in_x, 16)
            dve.wait_ge(pre_a, 1)


            def a_dve_ending(t, h):
                if h == 0:
                    t.wait_ge(a_y, 8, 8, pair=-1)
                    for k in range(2):
                        STT(Y[:, k, :], XA[(t.j - 1) % 2][:, k, :], F("a_d", k, k + 1), Y_BANK[k], ALU.mult, ALU.add).then_inc(a_yd, 1)
                elif h == 1:
                    for k in range(2):
                        t.wait_ge(a_yd, 2, k + 1, pair=-1)
                        TT(Y[:, k, :], Y[:, k, :], ZA[(t.j - 1) % 2][:, k, :], ALU.mult).then_inc(a_yg, 1)
                elif h == 7:
                    t.wait_ge(a_rs, 1, 1, pair=-1)
                    for k in range(2):
                        t.wait_ge(a_yg, 2, k + 1, pair=-1)
                        TT(Y[:, k, :], Y[:, k, :], LRS2[:, :], ALU.mult).then_inc(a_yn, 1)
                elif h == 10:
                    xs = X[:, t.tokens(-1)]
                    t.wait_ge(a_out, 1, 1, pair=-1)
                    TT(xs, xs, STAT, ALU.add).then_inc(a_x, 1)

            def a_dve_beginning(t, h):
                side = (t.j + 1) % 2
                if h == 0:
                    t.wait_ge(ln_cen, 1, 1)
                    TS(XC[:, :], X[:, t.tokens(1)], 1.0, None, ALU.mult).then_inc(ln_in, 1)
                elif h == 1:
                    t.wait_ge(ln_mean, 1, 1, pair=1)
                    t.wait_ge(ln_in, 1, 1, pair=1)
                    TT(CEN[:, :], XC[:, :], X_BANK[1], ALU.subtract).then_inc(ln_cen, 1)
                elif h == 5:
                    t.wait_ge(ln_rs, 1, 1, pair=1)
                    t.wait_ge(ln_cen, 1, 1, pair=1)
                    t.wait_ge(a_z, 5, 5)
                    TT(XN[:, :, CONV - 1:], pair(CEN), pair(LRS), ALU.mult).then_inc(ln_out, 1)
                elif h == 7:
                    t.wait_ge(a_dt, 1, 1, pair=1)
                    TT(sp[:, 0, :], X_BANK[1][:, 0:16], F("a_dtb"), ALU.add).then_inc(a_spd, 1)
                elif h == 9:
                    t.wait_ge(a_sp, 3, 2, pair=1)
                    TS(sp[:, 3, :], sp[:, 2, :], 1.0, None, ALU.add).then_inc(a_spd, 1)
                elif h == 11:
                    t.wait_ge(a_spd, 2, 2, pair=1)
                    STT(sp[:, 5, :], sp[:, 3, :], -1.0, sp[:, 2, :], ALU.add, ALU.subtract).then_inc(a_adt1, 1)
                    t.wait_ge(a_adt1, 3, 1, pair=1)
                    t.wait_ge(a_sp, 3, 3, pair=1)
                    TT(sp[:, 6, :], sp[:, 4, :], sp[:, 5, :], ALU.subtract).then_inc(a_adt1, 1)
                    t.wait_ge(a_adt1, 3, 2, pair=1)
                    STT(sp[:, 7, :], sp[:, 0, :], 0.0, sp[:, 6, :], ALU.max, ALU.add).then_inc(a_adt1, 1)
                    t.wait_ge(a_adt1, 3, 3, pair=1)
                    STT(adt[:, side, :], sp[:, 7, :], -1.0, a_exp[:, :], ALU.mult, ALU.mult).then_inc(a_adt, 1)
                elif h == 15:
                    for tt in range(4):
                        t.wait_ge(a_xtp, 2, tt // 2 + 1, pair=1)
                        at = 256 * (tt % 2)
                        TT(XT[side][:, tt, :].rearrange("p (h d) -> p h d", h=SSD_HEADS),
                           X_BANK[tt // 2][:, at:at + 256].rearrange("p (h d) -> p h d", h=SSD_HEADS),
                           sp[:, 7, 4 * tt:4 * tt + 4].unsqueeze(2).to_broadcast([128, SSD_HEADS, DH]), ALU.mult).then_inc(a_xt, 1)

            def a_dve_turn(t):
                for h in range(16):
                    if t.states and h % 2 == 0:
                        q = h // 2
                        t.wait_ge(a_cb, 2, q // 4 + 1)
                        t.wait_ge(a_lm, 8, q + 1)
                        t.wait_ge(a_y, 8, q - 1)
                        TT(MM[:, q % 2, :], LM[:, q % 2, :], CB_BANK[:, 0:384], ALU.mult).then_inc(a_mm, 1)
                    if t.before:
                        a_dve_ending(t, h)
                    if t.after:
                        a_dve_beginning(t, h)

            pairs(dve, a_dve_turn)
            dve.wait_ge(a_x, PAIRS)

            dve.wait_ge(in_rest, 16)
            dve.wait_ge(pre_ps, 1)
            for l in range(DEPTH):
                for g in range(2):
                    for m, (at, size) in enumerate(HID_TILES):
                        c = 3 * g + m
                        TT(b1f[0:size, l, c:c + 1], bank[0][0:size, 8 * l + c:8 * l + c + 1],
                           W(f"b1{l}", c, c + 1, p=size), ALU.add)
                TS(W(f"w1{l}"), W(f"w1{l}"), W(f"lg{l}"), None, ALU.mult)
                for t in range(2):
                    TT(tab[:, l, t, :, :].rearrange("p a d -> p (a d)"), W("rotary", 4 * DH * t, 4 * DH * t + 4 * DH),
                       W(f"qks{l}"), ALU.mult)
            v.tensor_copy(out_bias_b[:, :], bank[0][:, 16:17])
            for k in range(2):
                TS(W("b_wout", 128 * k, 128 * k + 128), W("b_wout", 128 * k, 128 * k + 128), W("b_gamma", k, k + 1),
                   None, ALU.mult)
            TT(dt_bias_b[:, :], W("b_bdt"), W("b_dtb"), ALU.add)
            TS(sg_bias[:, :], W("b_alog"), -1.0, float(np.log(2.0)), ALU.mult, ALU.add)
            TS(th_bias[:, :], W("b_alog"), -0.5, float(0.5 * np.log(2.0)), ALU.mult, ALU.add).then_inc(pre_b, 1)
            dve.wait_ge(pre_b, 1)
            dve.wait_ge(a_x, PAIRS)

            def shifted(src, dst, done):
                TS(dst[0:64, :], src[0:64, :], 1.0, None, ALU.mult)
                TS(dst[64:128, :].rearrange("p (b t) -> p b t", b=2)[:, :, 1:],
                   src[64:128, :].rearrange("p (b t) -> p b t", b=2)[:, :, 0:SEQ - 1], 1.0, None, ALU.mult).then_inc(done, 1)

            def maxima(k, m, u):
                k.wait_ge(f_sim, 16, u + 1, slot=m)
                k.wait_ge(f_exp, 16, u - 1, slot=m)
                v.reduce_max(NB[:, u % 2, :], bank[S_BANK[u % 2]][:, 0:384].rearrange("p (k s) -> p k s", k=2), AX.X,
                             negate=True).then_inc(f_nb, 1)

            def probabilities(k, m, u):
                k.wait_ge(f_exp, 16, u + 1, slot=m)
                v.reciprocal(RC[:, u % 2, :], LS[:, u % 2, :]).then_inc(f_rc, 1)
                k.wait_ge(f_rc, 16, u + 1, slot=m)
                TS(P[:, u % 2, 64:256], P[:, u % 2, 64:256], RC[:, u % 2, 0:1], None, ALU.mult)
                TS(P[:, u % 2, 256:384], P[:, u % 2, 256:384], RC[:, u % 2, 1:2], None, ALU.mult).then_inc(f_p, 1)

            def flipped_dve(k, m, u):
                k.wait_ge(f_ptp, 16, u + 1, slot=m)
                k.wait_ge(f_pv, 16, u - 1, slot=m)
                v.tensor_copy(PT[:, 1, :], bank[P_BANK][:, 0:384]).then_inc(f_ptd, 1)

            def after_attention(k):
                r = R[:, k.tokens(-1)]
                k.wait_ge(f_at, 1, 1, slot=-1)
                TT(r, r, STAT, ALU.add).then_inc(f_r1, 1)
                k.wait_ge(f_r1, 1, 1, slot=-1)
                shifted(r, HF, inner.ready)

            def centre(norm, wait, src, mean, dst):
                wait(norm.mean)
                TT(dst, src, mean, ALU.subtract).then_inc(norm.cen, 1)

            def normalise(norm, wait, centred, root, dst):
                wait(norm.rs)
                wait(norm.cen)
                TT(dst, centred, root, ALU.mult).then_inc(norm.out, 1)

            def gated(k, m):
                size = HID_TILES[m][1]
                k.wait_ge(f_a, 3, m + 1, slot=-1)
                STT(GE[0:size, m, :], HID_BANK[0][m][0:size, :], b1f[0:size, k.layer(-1), m:m + 1],
                    GE[0:size, m, :], ALU.add, ALU.mult).then_inc(f_ga, 1)

            def after_feed_forward(k):
                r = R[:, k.tokens(-1)]
                k.wait_ge(f_ff, 1, 1, slot=-1)
                STT(r, STAT, W(f"b2{k.layer(-1)}"), r, ALU.add, ALU.add).then_inc(f_r2, 1)
                if k.layer(-1) == DEPTH - 1:
                    k.wait_ge(f_r2, 1, 1, slot=-1)
                    xs = X[:, k.tokens(-1)]
                    TT(xs, xs, r, ALU.add).then_inc(f_x, 1)

            def begin_slot(k):
                if k.layer(1):
                    k.wait_ge(f_r2, 1, 1, slot=1 - PAIRS)
                else:
                    k.wait_pair(outer.out, 1)
                k.wait_ge(f_pj, 8, 8)
                k.wait_ge(f_vp, 4, 4)
                shifted(R[:, k.tokens(1)], HA, f_h)

            def products(k, m, n):
                tt, part = divmod(n, 2)
                k.wait_ge(f_sq, 8, n + 1, slot=m)
                k.wait_ge(f_ss, 8, n + 1, slot=m)
                k.wait_ge(f_xp, 8, n - 1, slot=m)
                x = bank[QK_BANK[part]].rearrange("p (h r d) -> p h r d", h=HEADS, r=2)
                t = tab[:, k.layer(m), tt % 2, :, :]
                TT(CQ[:, part, :].rearrange("p (h d) -> p h d", h=HEADS), bank[QK_BANK[part]].rearrange("p (h d) -> p h d", h=HEADS),
                   t[:, part, :].unsqueeze(1).to_broadcast([128, HEADS, DH]), ALU.mult)
                y = SQN[:, part, :].rearrange("p (h r d) -> p h r d", h=HEADS, r=2)
                for r in range(2):
                    sin = t[:, 2 + part, 32 * r:32 * r + 32].unsqueeze(1).to_broadcast([128, HEADS, 32])
                    last = TT(y[:, :, r, :], x[:, :, 1 - r, :], sin, ALU.mult)
                last.then_inc(f_prod, 1)

            def sums(k, m, n):
                k.wait_ge(f_sq, 8, n + 1, slot=m)
                k.wait_ge(f_sl, 8, n - 1, slot=m)
                v.reduce_sum(SS[:, n % 2, :], SQN[:, n % 2, :].rearrange("p (h d) -> p h d", d=DH), AX.X).then_inc(f_ss, 1)

            def clipped(k, m, n):
                k.wait_ge(f_sr, 8, n + 1, slot=m)
                k.wait_ge(f_qk, 8, n - 1, slot=m)
                TS(SC[:, n % 2, :], SR[:, n % 2, :], NORM_CLIP, None, ALU.min).then_inc(f_sc, 1)

            def dve_dense(k, h):
                def inner_at(semaphore):
                    k.wait_ge(semaphore, 1, 1, slot=-1)

                def outer_at(semaphore):
                    k.wait_pair(semaphore, 2)

                if k.pre and h == 0:
                    begin_slot(k)
                if k.outer and h == 0:
                    if k.j > -2:
                        k.wait_pair(outer.cen, 1)
                    TS(XC[:, :], X[:, k.tokens(2)], 1.0, None, ALU.mult).then_inc(outer.ready, 1)
                if k.outer and h == 2:
                    k.wait_pair(outer.ready, 2)
                    centre(outer, outer_at, XC[:, :], STAT, CEN2[:, :])
                if k.outer and h == 7:
                    normalise(outer, outer_at, CEN2[:, :], LSQ2[:, :], R[:, k.tokens(2)])
                if k.post:
                    if h == 7:
                        after_attention(k)
                    elif h == 11:
                        centre(inner, inner_at, HF[:, :], STAT, CEN[:, :])
                    elif h == 16:
                        normalise(inner, inner_at, CEN[:, :], LSQ[:, :], HN[:, :])
                    elif h in (22, 23, 25):
                        gated(k, (22, 23, 25).index(h))
                    elif h == 29:
                        after_feed_forward(k)
                if item(k, h, 2):
                    sums(k, *item(k, h, 2))
                    products(k, *item(k, h, 2))
                if item(k, h, 4):
                    clipped(k, *item(k, h, 4))

            def dve_slot(k):
                for u in range(16):
                    if k.unit(u + 2):
                        maxima(k, *k.unit(u + 2))
                    dve_dense(k, 2 * u)
                    if k.unit(u + 1):
                        probabilities(k, *k.unit(u + 1))
                    dve_dense(k, 2 * u + 1)
                    if u % 2 and k.unit(u):
                        flipped_dve(k, *k.unit(u))

            def layers_dve(ph):
                passes(dve, ph, dve_slot)

            layers_dve(0)
            dve.wait_ge(f_x, PAIRS)

            def times_b(t, k):
                if k % 2 == 0:
                    t.wait_ge(m_bb, NS, k // 2 + 1)
                t.wait_ge(m_wu, STEPS, k + 1)
                t.wait_ge(m_hs, 2 * STEPS, 2 * k - 2)
                TT(VB[:, k % 2, :], WU[:, k % DEEP, :], B_BANK[k // 2 % 2], ALU.mult).then_inc(m_vb, 1)

            def states(t, k):
                t.wait_ge(m_vb, STEPS, k + 1)
                t.wait_ge(m_ab, STEPS, k + 1)
                t.wait_ge(m_pc, STEPS, k - 1)
                for b in range(2):
                    cols = slice(SEQ * b, SEQ * b + SEQ)
                    v.tensor_tensor_scan(HS[:, k % 2, cols], AB[:, k % DEEP, cols], VB[:, k % 2, cols], 0.0,
                                         ALU.mult, ALU.add).then_inc(m_hs, 1)

            def times_c(t, k):
                if k % 2 == 0:
                    t.wait_ge(m_bc, NS, k // 2 + 1)
                t.wait_ge(m_hs, 2 * STEPS, 2 * k + 2)
                t.wait_ge(m_acc, STEPS, k + 1 - DEEP)
                TT(PC[:, k % DEEP, :], HS[:, k % 2, :], C_BANK[k // 2 % 2], ALU.mult).then_inc(m_pc, 1)

            def dve_ending(t, k):
                if k in (0, 1):
                    t.wait_ge(m_acc, STEPS, STEPS - 1 + k, pair=-1)
                    t.wait_ge(m_zs, 2, k + 1, pair=-1)
                    TT(Y[:, k, :], ZM[(t.j - 1) % 2][:, k, :], ACC_BANK[k], ALU.mult).then_inc(m_g, 1)
                elif k in (5, 6):
                    half = k - 5
                    t.wait_ge(m_mean, 1, 1, pair=-1)
                    t.wait_ge(m_g, 2, half + 1, pair=-1)
                    TT(Y[:, half, :], Y[:, half, :], STAT, ALU.subtract).then_inc(m_cen, 1)
                elif k in (14, 15):
                    half = k - 14
                    t.wait_ge(m_rs, 1, 1, pair=-1)
                    t.wait_ge(m_cen, 2, half + 1, pair=-1)
                    TT(Y[:, half, :], Y[:, half, :], LRS2[:, :], ALU.mult).then_inc(m_n, 1)
                elif k == 22:
                    xs = X[:, t.tokens(-1)]
                    t.wait_ge(m_out, 1, 1, pair=-1)
                    STT(xs, STAT, out_bias_b[:, :], xs, ALU.add, ALU.add).then_inc(m_x, 1)

            def dve_beginning(t, k):
                if k == 0:
                    t.wait_ge(ln_cen, 1, LN_M + 1)
                    TS(XC[:, :], X[:, t.tokens(1)], 1.0, None, ALU.mult).then_inc(m_in, 1)
                elif k == 3:
                    t.wait_ge(ln_mean, 1, LN_M + 1, pair=1)
                    t.wait_ge(m_in, 1, 1, pair=1)
                    TT(CEN[:, :], XC[:, :], SIDE, ALU.subtract).then_inc(ln_cen, 1)
                elif k == 12:
                    t.wait_ge(ln_rs, 1, LN_M + 1, pair=1)
                    t.wait_ge(ln_cen, 1, LN_M + 1, pair=1)
                    t.wait_ge(m_bp, 1, 1)
                    t.wait_ge(m_zp, 2, 2)
                    TT(HN[:, :], CEN[:, :], LRS[:, :], ALU.mult).then_inc(ln_out, 1)
                elif k == 15:
                    t.wait_ge(m_exp, 1, 1, pair=1)
                    t.wait_ge(m_ld, 1, 1)
                    TS(WV[:, :, :], AV[:, :, :], 1.0, None, ALU.add).then_inc(m_w, 1)
                    for half in range(2):
                        TS(PV[:, half, :], (SIDE, STAT)[half], dt_bias_b[:, half:half + 1], 0.0,
                           ALU.add, ALU.max).then_inc(m_max, 1)
                elif k == 16:
                    t.wait_ge(m_w, 1, 1, pair=1)
                    STT(AV[:, :, :], WV[:, :, :], -1.0, AV[:, :, :], ALU.add, ALU.subtract).then_inc(m_lost, 1)
                elif k in (24, 26):
                    part = (k - 24) // 2
                    bs = BS[(t.j + 1) % 2]
                    t.wait_ge(m_bs, 3, part + 1, pair=1)
                    if part:
                        t.wait_ge(m_bd, 2, 1, pair=1)
                    TT(BR[32 * part + 32:32 * part + 64, :], BR[32:64, :] if part else SIDE[0:32, :],
                       bs[32 * part:32 * part + 32, :], ALU.subtract).then_inc(m_bd, 1)
                elif k == 25:
                    t.wait_ge(m_dt, 1, 1, pair=1)
                    t.wait_ge(m_ln, 1, 1, pair=1)
                    TS(WV[:, :, :], LV[:, :, :], 1e-19, None, ALU.max).then_inc(m_dc, 1)
                elif k in (28, 31):
                    half = (k - 28) // 3
                    z = ZM[(t.j + 1) % 2][:, half, :]
                    t.wait_ge(m_zg, 2, half + 1, pair=1)
                    TT(z, z, SIDE, ALU.mult).then_inc(m_zs, 1)

            def dve_turn(t):
                if t.states:
                    times_b(t, 0)
                    times_b(t, 1)
                    states(t, 0)
                for k in range(STEPS + 1):
                    if t.states:
                        if k >= 1:
                            times_c(t, k - 1)
                        if k + 2 < STEPS:
                            times_b(t, k + 2)
                        if k + 1 < STEPS:
                            states(t, k + 1)
                    if t.before:
                        dve_ending(t, k)
                    if t.after:
                        dve_beginning(t, k)

            pairs(dve, dve_turn)
            dve.wait_ge(m_x, PAIRS)
            layers_dve(1)


def shape_tables():
    p = np.arange(128)
    one = np.ones((128, 128), np.float32)
    le = (p[:, None] <= p[None, :]).astype(np.float32)
    strict = (p[:, None] > p[None, :]).astype(np.float32)
    half = np.arange(0, DH, 2, dtype=np.float32)
    inv_freq = (1.0 / 10000.0 ** (half / DH)).astype(np.float32)
    t = np.arange(SEQ, dtype=np.float32)
    freqs = (t[:, None] * inv_freq[None, :]).astype(np.float32).astype(np.float64)
    base = (half.astype(np.float64) + 0.4 * DH) / (1.4 * DH)
    scale = base[None, :] ** ((t.astype(np.float64) - SEQ // 2) / (WINDOW // 2))[:, None]
    cos, sin = np.cos(freqs), np.sin(freqs)

    def halves(a, sign):
        return np.concatenate([sign * a, a], 1)

    kinds = [halves(QK_SCALE * cos * scale, 1), halves(cos / scale, 1), halves(QK_SCALE * sin * scale, -1),
             halves(sin / scale, -1)]
    rotary = np.stack(kinds, 1).reshape(2, 128, 4 * DH).transpose(1, 0, 2).reshape(128, 2 * 4 * DH)

    f = {"ident": np.eye(128, dtype=np.float32), "mean128": one / 128, "mean256": one / 256, "ones": one,
         "le": le, "strict": np.concatenate([strict, strict], 1)}
    r = {"rotary": rotary.astype(np.float32)}
    q, k = p[:, None], p[None, :]
    k1 = np.arange(192)[None, :] + 64
    ok1 = (k1 <= q + 128) & (k1 >= q + 128 - WINDOW)
    ok0 = (k <= q) & (k >= q - WINDOW)
    band = np.concatenate([ok1, np.zeros((128, 64), bool), ok0], 1)
    causal = np.concatenate([le > 0, np.ones((128, 128), bool), le > 0], 1)
    sel = np.zeros((128, 32, 128), np.float32)
    for s in range(32):
        for part in range(3):
            sel[32 * part + s, s, :] = 1.0
    b = {"ident16": np.eye(128), "band": np.where(band, 0.0, MASKED), "causal": np.where(causal, 0.0, MASKED),
         "sel": sel.reshape(128, 32 * 128)}
    return f, r, b


def pack(sizes, total, parts, dtype):
    out = np.zeros((128, total), dtype)
    for name, (at, n) in sizes.items():
        a = parts[name]
        out[:a.shape[0], at:at + n] = a
    return out


def kernel(**inputs):
    import concourse.bacc as _bacc
    import ml_dtypes
    from concourse.bass_utils import run_bass_kernel_spmd as _run
    g = {k: np.asarray(a) for k, a in inputs.items()}
    x = np.ascontiguousarray(g["L0_attn_a_u"].transpose(2, 0, 1).reshape(D, NTOK))
    f, r, b = shape_tables()
    A = {k[10:]: a for k, a in g.items() if k.startswith("L0_attn_a_")}
    B = {k[10:]: a for k, a in g.items() if k.startswith("L0_attn_b_")}
    L = {k[7:]: a for k, a in g.items() if k.startswith("L0_ffn_")}

    def cols(a, n):
        return a.reshape(n, 128, -1).transpose(1, 0, 2).reshape(128, -1)

    f.update({
        "a_win": A["W_in"].T, "a_convw": np.tile(A["conv_w"][:, 0, :].T.reshape(1, -1), (128, 1)),
        "a_convb": cols(A["conv_b"][:256, None], 2), "a_convb_bc": np.pad(A["conv_b"][256:].reshape(2, NS), ((0, 0), (0, 32 - NS))).reshape(64, 1),
        "a_dtb": np.tile(A["dt_bias"][None, :], (128, 4)), "a_alog": np.tile(A["A_log"][None, :], (128, 4)),
        "a_d": cols(np.repeat(A["D"], DH)[:, None], 2), "a_normw": cols(A["norm_w"][:, None], 2),
        "a_wout": cols(A["W_out"].T, 2)})
    for l in range(DEPTH):
        b1 = np.zeros((2, 3 * 128), np.float32)
        b1[:, :HID] = L["b1"][l].reshape(2, HID)
        w2 = np.zeros((3 * 128, D), np.float32)
        w2[:HID] = L["w2"][l]
        qs, ks = L["q_scale"][l], L["k_scale"][l]
        r.update({
            f"wqkv{l}": L["wqkv"][l], f"wo{l}": cols(L["wo"][l], 4),
            f"w1{l}": L["w1"][l], f"w2{l}": cols(w2, 3), f"b1{l}": b1.reshape(6, 128).T, f"b2{l}": L["b2"][l][:, None],
            f"lg{l}": L["ln_g"][l][:, None], f"lb{l}": L["ln_b"][l][:, None],
            f"qks{l}": np.tile(np.concatenate([qs, ks, np.roll(qs, DH // 2), np.roll(ks, DH // 2)])[None, :], (128, 1))})
    r.update({
        "b_win": B["Win"].T, "b_wbc": np.concatenate([B["WB"], B["WC"]]).T, "b_wdt": B["Wdt"].T,
        "b_alog": cols(B["A_log"], 2), "b_bdt": cols(B["bdt"][:, None], 2), "b_dtb": cols(B["dt_bias"][:, None], 2),
        "b_gamma": cols(B["gamma"][:, None], 2), "b_beta": cols(B["beta"][:, None], 2), "b_wout": cols(B["Wout"].T, 2)})
    arrays = {"x": x, "first": pack(FIRST, N_FIRST, f, np.float32), "rest": pack(REST, N_REST, r, np.float32),
              "tabs16": pack(BF, N_BF, b, ml_dtypes.bfloat16)}
    nc = _bacc.Bacc("TRN2", target_bir_lowering=False, num_devices=1)
    args = [nc.dram_tensor(f"in_{k}", a.shape, mybir.dt.from_np(a.dtype), kind="ExternalInput").ap()
            for k, a in arrays.items()]
    out = nc.dram_tensor("out", (D, NTOK), mybir.dt.float32, kind="ExternalOutput").ap()
    program(nc, *args, out)
    got = _run(nc, [{f"in_{k}": a for k, a in arrays.items()}], core_ids=[0]).results[0]["out"]
    return np.ascontiguousarray(got.reshape(D, BATCH, SEQ).transpose(1, 2, 0))
```
